# Optimizing a Trainium2 kernel written in Bass

```python
import numpy as np
import jax
import jax.numpy as jnp

def _softmax(x, axis=-1):
    return jax.nn.softmax(x, axis=axis)

def _gelu(x):
    return jax.nn.gelu(x, approximate=True)

def _silu(x):
    return jax.nn.silu(x)

def _sigmoid(x):
    return jax.nn.sigmoid(x)

def _layernorm(x, axis=-1, eps=1e-05):
    m = jnp.mean(x, axis=axis, keepdims=True)
    v = jnp.var(x, axis=axis, keepdims=True)
    return (x - m) / jnp.sqrt(v + eps)

def _scatter_add(tgt, idx, src, axis=0):
    return tgt.at[idx].add(src)

def _segment_sum(src, seg, n):
    return jax.ops.segment_sum(src, seg, n)
kernel_name = 'mk_gnn_ffn_d1_gnn_r16_7a6314'

def setup_inputs(seed: int=0):
    np.random.seed(seed)
    _w = jnp.asarray

    def _rec_inputs():
        import jax
        import jax.numpy as jnp
        _gk = jax.random.key(seed)
        x = -0.0003713 + 1 * jax.random.normal(jax.random.fold_in(_gk, 1), (3125, 256), jnp.float32)
        _s = jax.random.randint(jax.random.fold_in(_gk, 2), (50000,), 0, 3125, jnp.int32)
        _d = jax.random.randint(jax.random.fold_in(_gk, 3), (50000,), 0, 3125, jnp.int32)
        _loop = jnp.arange(3125, dtype=jnp.int32)
        src = jnp.concatenate([_s, _d, _loop])
        dst = jnp.concatenate([_d, _s, _loop])
        _o = jnp.argsort(dst, stable=True)
        src = src[_o]
        dst = dst[_o]
        return (x, src, dst)
    x, src, dst = _rec_inputs()

    def _L0_gnn_setup():
        import jax, jax.numpy as jnp
        import numpy as np
        N_NODES = 3125
        N_HYPEREDGES = 3125
        E = 20000
        D = 256

        def _prelu(x, a):
            return jnp.where(x >= 0, x, a * x)

        def _hypergraph_conv(x, hei, W, b, num_nodes, num_edges):
            src = hei[0]
            he = hei[1]
            xw = x @ W.T
            ones = jnp.ones((hei.shape[1],), x.dtype)
            deg_n = jax.ops.segment_sum(ones, src, num_segments=num_nodes)
            deg_e = jax.ops.segment_sum(ones, he, num_segments=num_edges)
            d_inv = jnp.where(deg_n > 0, 1.0 / deg_n, 0.0)
            b_inv = jnp.where(deg_e > 0, 1.0 / deg_e, 0.0)
            edge_feat = b_inv[:, None] * jax.ops.segment_sum(xw[src], he, num_segments=num_edges)
            out = d_inv[:, None] * jax.ops.segment_sum(edge_feat[he], src, num_segments=num_nodes)
            return out + b
        key = jax.random.key(seed)
        ks = jax.random.split(key, 6)
        std = np.sqrt(2.0 / D)
        x = jax.random.normal(ks[0], (N_NODES, D), dtype=jnp.float32)
        hyper_edge_index = jax.random.randint(ks[1], (2, E), 0, N_HYPEREDGES, dtype=jnp.int64)
        W1 = jax.random.normal(ks[2], (D, D), dtype=jnp.float32) * std
        b1 = jnp.zeros((D,), jnp.float32)
        W2 = jax.random.normal(ks[3], (D, D), dtype=jnp.float32) * std
        b2 = jnp.zeros((D,), jnp.float32)
        prelu_a = jnp.asarray(0.25, jnp.float32)
        return {'x': x, 'W1': W1, 'b1': b1, 'W2': W2, 'b2': b2, 'prelu_a': prelu_a, 'hyper_edge_index': hyper_edge_index}
    _L0_gnn_all = _L0_gnn_setup()
    _L0_gnn_in = {k: v for k, v in _L0_gnn_all.items() if k in ('W1', 'b1', 'W2', 'b2', 'prelu_a')}
    del _L0_gnn_all

    def _L0_ffn_setup():
        import jax, jax.numpy as jnp
        import numpy as np
        B, T, D, H, E = (16, 256, 256, 512, 8)
        key = jax.random.key(seed)
        ks = jax.random.split(key, 5)
        x = jax.random.normal(ks[0], (B, T, D), dtype=jnp.float32)
        gate_w = jax.random.normal(ks[1], (D, E), dtype=jnp.float32) * 0.02
        gate_b = jnp.zeros((E,), dtype=jnp.float32)
        W1 = jax.random.normal(ks[2], (E, D, H), dtype=jnp.float32) * 0.02
        b1 = jnp.zeros((E, H), dtype=jnp.float32)
        W2 = jax.random.normal(ks[3], (E, H, D), dtype=jnp.float32) * 0.02
        b2 = jnp.zeros((E, D), dtype=jnp.float32)
        return {'x': x, 'gate_w': gate_w, 'gate_b': gate_b, 'W1': W1, 'b1': b1, 'W2': W2, 'b2': b2}
    _L0_ffn_all = _L0_ffn_setup()
    _L0_ffn_in = {k: v for k, v in _L0_ffn_all.items() if k in ('gate_w', 'gate_b', 'W1', 'b1', 'W2', 'b2')}
    del _L0_ffn_all
    return {'x': x, 'src': src, 'dst': dst, 'L0_gnn_W1': _L0_gnn_in['W1'], 'L0_gnn_b1': _L0_gnn_in['b1'], 'L0_gnn_W2': _L0_gnn_in['W2'], 'L0_gnn_b2': _L0_gnn_in['b2'], 'L0_gnn_prelu_a': _L0_gnn_in['prelu_a'], 'L0_ffn_gate_w': _L0_ffn_in['gate_w'], 'L0_ffn_gate_b': _L0_ffn_in['gate_b'], 'L0_ffn_W1': _L0_ffn_in['W1'], 'L0_ffn_b1': _L0_ffn_in['b1'], 'L0_ffn_W2': _L0_ffn_in['W2'], 'L0_ffn_b2': _L0_ffn_in['b2']}

def reference(x, src, dst, L0_gnn_W1, L0_gnn_b1, L0_gnn_W2, L0_gnn_b2, L0_gnn_prelu_a, L0_ffn_gate_w, L0_ffn_gate_b, L0_ffn_W1, L0_ffn_b1, L0_ffn_W2, L0_ffn_b2):
    import jax
    import jax.numpy as jnp

    def _L0_gnn_ref(x, W1, b1, W2, b2, prelu_a, hyper_edge_index):
        import jax, jax.numpy as jnp
        import numpy as np
        N_NODES = 3125
        N_HYPEREDGES = 3125
        E = 20000
        D = 256

        def _prelu(x, a):
            return jnp.where(x >= 0, x, a * x)

        def _hypergraph_conv(x, hei, W, b, num_nodes, num_edges):
            src = hei[0]
            he = hei[1]
            xw = x @ W.T
            ones = jnp.ones((hei.shape[1],), x.dtype)
            deg_n = jax.ops.segment_sum(ones, src, num_segments=num_nodes)
            deg_e = jax.ops.segment_sum(ones, he, num_segments=num_edges)
            d_inv = jnp.where(deg_n > 0, 1.0 / deg_n, 0.0)
            b_inv = jnp.where(deg_e > 0, 1.0 / deg_e, 0.0)
            edge_feat = b_inv[:, None] * jax.ops.segment_sum(xw[src], he, num_segments=num_edges)
            out = d_inv[:, None] * jax.ops.segment_sum(edge_feat[he], src, num_segments=num_nodes)
            return out + b
        out = _hypergraph_conv(x, hyper_edge_index, W1, b1, N_NODES, N_HYPEREDGES)
        out = _prelu(out, prelu_a)
        out = _hypergraph_conv(out, hyper_edge_index, W2, b2, N_NODES, N_HYPEREDGES)
        out = out + x
        out = _prelu(out, prelu_a)
        return out

    def _L0_ffn_ref(x, gate_w, gate_b, W1, b1, W2, b2):
        import jax, jax.numpy as jnp
        import numpy as np
        B, T, D, H, E = (16, 256, 256, 512, 8)
        Bb, Tt, Dd = x.shape
        Ee = gate_w.shape[1]
        xf = x.reshape(-1, Dd)
        N = xf.shape[0]
        logits = xf @ gate_w + gate_b
        probs = jax.nn.softmax(logits, axis=-1)
        top2_vals, top2_idx = jax.lax.top_k(probs, 2)
        cw = jnp.zeros((N, Ee), dtype=xf.dtype).at[jnp.arange(N)[:, None], top2_idx].add(top2_vals)

        def step(acc, params):
            w1, bb1, w2, bb2, we = params
            h = jax.nn.gelu(xf @ w1 + bb1, approximate=False)
            y = h @ w2 + bb2
            return (acc + we[:, None] * y, None)
        out, _ = jax.lax.scan(step, jnp.zeros_like(xf), (W1, b1, W2, b2, cw.T))
        return out.reshape(Bb, Tt, Dd)
    edge_index = jnp.stack([src, dst])
    x = x + _L0_gnn_ref(_layernorm(x, axis=-1), L0_gnn_W1, L0_gnn_b1, L0_gnn_W2, L0_gnn_b2, L0_gnn_prelu_a, edge_index)
    x = x + _L0_ffn_ref(_layernorm(x, axis=-1)[None], L0_ffn_gate_w, L0_ffn_gate_b, L0_ffn_W1, L0_ffn_b1, L0_ffn_W2, L0_ffn_b2)[0]
    return x

_drawn_inputs = setup_inputs


def setup_inputs(seed=0):
    import zlib

    import numpy as np

    out = dict(_drawn_inputs(seed))
    spreads = {'L0_gnn_b1': (0.0, 0.1),
     'L0_gnn_b2': (0.0, 0.1),
     'L0_ffn_gate_b': (0.0, 0.717),
     'L0_ffn_b1': (0.0, 0.8),
     'L0_ffn_b2': (0.0, 0.522)}
    factors = {'L0_gnn_W1': 5.094, 'L0_ffn_gate_w': 3.339, 'L0_ffn_W1': 4.764, 'L0_ffn_W2': 4.476}
    for name, (base, spread) in spreads.items():
        noise = np.random.default_rng([zlib.crc32(name.encode()), seed]).standard_normal(out[name].shape)
        drawn = base * np.exp(spread * noise) if base else spread * noise
        out[name] = jnp.asarray(drawn.astype(out[name].dtype))
    for name, factor in factors.items():
        out[name] = (out[name] * factor).astype(out[name].dtype)
    return out
```

```python
from contextlib import ExitStack

import concourse.bass as bass
from concourse import mybir

ALU = mybir.AluOpType
ACT = mybir.ActivationFunctionType
AX = mybir.AxisListType
F32 = mybir.dt.float32
F16 = mybir.dt.float16
I32 = mybir.dt.int32
U32 = mybir.dt.uint32

P = 128
GROUP = 5
STRIP_GROUPS = 25
CHUNK = 32
WINDOW = 256
SRC_BITS = 12
FEATURE_SCALE = 1024.0
HALF_TOP = 16384.0
LN_EPS = 1e-5


class Signal:

    def __init__(self, sem):
        self.sem, self.value = sem, 0

    def up(self, by=1):
        self.value += by
        return (self.sem, self.value)


class Program:

    def __init__(self):
        self.queues = {"pe": [], "act": [], "dve": [], "pool": [], "sp": []}

    def put(self, engine, fn, after=(), done=None):
        token = done.up() if done is not None else None
        self.queues[engine].append((tuple(after), fn, done, 1))
        return token

    def dma(self, engine, fn, after=(), done=None):
        token = done.up(16)
        self.queues[engine].append((tuple(after), fn, done, 16))
        return token

    def emit(self, engine, eng):
        reached = {}
        for after, fn, done, by in self.queues[engine]:
            for wait in after:
                if wait is None:
                    continue
                sem, value = wait
                if reached.get(id(sem), 0) < value:
                    eng.wait_ge(sem, value)
                    reached[id(sem)] = value
            ins = fn(eng)
            if done is not None:
                ins.then_inc(done.sem, by)


def gnn_moe_kernel(nc, x, src, dst, gW1, gb1, gW2, gb2, prelu_a, gate_w, gate_b, W1, b1, W2, b2, out):
    N, D = x.shape
    E = src.shape[0]
    NE, _, H = W1.shape
    NT = -(-N // P)
    TAIL = N - (NT - 1) * P
    NG = N // GROUP
    NS = NG // STRIP_GROUPS
    SROWS = GROUP * STRIP_GROUPS
    GC = GROUP * NT
    NPAD = NT * P
    FB = D // P
    HB = H // P
    CH_ROW = 26
    EROW = CH_ROW * CHUNK
    EPARTS = 125
    NCHUNK = CH_ROW * EPARTS
    EFULL = E // EROW
    EREST = E - EFULL * EROW
    assert N == NG * GROUP and NG == NS * STRIP_GROUPS and SROWS == 125 and EPARTS * EROW > E
    NO_EDGE = float(4095 * 4096)
    QUADS = [(q, min(4, STRIP_GROUPS - q)) for q in range(0, STRIP_GROUPS, 4)]
    TGROUPS = [(0, 7), (7, 6), (13, 6), (19, 6)]
    BLOCKS = [(b, min(4, NT - b)) for b in range(0, NT, 4)]

    with ExitStack() as ctx:
        def sb(name, shape, dt):
            return ctx.enter_context(nc.sbuf_tensor(name, shape, dt))

        def sig(name):
            return Signal(ctx.enter_context(nc.semaphore(name)))

        prog = Program()
        put, dma = prog.put, prog.dma

        word_dram = nc.dram_tensor("edge_words", [NCHUNK * CHUNK + WINDOW], F32, kind="Internal").ap()
        cmax_dram = nc.dram_tensor("chunk_max", [NCHUNK], F32, kind="Internal").ap()
        win_dram = nc.dram_tensor("windows", [NCHUNK, WINDOW], F32, kind="Internal").ap()
        srcside_dram = nc.dram_tensor("counts_src_side", [NS, P, NT * SROWS], F16, kind="Internal").ap()
        dstside_dram = nc.dram_tensor("counts_dst_side", [NS, P, NPAD], F16, kind="Internal").ap()

        xt = sb("xt", [P, NT, D], F32)
        h0 = sb("h0", [P, NT, D], F32)
        feat = sb("feat", [P, NT, 2 * D], F16)
        ef = sb("ef", [P, NS, 2 * D], F16)
        strips = sb("strips", [P, 4, NPAD], F16)
        blocks = sb("blocks", [P, 2, NS, 512], F16)
        stT = sb("stT", [P, 2, FB, 512], F32)
        onehots = stT[:, :, :, :].rearrange("p a b c -> p (a b c)").bitcast(F16).rearrange("p (k o r c) -> p k o r c", k=2, o=8, r=2)
        ohA = onehots[:, 0]
        ohQ = onehots[:, 1]
        edge_cols = sb("edge_cols", [P, 2, 2, NG], F32)
        codeT, placeT = edge_cols[:, 0, :, :], edge_cols[:, 1, :, :]
        iota_i = sb("iota_i", [P, P], I32)
        iota_h = sb("iota_h", [P, P], F16)
        iota_f = sb("iota_f", [P, P], F32)
        part_i = sb("part_i", [P, 1], I32)
        part_f = sb("part_f", [P, 1], F32)
        ident_h = sb("ident_h", [P, P], F16)
        ident_f = sb("ident_f", [P, P], F32)
        ones_h = sb("ones_h", [P, 1], F16)
        g5_i = sb("g5_i", [P, NG // 125], I32)
        g5_f = sb("g5_f", [P, NG // 125], F32)
        thr = sb("thr", [P, NG // 125], F32)
        start_f = sb("start_f", [P, NG // 125], F32)
        start_u = sb("start_u", [P, NG // 125], U32)
        cmax = sb("cmax", [P, CH_ROW], F32)
        work = sb("work", [P, 4, D], F32)
        gb1b = work[:, 2, 0:P]
        bn6 = sb("bn6", [P, NT, 6], F32)
        mv = sb("mv", [P, NT, 2], F32)
        rstd = sb("rstd", [P, NT], F32)
        nmr = sb("nmr", [P, NT], F32)
        epsc = sb("epsc", [P, 1], F32)
        degj = sb("degj", [P, 2, 4], F32)
        binv = sb("binv", [P, NS], F32)
        dinv = sb("dinv", [P, NT], F32)
        alpha = sb("alpha", [P, 1], F32)
        amax = sb("amax", [P, 1], F32)
        gw1T = sb("gw1T", [P, FB, D], F32)
        gw2T = sb("gw2T", [P, FB, D], F32)
        gb1c = sb("gb1c", [P, FB], F32)
        gb1s = sb("gb1s", [P, FB], F32)
        gb1row = sb("gb1row", [P, D], F32)
        gb2row = sb("gb2row", [P, D], F32)
        nrm = sb("nrm", [P, FB], F32)
        invs = sb("invs", [P, FB], F32)
        scl = sb("scl", [P, FB], F32)
        gatew = sb("gatew", [P, FB, NE], F32)
        gatebr = sb("gatebr", [P, NE], F32)
        cols_flat = edge_cols[:, :, :, :].rearrange("p a b c -> p (a b c)")
        g0 = NT * NE * NE
        logit, cw, rank = [cols_flat[:, g0 + i * NT * NE:g0 + (i + 1) * NT * NE].rearrange("p (a n) -> p a n", n=NE) for i in range(3)]
        g1 = g0 + 3 * NT * NE
        cwT = cols_flat[0:NE, g1:g1 + 2 * P].rearrange("p (k q) -> p k q", k=2)
        cmp1 = edge_cols[:, :, :, :].rearrange("p a b c -> p (a b c)")[:, 0:NT * NE * NE].rearrange("p (a n) -> p a n", n=NE)
        red = sb("red", [P, NT], F32)
        b1sb = sb("b1sb", [P, NE, HB], F32)

        flat = ef[:, :, :].rearrange("p a b -> p (a b)").bitcast(F32)
        yT = feat[:, :, :].rearrange("p a b -> p (a b)").bitcast(F32).rearrange("p (b n) -> p b n", b=FB)
        W5 = (NG // 125) * WINDOW
        win = flat[:, 0:W5].rearrange("p (t w) -> p t w", w=WINDOW)
        word_i = flat[:, W5:2 * W5].bitcast(I32)
        place_i = flat[:, 2 * W5:3 * W5].bitcast(I32)
        tile_i = flat[:, 3 * W5:4 * W5].bitcast(I32)
        dest_i = flat[:, 4 * W5:5 * W5].bitcast(I32)
        blk_f = blocks[:, :, :, :].rearrange("p a b c -> p (a b c)").bitcast(F32)
        run_max = blk_f[:, 0:NCHUNK]
        cm_all = blk_f[:, NCHUNK:2 * NCHUNK]
        src_i = blk_f[:, 2 * NCHUNK:2 * NCHUNK + EROW].bitcast(I32)
        dst_i = blk_f[:, 2 * NCHUNK + EROW:2 * NCHUNK + 2 * EROW].bitcast(I32)
        word_f = blk_f[:, 2 * NCHUNK + 2 * EROW:2 * NCHUNK + 3 * EROW]
        GW = 2 * NCHUNK + 3 * EROW
        gw1 = blk_f[:, GW:GW + FB * D].rearrange("p (b d) -> p b d", b=FB)
        gw2 = blk_f[:, GW + FB * D:GW + 2 * FB * D].rearrange("p (b d) -> p b d", b=FB)
        pad_row = blk_f[0:1, GW + 2 * FB * D:GW + 2 * FB * D + WINDOW]
        b2sb = blk_f[0:NE, 4 * FB * H + 4096:4 * FB * H + 4096 + D]
        w1e = blk_f[:, 0:2 * FB * H].rearrange("p (w b h) -> p w b h", w=2, b=FB)
        w2e = blk_f[:, 2 * FB * H:4 * FB * H].rearrange("p (w b d) -> p w b d", w=2, b=HB)
        hT = blk_f[:, 4 * FB * H:4 * FB * H + 4096].rearrange("p (w b n) -> p w b n", w=2, b=HB)
        code_f = flat[:, 0:W5]
        place_f = stT[:, :, :, :].rearrange("p a b c -> p (a b c)")[:, 0:W5]

        ps = ctx.enter_context(nc.psum_tensor("ps", [P, 8, 512], F32))

        def bank_h(b):
            return ps[:, b, :].bitcast(F16)

        s_edges, s_x, s_w, s_word_st, s_cmax_st, s_cmax_ld, s_win, s_gather = [
            sig(n) for n in ("edges_loaded", "x_loaded", "weights_loaded", "words_stored", "cmax_stored",
                             "cmax_loaded", "windows_written", "windows_gathered")]
        dve, act, pool, pe = sig("dve_step"), sig("act_step"), sig("pool_step"), sig("pe_step")

        def V(fn, *after):
            return put("dve", fn, after, dve)

        def A(fn, *after):
            return put("act", fn, after, act)

        k_iota = put("pool", lambda e: e.iota(iota_i[:, :], [[1, P]], base=0, channel_multiplier=0), (), pool)
        k_part = put("pool", lambda e: e.iota(part_i[:, :], [[1, 1]], base=0, channel_multiplier=1), (), pool)
        k_g5 = put("pool", lambda e: e.iota(g5_i[:, :], [[GROUP * 125, NG // 125]], base=0, channel_multiplier=GROUP), (), pool)

        pad_i = V(lambda e: e.memset(dst_i[96:128, :], 4095))
        pad_s = V(lambda e: e.memset(src_i[96:128, :], 0))
        pad_r = V(lambda e: e.memset(pad_row[:, :], NO_EDGE))
        for name, arr, tile in (("dst", dst, dst_i), ("src", src, src_i)):
            full = arr[0:EFULL * EROW].rearrange("(p m) -> p m", m=EROW)
            rest = arr[EFULL * EROW:E].rearrange("(p m) -> p m", p=1)
            dma("sp", lambda e, t=tile, f=full: e.dma_start(t[0:96, :], f[0:96, :]), (), s_edges)
            dma("sp", lambda e, t=tile, f=full: e.dma_start(t[96:EFULL, :], f[96:EFULL, :]), (pad_i, pad_s), s_edges)
            edges = dma("sp", lambda e, t=tile, r=rest: e.dma_start(t[EFULL:EFULL + 1, 0:EREST], r), (pad_i, pad_s), s_edges)

        zero_x = V(lambda e: e.memset(xt[:, NT - 1, :], 0.0))
        dma("act", lambda e: e.dma_start(xt[:, 0:NT - 1, :], x[0:(NT - 1) * P, :].rearrange("(a q) f -> q a f", q=P)), (), s_x)
        x_in = dma("act", lambda e: e.dma_start(xt[0:TAIL, NT - 1, :], x[(NT - 1) * P:N, :]), (zero_x,), s_x)
        for fn in (lambda e: e.dma_start(gw1[:, :, :], gW1.rearrange("(b p) f -> p b f", p=P)),
                   lambda e: e.dma_start(gw2[:, :, :], gW2.rearrange("(b p) f -> p b f", p=P)),
                   lambda e: e.dma_start(gb1c[:, :], gb1.rearrange("(b p) -> p b", p=P)),
                   lambda e: e.dma_start(gb2row[:, :], gb2.partition_broadcast(P)),
                   lambda e: e.dma_start(alpha[:, :], prelu_a.partition_broadcast(P)),
                   lambda e: e.dma_start(gatew[:, :, :], gate_w.rearrange("(b p) n -> p b n", p=P)),
                   lambda e: e.dma_start(gatebr[:, :], gate_b.partition_broadcast(P)),
                   lambda e: e.dma_start(b1sb[:, :, :], b1.rearrange("n (b p) -> p n b", p=P))):
            w_in = dma("act", fn, (), s_w)

        words = V(lambda e: e.scalar_tensor_tensor(out=word_f[0:EPARTS, :], in0=dst_i[0:EPARTS, :], scalar=float(1 << SRC_BITS),
                                                   in1=src_i[0:EPARTS, :], op0=ALU.mult, op1=ALU.add), edges)
        cm = V(lambda e: e.tensor_reduce(cmax[0:EPARTS, :], word_f[0:EPARTS, :].rearrange("p (c k) -> p c k", k=CHUNK), AX.X, ALU.max), words)
        dma("sp", lambda e: e.dma_start(word_dram[0:EPARTS * EROW].rearrange("(p m) -> p m", m=EROW), word_f[0:EPARTS, :]), (words,), s_word_st)
        words_st = dma("sp", lambda e: e.dma_start(word_dram[EPARTS * EROW:].rearrange("(p m) -> p m", p=1), pad_row[:, :]), (pad_r,), s_word_st)
        cm_st = dma("act", lambda e: e.dma_start(cmax_dram.rearrange("(p m) -> p m", m=CH_ROW), cmax[0:EPARTS, :]), (cm,), s_cmax_st)
        cm_ld = dma("act", lambda e: e.dma_start(cm_all, cmax_dram.partition_broadcast(P)), (cm_st,), s_cmax_ld)
        win_src = bass.AP(tensor=word_dram.tensor, offset=0, ap=[[CHUNK, NCHUNK], [1, WINDOW]])
        win_ok = dma("sp", lambda e: e.dma_start(win_dram, win_src), (words_st,), s_win)
        c_ih = V(lambda e: e.tensor_copy(iota_h[:, :], iota_i[:, :]), k_iota)
        c_if = V(lambda e: e.tensor_copy(iota_f[:, :], iota_i[:, :]))
        c_pf = V(lambda e: e.tensor_copy(part_f[:, :], part_i[:, :]), k_part)
        c_idf = V(lambda e: e.tensor_scalar(ident_f[:, :], iota_f[:, :], part_f[:, 0:1], None, ALU.is_equal), c_pf)
        c_idh = V(lambda e: e.tensor_scalar(ident_h[:, :], iota_f[:, :], part_f[:, 0:1], None, ALU.is_equal))
        V(lambda e: e.memset(ones_h[:, :], 1.0))
        V(lambda e: e.memset(epsc[:, :], LN_EPS))
        V(lambda e: e.memset(strips[96:128, 2:4, :], 0.0))
        c_g5 = V(lambda e: e.tensor_copy(g5_f[:, :], g5_i[:, :]), k_g5)
        c_thr = V(lambda e: e.tensor_scalar(thr[:, :], g5_f[:, :], float(1 << SRC_BITS), None, ALU.mult), c_g5)
        rm = V(lambda e: e.tensor_tensor_scan(run_max, cm_all, cm_all, 0.0, ALU.max, ALU.max), cm_ld)
        for t in range(NG // 125):
            st = V(lambda e, t=t: e.tensor_scalar(cm_all, run_max, thr[:, t:t + 1], 0.0, ALU.is_lt, ALU.add, accum_out=start_f[:, t:t + 1]), rm, c_thr)
            rm = st
        st_u = V(lambda e: e.tensor_copy(start_u[:, :], start_f[:, :]), st)
        for t in range(NG // 125):
            gat = dma("pool", lambda e, t=t: e.indirect_dma_start(
                out=win[0:125, t, :], out_offset=None, in_=win_dram,
                in_offset=bass.IndirectOffsetOnAxis(ap=start_u[0:125, t:t + 1], axis=0)), (st_u, win_ok), s_gather)
        u1 = V(lambda e: e.tensor_copy(word_i[0:125, :], win[0:125, :, :].rearrange("p t w -> p (t w)")), gat)
        u2 = V(lambda e: e.tensor_scalar(place_i[0:125, :], word_i[0:125, :], P - 1, None, ALU.bitwise_and), u1)
        u3 = V(lambda e: e.tensor_scalar(tile_i[0:125, :], word_i[0:125, :], 7, 31, ALU.logical_shift_right, ALU.bitwise_and))
        u4 = V(lambda e: e.tensor_scalar(dest_i[0:125, :], word_i[0:125, :], SRC_BITS, None, ALU.logical_shift_right))
        u5 = V(lambda e: e.tensor_copy(place_f[0:125, :], place_i[0:125, :]), u2)
        for t in range(NG // 125):
            u6 = V(lambda e, t=t: e.tensor_scalar(code_f[0:125, t * WINDOW:(t + 1) * WINDOW], dest_i[0:125, t * WINDOW:(t + 1) * WINDOW],
                                                  g5_f[0:125, t:t + 1], float(NT), ALU.subtract, ALU.mult), u4)
        u7 = V(lambda e: e.tensor_tensor(code_f[0:125, :], code_f[0:125, :], tile_i[0:125, :], ALU.add), u6, u3)
        turned = None
        n_turn = 0
        bank_free = [None] * 8
        for srcf, dstT, ready in ((place_f, placeT, u5), (code_f, codeT, u7)):
            for r in range(2):
                for t0 in range(0, NG // 125, 4):
                    tn = min(4, NG // 125 - t0)
                    b = n_turn % 4
                    for t in range(t0, t0 + tn):
                        last = t == t0 + tn - 1
                        tok = put("pe", lambda e, t=t, t0=t0, b=b, s=srcf, r=r: e.transpose(
                            ps[:, b, (t - t0) * 125:(t - t0 + 1) * 125], s[0:125, t * WINDOW + r * P:t * WINDOW + r * P + P], ident_f[0:125, 0:125]),
                            (ready, c_idf, bank_free[b]), pe if last else None)
                    bank_free[b] = turned = V(lambda e, d=dstT, r=r, t0=t0, tn=tn, b=b: e.tensor_copy(
                        d[:, r, t0 * 125:(t0 + tn) * 125], ps[:, b, 0:tn * 125]), tok)
                    n_turn += 1

        V(lambda e: e.memset(ef[96:128, :, :], 0.0), (pe.sem, pe.value))

        for a in range(NT):
            V(lambda e, a=a: e.bn_stats(bn6[:, a, :], xt[:, a, :]), x_in)
        t0 = (dve.sem, dve.value)
        for a in range(NT):
            t1 = V(lambda e, a=a: e.bn_aggr(mv[:, a, :], bn6[:, a, :]), t0)
        t2 = A(lambda e: e.activation(rstd[:, :], mv[:, :, 1], ACT.Sqrt, bias=epsc[:, 0:1]), t1)
        t3 = V(lambda e: e.reciprocal(rstd[:, :], rstd[:, :]), t2)
        t4 = V(lambda e: e.scalar_tensor_tensor(out=nmr[:, :], in0=mv[:, :, 0], scalar=-1.0, in1=rstd[:, :], op0=ALU.mult, op1=ALU.mult), t3)
        feat_ready = [None] * NT
        for a in range(NT):
            t5 = A(lambda e, a=a: e.activation(h0[:, a, :], xt[:, a, :], ACT.Identity, bias=nmr[:, a:a + 1], scale=rstd[:, a:a + 1]), t4)
            t6 = A(lambda e, a=a: e.activation(feat[:, a, 0:D], h0[:, a, :], ACT.Copy, scale=FEATURE_SCALE), t5)
            feat_ready[a] = V(lambda e, a=a: e.scalar_tensor_tensor(out=feat[:, a, D:2 * D], in0=h0[:, a, :], scalar=FEATURE_SCALE,
                                                                    in1=feat[:, a, 0:D], op0=ALU.mult, op1=ALU.subtract), t6)

        for b in range(FB):
            q1 = A(lambda e, b=b: e.activation(work[:, b, :], gw1[:, b, :], ACT.Square, accum_out=nrm[:, b:b + 1]), w_in)
        q2 = A(lambda e: e.activation(nrm[:, :], nrm[:, :], ACT.Sqrt), q1)
        q3 = V(lambda e: e.scalar_tensor_tensor(out=amax[:, :], in0=alpha[:, :], scalar=-1.0, in1=alpha[:, :], op0=ALU.mult, op1=ALU.max), w_in)
        q3 = V(lambda e: e.tensor_scalar(amax[:, :], amax[:, :], 1.0, None, ALU.max), q3)
        q4 = V(lambda e: e.scalar_tensor_tensor(out=gb1s[:, :], in0=gb1c[:, :], scalar=-1.0, in1=gb1c[:, :], op0=ALU.mult, op1=ALU.max))
        q5 = V(lambda e: e.scalar_tensor_tensor(out=invs[:, :], in0=nrm[:, :], scalar=16.0, in1=gb1s[:, :], op0=ALU.mult, op1=ALU.add), q2, q4)
        q6 = V(lambda e: e.tensor_scalar(invs[:, :], invs[:, :], amax[:, 0:1], 1.0 / HALF_TOP, ALU.mult, ALU.mult), q5)
        q7 = V(lambda e: e.tensor_scalar(invs[:, :], invs[:, :], 1e-30, None, ALU.max), q6)
        q8 = V(lambda e: e.reciprocal(scl[:, :], invs[:, :]), q7)
        q9 = V(lambda e: e.tensor_tensor(gb1s[:, :], gb1c[:, :], scl[:, :], ALU.mult), q8)
        for b in range(FB):
            q10 = V(lambda e, b=b: e.tensor_scalar(gw1[:, b, :], gw1[:, b, :], scl[:, b:b + 1], 1.0 / FEATURE_SCALE, ALU.mult, ALU.mult), q8)
        for b in range(FB):
            q11 = V(lambda e, b=b: e.tensor_scalar(gb1b[:, :], iota_f[:, :], 0.0, gb1s[:, b:b + 1], ALU.mult, ALU.add), q9, (pe.sem, pe.value))
            q12 = put("pe", lambda e, b=b: e.matmul(ps[:, 7, 0:P], gb1b[:, :], ident_f[:, :], start=True, stop=True), (q11,), pe)
            q13 = V(lambda e, b=b: e.tensor_copy(gb1row[:, b * P:(b + 1) * P], ps[:, 7, 0:P]), q12)
            bank_free[7] = q13
        for w, wT, ready in ((gw1, gw1T, q10), (gw2, gw2T, w_in)):
            for ob in range(FB):
                for fb in range(FB):
                    tok = put("pe", lambda e, w=w, ob=ob, fb=fb: e.transpose(ps[:, 7, 0:P], w[:, ob, fb * P:(fb + 1) * P], ident_f[:, :]), (ready, bank_free[7], c_idf), pe)
                    if wT is gw1T:
                        bank_free[7] = V(lambda e, ob=ob, fb=fb: e.tensor_copy(gw1T[:, fb, ob * P:(ob + 1) * P], ps[:, 7, 0:P]), tok)
                    else:
                        bank_free[7] = V(lambda e, ob=ob, fb=fb: e.tensor_scalar(gw2T[:, fb, ob * P:(ob + 1) * P], ps[:, 7, 0:P], invs[:, fb:fb + 1], None, ALU.mult), tok)
        weights_ready = bank_free[7]

        s_oh, s_used, s_quad, s_quad_out = sig("onehots_made"), sig("onehots_used"), sig("quad_counted"), sig("quad_copied")
        s_turn, s_turn_out, s_p1, s_hi, s_lo = sig("tiles_turned"), sig("turned_copied"), sig("p1_summed"), sig("ef_high"), sig("ef_rest")
        s_st = [[sig(f"stored_{side}_{b}") for b in range(2)] for side in ("src", "dst")]
        used = [None] * NG
        quad_out = [None, None]
        turn_out = [None, None]
        p1_out = [(None, None), (None, None)]
        src_stored = [None, None]
        dst_stored = [None, None]
        src_read = [None, None]
        dst_read = [None, None]
        n_quad = n_tg = 0

        def p1(bank, counts, rows, ready, free, done):
            for a in range(NT):
                for part in range(2):
                    fin = a == NT - 1 and part == 1
                    tok = put("pe", lambda e, a=a, part=part: e.matmul(
                        ps[0:rows, bank, 0:D], counts[:, a, :], feat[:, a, part * D:(part + 1) * D],
                        start=a == 0 and part == 0, stop=a == NT - 1 and part == 1),
                        tuple(free) + (ready, feat_ready[a]), done if fin else None)
            return tok

        def split_ef(bank, s, summed, extra=()):
            hi = put("act", lambda e: e.activation(ef[0:SROWS, s, 0:D], ps[0:SROWS, bank, 0:D], ACT.Copy, scale=binv[0:SROWS, s:s + 1]), (summed,) + tuple(extra), s_hi)
            lo = put("dve", lambda e: e.scalar_tensor_tensor(out=ef[0:SROWS, s, D:2 * D], in0=ps[0:SROWS, bank, 0:D], scalar=binv[0:SROWS, s:s + 1],
                                                             in1=ef[0:SROWS, s, 0:D], op0=ALU.mult, op1=ALU.subtract), (summed, hi), s_lo)
            return hi, lo

        behind = []

        def after_strip(s, strip_ready):
            nonlocal n_tg
            slot = s % 2
            counts = strips[:, slot, 0:NT * SROWS].rearrange("p (a j) -> p a j", j=SROWS)
            pieces = []
            state = {}

            def turn(k):
                def go():
                    nonlocal n_tg
                    a0, an = TGROUPS[k]
                    b = n_tg % 2
                    n_tg += 1
                    for a in range(a0, a0 + an):
                        tok = put("pe", lambda e, a=a: e.transpose(bank_h(2 + b)[0:SROWS, (a - a0) * P:(a - a0 + 1) * P], counts[:, a, :], ident_h[:, :]),
                                  (strip_ready, turn_out[b], c_idh), s_turn if a == a0 + an - 1 else None)
                    turn_out[b] = put("act", lambda e: e.activation(strips[0:SROWS, 2 + slot, a0 * P:(a0 + an) * P], bank_h(2 + b)[0:SROWS, 0:an * P], ACT.Copy,
                                                                    accum_out=degj[0:SROWS, slot, k:k + 1]),
                                      (tok, dst_stored[slot], dst_read[slot], state.get("deg_free")), s_turn_out)
                    state["turned"] = turn_out[b]
                return go

            def store():
                src_stored[slot] = dma("sp", lambda e: e.dma_start(srcside_dram[s], strips[:, slot, 0:NT * SROWS]), (strip_ready,), s_st[0][slot])
                r1 = V(lambda e: e.tensor_reduce(binv[0:SROWS, s:s + 1], degj[0:SROWS, slot, :], AX.X, ALU.add), state["turned"])
                r2 = V(lambda e: e.tensor_scalar(binv[0:SROWS, s:s + 1], binv[0:SROWS, s:s + 1], 1.0, None, ALU.max), r1)
                state["binv"] = V(lambda e: e.reciprocal(binv[0:SROWS, s:s + 1], binv[0:SROWS, s:s + 1]), r2)
                dst_stored[slot] = dma("sp", lambda e: e.dma_start(dstside_dram[s], strips[:, 2 + slot, :]), (state["turned"], zero_pad), s_st[1][slot])

            def product():
                bank = 4 + s % 2
                tok = p1(bank, counts, SROWS, strip_ready, p1_out[s % 2], s_p1)
                src_read[slot] = tok
                p1_out[s % 2] = split_ef(bank, s, tok, (state["binv"], zero_pad))

            def source_degrees():
                for a in range(NT):
                    dst_read[slot] = put("pe", lambda e, a=a: e.matmul(
                        ps[:, 6, a:a + 1], strips[:, 2 + slot, a * P:(a + 1) * P], ones_h[:, :], start=s == 0 and a == 0,
                        stop=s == NS - 1 and a == NT - 1, skip_group_check=True), (state["turned"], zero_pad), s_p1 if a == NT - 1 else None)

            for k in range(len(TGROUPS)):
                pieces.append(turn(k))
            pieces += [store, product, source_degrees]
            return pieces

        zero_pad = (dve.sem, dve.value)
        for s in range(NS):
            slot = s % 2
            strip_view = strips[:, slot, 0:NT * SROWS].rearrange("p (a j) -> p j a", j=SROWS)
            for q0, qn in QUADS:
                b = n_quad % 2
                n_quad += 1
                for gi in range(q0, q0 + qn):
                    g = s * STRIP_GROUPS + gi
                    ring = g % 8
                    for r in range(2):
                        put("dve", lambda e, g=g, ring=ring, r=r: e.tensor_scalar(ohA[:, ring, r, 0:GC], iota_h[:, 0:GC], codeT[:, r, g:g + 1], None, ALU.is_equal),
                            (used[g - 8] if g >= 8 else None, turned, c_ih), None)
                        made = put("dve", lambda e, g=g, ring=ring, r=r: e.tensor_scalar(ohQ[:, ring, r, :], iota_h[:, :], placeT[:, r, g:g + 1], None, ALU.is_equal),
                                   (), s_oh if r == 1 else None)
                    for r in range(2):
                        used[g] = put("pe", lambda e, gi=gi, ring=ring, r=r, b=b, q0=q0: e.matmul(
                            ps[:, b, (gi - q0) * GC:(gi - q0 + 1) * GC], ohQ[:, ring, r, :], ohA[:, ring, r, 0:GC], start=r == 0, stop=r == 1),
                            (made, quad_out[b], turned), s_used if r == 1 else None)
                quad_out[b] = put("act", lambda e, v=strip_view, q0=q0, qn=qn, b=b: e.activation(
                    v[:, q0 * GROUP:(q0 + qn) * GROUP, :], ps[:, b, 0:qn * GC].rearrange("p (j a) -> p j a", a=NT), ACT.Copy),
                    (used[g], src_stored[slot], src_read[slot]), s_quad_out)
                if behind:
                    behind.pop(0)()
            while behind:
                behind.pop(0)()
            behind = after_strip(s, quad_out[b])
        while behind:
            behind.pop(0)()
        dv1 = V(lambda e: e.tensor_scalar(dinv[:, :], ps[:, 6, 0:NT], 1.0, None, ALU.max), dst_read[(NS - 1) % 2])
        dinv_ready = V(lambda e: e.reciprocal(dinv[:, :], dinv[:, :]), dv1)

        s_blk = [sig(f"block_loaded_{b}") for b in range(2)]
        s_p2, s_p2_out, s_wp, s_post = sig("p2_summed"), sig("p2_copied"), sig("weight_product"), sig("node_rows_done")
        s_sr = [sig(f"strip_loaded_{b}") for b in range(4)]
        blk_read = [(w, w2) for w, w2 in ((st, st), (st, st))]
        p2_out = [None, None]
        stT_free = [None, None]
        wp_out = [bank_free[7], bank_free[7]]
        n_blk = 0
        n_tile = 0

        def p2_layer(wT, ef_ready, post):
            nonlocal n_blk, n_tile
            stored = [d for d in src_stored + dst_stored]
            waiting = None

            def weight(bi, buf, copied):
                nonlocal n_tile
                b0, bn = BLOCKS[bi]
                for k in range(bn):
                    bank = 4 + n_tile % 2
                    for fb in range(FB):
                        tok = put("pe", lambda e, fb=fb, k=k, bank=bank, buf=buf: e.matmul(
                            ps[:, bank, 0:D], stT[:, buf, fb, k * P:(k + 1) * P], wT[:, fb, :], start=fb == 0, stop=fb == FB - 1),
                            (copied, wp_out[n_tile % 2], weights_ready), s_wp if fb == FB - 1 else None)
                    wp_out[n_tile % 2] = post(b0 + k, bank, tok)
                    n_tile += 1
                stT_free[buf] = tok

            for bi, (b0, bn) in enumerate(BLOCKS):
                buf = n_blk % 2
                n_blk += 1
                w = bn * P
                loaded = dma("sp", lambda e, b0=b0, w=w, buf=buf: e.dma_start(
                    blocks[:, buf, :, 0:w], dstside_dram.rearrange("s p n -> p s n")[:, :, b0 * P:b0 * P + w]),
                    tuple(stored) + tuple(blk_read[buf]), s_blk[buf])
                for s in range(NS):
                    for fb in range(FB):
                        for part in range(2):
                            fin = s == NS - 1 and fb == FB - 1 and part == 1
                            tok = put("pe", lambda e, s=s, fb=fb, part=part, buf=buf, w=w: e.matmul(
                                ps[:, 2 * buf + fb, 0:w], ef[:, s, part * D + fb * P:part * D + (fb + 1) * P], blocks[:, buf, s, 0:w],
                                start=s == 0 and part == 0, stop=s == NS - 1 and part == 1),
                                (loaded, ef_ready, p2_out[buf], zero_pad), s_p2 if fin else None)
                blk_read[buf] = (tok, tok)
                for fb in range(FB):
                    p2_out[buf] = put("act", lambda e, fb=fb, buf=buf, w=w: e.activation(stT[:, buf, fb, 0:w], ps[:, 2 * buf + fb, 0:w], ACT.Copy),
                                      (tok, stT_free[buf]), s_p2_out)
                if waiting:
                    weight(*waiting)
                waiting = (bi, buf, p2_out[buf])
            weight(*waiting)
            return tok

        p2_out = list(quad_out)
        p2_out = [quad_out[1], turn_out[1]]
        stT_free = [used[NG - 1], used[NG - 1]]

        def prelu_into(dst_ap, u, tok):
            m = V(lambda e: e.tensor_scalar(work[:, 3, :], u, 0.0, alpha[:, 0:1], ALU.min, ALU.mult), tok)
            return V(lambda e: e.scalar_tensor_tensor(out=dst_ap, in0=u, scalar=0.0, in1=work[:, 3, :], op0=ALU.max, op1=ALU.add), m)

        feat2_ready = [None] * NT

        def post1(a, bank, summed):
            u = V(lambda e: e.scalar_tensor_tensor(out=work[:, 0, :], in0=ps[:, bank, 0:D], scalar=dinv[:, a:a + 1], in1=gb1row[:, :], op0=ALU.mult, op1=ALU.add), summed, dinv_ready)
            v = prelu_into(work[:, 1, :], work[:, 0, :], u)
            hi = V(lambda e: e.tensor_copy(feat[:, a, 0:D], work[:, 1, :]), v)
            feat2_ready[a] = V(lambda e: e.tensor_tensor(feat[:, a, D:2 * D], work[:, 1, :], feat[:, a, 0:D], ALU.subtract), hi)
            return u

        ef_ready = p1_out[(NS - 1) % 2][1]
        last_p2 = p2_layer(gw1T, ef_ready, post1)

        feat_ready = feat2_ready
        ring_read = [src_stored[0], src_stored[1], dst_stored[0], dst_stored[1]]
        for s in range(NS):
            slot = s % 4
            loaded = dma("sp", lambda e, s=s, slot=slot: e.dma_start(strips[:, slot, 0:NT * SROWS], srcside_dram[s]),
                         (src_stored[0], src_stored[1], dst_stored[0], dst_stored[1], dst_read[0], dst_read[1], ring_read[slot]), s_sr[slot])
            counts = strips[:, slot, 0:NT * SROWS].rearrange("p (a j) -> p a j", j=SROWS)
            bank = 6 + s % 2
            free = p1_out[s % 2] if s >= 2 else (dv1, bank_free[7])
            tok = p1(bank, counts, SROWS, loaded, free, s_p1)
            ring_read[slot] = tok
            p1_out[s % 2] = split_ef(bank, s, tok, (last_p2,))
        ef_ready = p1_out[(NS - 1) % 2][1]

        s_yt, s_yt_out = sig("y_turned"), sig("y_turned_copied")
        yt_out = [p1_out[0], p1_out[1]]
        n_yt = 0

        def post2(a, bank, summed):
            nonlocal n_yt
            u = V(lambda e: e.scalar_tensor_tensor(out=work[:, 0, :], in0=ps[:, bank, 0:D], scalar=dinv[:, a:a + 1], in1=gb2row[:, :], op0=ALU.mult, op1=ALU.add), summed, dinv_ready)
            u2 = V(lambda e: e.tensor_tensor(work[:, 0, :], work[:, 0, :], h0[:, a, :], ALU.add), u)
            v = prelu_into(work[:, 1, :], work[:, 0, :], u2)
            w = V(lambda e: e.tensor_tensor(xt[:, a, :], xt[:, a, :], work[:, 1, :], ALU.add), v)
            b6 = V(lambda e: e.bn_stats(bn6[:, a, :], xt[:, a, :]), w)
            ag = V(lambda e: e.bn_aggr(mv[:, a, :], bn6[:, a, :]), b6)
            sq = A(lambda e: e.activation(rstd[:, a:a + 1], mv[:, a, 1:2], ACT.Sqrt, bias=epsc[:, 0:1]), ag)
            rc = V(lambda e: e.reciprocal(rstd[:, a:a + 1], rstd[:, a:a + 1]), sq)
            y = V(lambda e: e.tensor_scalar(h0[:, a, :], xt[:, a, :], mv[:, a, 0:1], rstd[:, a:a + 1], ALU.subtract, ALU.mult), rc)
            k = n_yt % 2
            n_yt += 1
            for fb in range(FB):
                tok = put("pe", lambda e, fb=fb: e.transpose(ps[:, 6 + k, fb * P:(fb + 1) * P], h0[:, a, fb * P:(fb + 1) * P], ident_f[:, :]), (y,) + tuple(yt_out[k]), s_yt if fb == FB - 1 else None)
            c = put("act", lambda e: e.activation(yT[:, :, a * P:(a + 1) * P], ps[:, 6 + k, 0:D].rearrange("p (b q) -> p b q", b=FB), ACT.Copy), (tok,), s_yt_out)
            for fb in range(FB):
                tok = put("pe", lambda e, fb=fb: e.matmul(ps[:, 6 + k, D:D + NE], yT[:, fb, a * P:(a + 1) * P], gatew[:, fb, :], start=fb == 0, stop=fb == FB - 1), (c, w_in), s_yt if fb == FB - 1 else None)
            lg = V(lambda e: e.tensor_tensor(logit[:, a, :], ps[:, 6 + k, D:D + NE], gatebr[:, :], ALU.add), tok)
            yt_out[k] = (lg, c)
            return u

        p2_layer(gw2T, ef_ready, post2)

        m1 = V(lambda e: e.tensor_reduce(red[:, :], logit[:, :, :], AX.X, ALU.max), (dve.sem, dve.value))
        m2 = V(lambda e: e.tensor_tensor(logit[:, :, :], logit[:, :, :], red[:, :].rearrange("p (a o) -> p a o", o=1).broadcast_to([P, NT, NE]), ALU.subtract), m1)
        m3 = A(lambda e: e.activation(cw[:, :, :], logit[:, :, :], ACT.Exp), m2)
        m4 = V(lambda e: e.tensor_reduce(red[:, :], cw[:, :, :], AX.X, ALU.add), m3)
        m5 = V(lambda e: e.reciprocal(red[:, :], red[:, :]), m4)
        m6 = V(lambda e: e.tensor_tensor(cw[:, :, :], cw[:, :, :], red[:, :].rearrange("p (a o) -> p a o", o=1).broadcast_to([P, NT, NE]), ALU.mult), m5)
        for k in range(NE):
            m7 = V(lambda e, k=k: e.tensor_tensor(cmp1[:, k * NT:(k + 1) * NT, :], cw[:, :, :], cw[:, :, k:k + 1].broadcast_to([P, NT, NE]), ALU.is_gt), m6)
        m8 = V(lambda e: e.tensor_reduce(rank[:, :, :].rearrange("p a k -> p k a"), cmp1[:, :, :].rearrange("p (k a) n -> p k a n", k=NE), AX.X, ALU.add), m7)
        for k in range(1, NE):
            m9 = V(lambda e, k=k: e.tensor_tensor(cmp1[:, k * NT:(k + 1) * NT, 0:k], cw[:, :, 0:k], cw[:, :, k:k + 1].broadcast_to([P, NT, k]), ALU.is_equal), m8)
        for k in range(1, NE):
            m10 = V(lambda e, k=k: e.tensor_reduce(red[:, :], cmp1[:, k * NT:(k + 1) * NT, 0:k], AX.X, ALU.add), m9)
            m9 = V(lambda e, k=k: e.tensor_tensor(rank[:, :, k], rank[:, :, k], red[:, :], ALU.add), m10)
        m11 = V(lambda e: e.tensor_scalar(rank[:, :, :], rank[:, :, :], 2.0, None, ALU.is_lt), m9)
        cw_ready = V(lambda e: e.tensor_tensor(cw[:, :, :], cw[:, :, :], rank[:, :, :], ALU.mult), m11)

        s_we = [sig(f"expert_loaded_{b}") for b in range(2)]
        s_g1, s_gelu, s_g2, s_acc = sig("hidden_summed"), sig("hidden_gelu"), sig("expert_summed"), sig("expert_added")
        blocks_read = blk_read[0][0] if n_blk % 2 else blk_read[1][0]
        b2_in = dma("act", lambda e: e.dma_start(b2sb, b2), (blocks_read,), sig("b2_loaded"))
        y_all = (s_yt_out.sem, s_yt_out.value)
        cwt_out = [cw_ready, cw_ready]
        for a in range(NT):
            k = a % 2
            tok = put("pe", lambda e, a=a, k=k: e.transpose(ps[0:NE, 6 + k, 0:P], cw[:, a, :], ident_f[:, :]), (cw_ready, cwt_out[k]), pe)
            c = V(lambda e, k=k: e.tensor_copy(cwT[:, k, :], ps[0:NE, 6 + k, 0:P]), tok)
            tok = put("pe", lambda e, k=k: e.matmul(ps[:, 6 + k, P:P + D], cwT[:, k, :], b2sb, start=True, stop=True), (c, b2_in), pe)
            cwt_out[k] = V(lambda e, a=a, k=k: e.tensor_tensor(xt[:, a, :], xt[:, a, :], ps[:, 6 + k, P:P + D], ALU.add), tok)
        x_acc = [cwt_out[(NT - 1) % 2]] * NT
        g1_out = [p2_out[0], p2_out[0], p2_out[1], p2_out[1]]
        hid_read = [None, None]
        g2_out = list(wp_out)
        w_read = [blocks_read] * 2
        n1 = n2 = nh = 0
        for ex in range(NE):
            wb = ex % 2
            dma("sp", lambda e, ex=ex, wb=wb: e.dma_start(w1e[:, wb, :, :], W1[ex].rearrange("(b p) h -> p b h", p=P)), (w_read[wb],), s_we[wb])
            w_ok = dma("sp", lambda e, ex=ex, wb=wb: e.dma_start(w2e[:, wb, :, :], W2[ex].rearrange("(b p) f -> p b f", p=P)), (w_read[wb],), s_we[wb])
            for b0, bn in BLOCKS:
                w = bn * P
                hb2 = nh % 2
                nh += 1
                for hb in range(HB):
                    bank = n1 % 4
                    n1 += 1
                    for fb in range(FB):
                        tok = put("pe", lambda e, hb=hb, fb=fb, bank=bank, wb=wb, b0=b0, w=w: e.matmul(
                            ps[:, bank, 0:w], w1e[:, wb, fb, hb * P:(hb + 1) * P], yT[:, fb, b0 * P:b0 * P + w], start=fb == 0, stop=fb == FB - 1),
                            (w_ok, y_all, g1_out[bank]), s_g1 if fb == FB - 1 else None)
                    g1_out[bank] = gelu = put("act", lambda e, hb=hb, hb2=hb2, bank=bank, w=w, ex=ex: e.activation(
                        hT[:, hb2, hb, 0:w], ps[:, bank, 0:w], ACT.Gelu, bias=b1sb[:, ex, hb:hb + 1]), (tok, hid_read[hb2], w_in), s_gelu)
                for k in range(bn):
                    bank = 4 + n2 % 2
                    for hb in range(HB):
                        tok = put("pe", lambda e, hb=hb, hb2=hb2, k=k, bank=bank, wb=wb: e.matmul(
                            ps[:, bank, 0:D], hT[:, hb2, hb, k * P:(k + 1) * P], w2e[:, wb, hb, :], start=hb == 0, stop=hb == HB - 1),
                            (gelu, g2_out[n2 % 2]), s_g2 if hb == HB - 1 else None)
                    a = b0 + k
                    g2_out[n2 % 2] = x_acc[a] = put("dve", lambda e, a=a, bank=bank, ex=ex: e.scalar_tensor_tensor(
                        out=xt[:, a, :], in0=ps[:, bank, 0:D], scalar=cw[:, a, ex:ex + 1], in1=xt[:, a, :], op0=ALU.mult, op1=ALU.add), (tok, x_acc[a]), s_acc)
                    n2 += 1
                hid_read[hb2] = tok
            w_read[wb] = tok

        s_out = sig("out_stored")
        dma("sp", lambda e: e.dma_start(out[0:(NT - 1) * P, :].rearrange("(a q) f -> q a f", q=P), xt[:, 0:NT - 1, :]), (x_acc[NT - 2], x_acc[NT - 1]), s_out)
        fin = dma("sp", lambda e: e.dma_start(out[(NT - 1) * P:N, :], xt[0:TAIL, NT - 1, :]), (x_acc[NT - 1],), s_out)
        put("sp", lambda e: e.nop(), (fin,), None)

        ctx.enter_context(nc.allow_non_contiguous_dma(reason="bias columns, a few kilobytes"))
        block = ctx.enter_context(nc.Block())

        @block.tensor
        def _(e):
            prog.emit("pe", e)

        @block.scalar
        def _(e):
            prog.emit("act", e)

        @block.vector
        def _(e):
            prog.emit("dve", e)

        @block.gpsimd
        def _(e):
            prog.emit("pool", e)

        @block.sync
        def _(e):
            prog.emit("sp", e)


_INS = ["x", "src", "dst", "L0_gnn_W1", "L0_gnn_b1", "L0_gnn_W2", "L0_gnn_b2", "L0_gnn_prelu_a", "L0_ffn_gate_w",
        "L0_ffn_gate_b", "L0_ffn_W1", "L0_ffn_b1", "L0_ffn_W2", "L0_ffn_b2"]


def kernel(**inputs):
    import numpy as np
    import concourse.bacc as bacc
    from concourse.bass_utils import run_bass_kernel_spmd

    nc = bacc.Bacc("TRN2", target_bir_lowering=False, num_devices=1)
    arrays, args = {}, []
    for name in _INS:
        a = np.ascontiguousarray(inputs[name])
        a = a.reshape(a.shape or (1,))
        arrays[name] = a
        args.append(nc.dram_tensor(name, a.shape, mybir.dt.from_np(a.dtype), kind="ExternalInput").ap())
    out = nc.dram_tensor("out", arrays["x"].shape, F32, kind="ExternalOutput").ap()
    gnn_moe_kernel(nc, *args, out)
    r = run_bass_kernel_spmd(nc, [arrays], core_ids=[0])
    return r.results[0]["out"]
```

```python
from contextlib import ExitStack

import concourse.bass as bass
from concourse import mybir

ALU = mybir.AluOpType
ACT = mybir.ActivationFunctionType
AX = mybir.AxisListType
F32 = mybir.dt.float32
F16 = mybir.dt.float16
I32 = mybir.dt.int32
U32 = mybir.dt.uint32

P = 128
GROUP = 5
STRIP_GROUPS = 25
CHUNK = 32
WINDOW = 256
SRC_BITS = 12
FEATURE_SCALE = 1024.0
HALF_TOP = 16384.0
LN_EPS = 1e-5
TOP = 2


class Signal:

    def __init__(self, sem):
        self.sem, self.value = sem, 0

    def up(self, by=1):
        self.value += by
        return (self.sem, self.value)


class Program:

    def __init__(self):
        self.queues = {"pe": [], "act": [], "dve": [], "pool": [], "sp": []}

    def put(self, engine, fn, after=(), done=None):
        token = done.up() if done is not None else None
        self.queues[engine].append((tuple(after), fn, done, 1))
        return token

    def dma(self, engine, fn, after=(), done=None):
        token = done.up(16)
        self.queues[engine].append((tuple(after), fn, done, 16))
        return token

    def emit(self, engine, eng):
        reached = {}
        for after, fn, done, by in self.queues[engine]:
            for wait in after:
                if wait is None:
                    continue
                sem, value = wait
                if reached.get(id(sem), 0) < value:
                    eng.wait_ge(sem, value)
                    reached[id(sem)] = value
            ins = fn(eng)
            if done is not None:
                ins.then_inc(done.sem, by)


def gnn_moe_kernel(nc, x, src, dst, gW1, gb1, gW2, gb2, prelu_a, gate_w, gate_b, W1, b1, W2, b2, out):
    N, D = x.shape
    E = src.shape[0]
    NE, _, H = W1.shape
    NT = -(-N // P)
    TAIL = N - (NT - 1) * P
    NG = N // GROUP
    NS = NG // STRIP_GROUPS
    SROWS = GROUP * STRIP_GROUPS
    GC = GROUP * NT
    NPAD = NT * P
    FB = D // P
    HB = H // P
    CH_ROW = 26
    EROW = CH_ROW * CHUNK
    EPARTS = 125
    NCHUNK = CH_ROW * EPARTS
    EFULL = E // EROW
    EREST = E - EFULL * EROW
    assert N == NG * GROUP and NG == NS * STRIP_GROUPS and SROWS == 125 and EPARTS * EROW > E
    NO_EDGE = float(4095 * 4096)
    QUADS = [(q, min(4, STRIP_GROUPS - q)) for q in range(0, STRIP_GROUPS, 4)]
    TGROUPS = [(0, 7), (7, 6), (13, 6), (19, 6)]
    BLOCKS = [(b, 4) for b in range(0, NT - 5, 4)] + [(NT - 5, 3), (NT - 2, 2)]
    HALVES = [(0, 13), (13, NS)]
    CAP = NPAD
    ETILES = (TOP * N + NE * (P - 1)) // P

    with ExitStack() as ctx:
        def sb(name, shape, dt):
            return ctx.enter_context(nc.sbuf_tensor(name, shape, dt))

        def sig(name):
            return Signal(ctx.enter_context(nc.semaphore(name)))

        prog = Program()
        put, dma = prog.put, prog.dma

        word_dram = nc.dram_tensor("edge_words", [NCHUNK * CHUNK + WINDOW], F32, kind="Internal").ap()
        cmax_dram = nc.dram_tensor("chunk_max", [NCHUNK], F32, kind="Internal").ap()
        win_dram = nc.dram_tensor("windows", [NCHUNK, WINDOW], F32, kind="Internal").ap()
        shared_dram = nc.dram_tensor("counts_src_side_then_rows", [NE * CAP * 2 * D], F16, kind="Internal").ap()
        COUNTS = NS * P * NT * SROWS
        srcside_dram = shared_dram[0:COUNTS].rearrange("(s p n) -> s p n", s=NS, p=P)
        sent_dram = shared_dram.rearrange("(r c) -> r c", c=2 * D)
        expert_out_dram = nc.dram_tensor("expert_rows", [ETILES * P, D], F32, kind="Internal").ap()
        dstside_dram = nc.dram_tensor("counts_dst_side", [NS, P, NPAD], F16, kind="Internal").ap()

        xt = sb("xt", [P, NT, D], F32)
        EW = 2 * FB * H + 2 * HB * D
        region = sb("region", [P, NE * EW], F16)
        feat = region[:, 0:NT * 2 * D].rearrange("p (a c) -> p a c", c=2 * D)
        strips = region[:, NT * 2 * D:NT * 2 * D + 4 * NPAD].rearrange("p (k n) -> p k n", k=4)
        SPARE = NT * 2 * D + 4 * NPAD
        ef = sb("ef", [P, NS, 2 * D], F16)
        blocks = sb("blocks", [P, 3, 13, 512], F16)
        stT = sb("stT", [P, 2, FB, 512], F32)
        edge_cols = sb("edge_cols", [P, 2, 2, NG], F32)
        edge_cols_h = edge_cols[:, :, :, :].rearrange("p a b c -> p (a b c)").bitcast(F16)
        codeT = edge_cols_h[:, 0:2 * NG].rearrange("p (g r) -> p g r", r=2)
        placeT = edge_cols_h[:, 2 * NG:4 * NG].rearrange("p (g r) -> p g r", r=2)
        iota_h = sb("iota_h", [P, P, 2], F16)
        iota_f = sb("iota_f", [P, P], F32)
        part_i = sb("part_i", [P, 1], I32)
        part_f = sb("part_f", [P, 1], F32)
        ident_h = sb("ident_h", [P, P], F16)
        ident_f = sb("ident_f", [P, P], F32)
        ones_h = sb("ones_h", [P, 1], F16)
        g5_i = sb("g5_i", [P, NG // 125], I32)
        g5_f = sb("g5_f", [P, NG // 125], F32)
        thr = sb("thr", [P, NG // 125], F32)
        start_f = sb("start_f", [P, NG // 125], F32)
        start_u = sb("start_u", [P, NG // 125], U32)
        cmax = sb("cmax", [P, CH_ROW], F32)
        work = sb("work", [P, 4, D], F32)
        gb1b = work[:, 2, 0:P]
        bn6 = sb("bn6", [P, NT, 6], F32)
        mv = sb("mv", [P, NT, 2], F32)
        rstd = sb("rstd", [P, NT], F32)
        nmr = sb("nmr", [P, NT], F32)
        rstd_s, nmr_s = sb("rstd_s", [P, NT], F32), sb("nmr_s", [P, NT], F32)
        epsc = sb("epsc", [P, 1], F32)
        degj = sb("degj", [P, 2, 4], F32)
        binv = sb("binv", [P, NS], F32)
        dinv = sb("dinv", [P, NT], F32)
        alpha = sb("alpha", [P, 1], F32)
        amax = sb("amax", [P, 1], F32)
        gw1T = sb("gw1T", [P, FB, D], F32)
        gw2T = sb("gw2T", [P, FB, D], F32)
        gb1c = sb("gb1c", [P, FB], F32)
        gb1s = sb("gb1s", [P, FB], F32)
        gb1row = sb("gb1row", [P, D], F32)
        gb2row = sb("gb2row", [P, D], F32)
        nrm = sb("nrm", [P, FB], F32)
        invs = sb("invs", [P, FB], F32)
        scl = sb("scl", [P, FB], F32)
        gatew = sb("gatew", [P, FB, NE], F32)
        gatebr = sb("gatebr", [P, NE], F32)
        stage = sb("stage", [P, 2, 2 * H], F32)
        ybuf = sb("ybuf", [P, 4, D], F32)
        hbuf = ybuf
        ycol = sb("ycol", [P, 2, D], F32)
        lower = sb("lower", [P, NE, NE], F32)
        e_row = sb("e_row", [P, NE], F32)
        tri_h = sb("tri_h", [P, P], F16)
        ones_sq = sb("ones_sq", [P, P], F16)
        ones_f = sb("ones_f", [P, P], F32)
        valid = sb("valid", [P, 1], F32)
        pr = sb("pr", [P, 4, NE], F32)
        rd = sb("rd", [P, 4], F32)
        rank = sb("rank", [P, 4, NE], F32)
        place = sb("place", [P, 4, NE], F32)
        cw = sb("cw", [P, 4, NE], F32)
        pick = sb("pick", [P, NT, TOP, NE], F32)
        pick_h = sb("pick_h", [P, 4, NE], F16)
        cmps = sb("cmps", [P, 2, 4, NE, NE], F32)
        cmp_a, cmp_b = cmps[:, 0], cmps[:, 1]
        iota_i = cmps[:, 0, 0:2, :, :].rearrange("p a b c -> p (a b c)").bitcast(I32)
        logit_acc = sb("logit_acc", [P, 4, NE], F32)
        runs = sb("runs", [P, NT + 1, NE], F32)
        wgt = sb("wgt", [P, NT, TOP], F32)
        node_row = sb("node_row", [P, NT, TOP], F32)
        node_row_u = sb("node_row_u", [P, NT, TOP], U32)
        sumsq = sb("sumsq", [P, 2 * NE + 1], F32)
        ssum = sb("ssum", [P, 3], F32)
        sW1, sW2, sH, iW1, iW2 = [sb(n, [P, 1], F32) for n in ("sW1", "sW2", "sH", "iW1", "iW2")]
        tiles_i = sb("tiles_i", [P, NE], I32)
        tiles_f = sb("tiles_f", [P, NE], F32)
        base_f = sb("base_f", [P, NE], F32)
        ends_f = sb("ends_f", [P, NE], F32)
        tcol = sb("tcol", [P, ETILES], F32)
        tile_e = sb("tile_e", [P, ETILES], F32)
        tile_b = sb("tile_b", [P, ETILES], F32)
        row_u = sb("row_u", [P, ETILES], U32)
        off_w = sb("off_w", [P, ETILES], I32)
        off_b = sb("off_b", [P, ETILES], I32)
        cols_flat = edge_cols[:, :, :, :].rearrange("p a b c -> p (a b c)")
        yrow = cols_flat[:, 0:8 * D].bitcast(F16).rearrange("p (k c) -> p k c", k=8)
        cwT = cols_flat[0:NE, 8 * D:8 * D + P]
        b2sb = cols_flat[0:NE, 8 * D + P:8 * D + P + D]

        flat = ef[:, :, :].rearrange("p a b -> p (a b)").bitcast(F32)
        W5 = (NG // 125) * WINDOW
        win = flat[:, 0:W5].rearrange("p (t w) -> p t w", w=WINDOW)
        word_i = flat[:, W5:2 * W5].bitcast(I32)
        place_i = flat[:, 2 * W5:3 * W5].bitcast(I32)
        tile_i = flat[:, 3 * W5:4 * W5].bitcast(I32)
        dest_i = flat[:, 4 * W5:5 * W5].bitcast(I32)
        blk_f = blocks[:, :, :, :].rearrange("p a b c -> p (a b c)").bitcast(F32)
        OH_RING = 4
        OHW = 4 * P * 2 // 2
        ohA, ohQ = [blk_f[:, k * OH_RING * OHW:(k + 1) * OH_RING * OHW].bitcast(F16).rearrange(
            "p (o g c r) -> p o g c r", o=OH_RING, g=4, r=2) for k in range(2)]
        run_max = blk_f[:, 0:NCHUNK]
        cm_all = blk_f[:, NCHUNK:2 * NCHUNK]
        src_i = blk_f[:, 2 * NCHUNK:2 * NCHUNK + EROW].bitcast(I32)
        dst_i = blk_f[:, 2 * NCHUNK + EROW:2 * NCHUNK + 2 * EROW].bitcast(I32)
        word_f = blk_f[:, 2 * NCHUNK + 2 * EROW:2 * NCHUNK + 3 * EROW]
        spare_f = region[:, SPARE:].bitcast(F32)
        gw1 = spare_f[:, 0:FB * D].rearrange("p (b d) -> p b d", b=FB)
        gw2 = spare_f[:, FB * D:2 * FB * D].rearrange("p (b d) -> p b d", b=FB)
        ZW = 971
        zeros = region[:, SPARE + 4 * FB * D:SPARE + 4 * FB * D + ZW]
        pad_row = blk_f[0:1, 2 * NCHUNK + 3 * EROW:2 * NCHUNK + 3 * EROW + WINDOW]
        b1rows = flat[:, 0:NE * H]
        hid = flat[:, NE * H:NE * H + 2 * H].rearrange("p (k n) -> p k n", k=2)
        yo = flat[:, NE * H + 2 * H:NE * H + 2 * H + 4 * D].rearrange("p (k n) -> p k n", k=4)
        blk_h = blk_f.bitcast(F16)
        xg = blk_h[:, 0:8 * D].rearrange("p (k n) -> p k n", k=4)
        xcol = blk_h[:, 8 * D:12 * D].rearrange("p (k n) -> p k n", k=2)
        hcol = blk_h[:, 12 * D:12 * D + 4 * H].rearrange("p (k q n) -> p k q n", k=2, q=2)
        back = blk_f[:, 4096:4096 + 8 * D].rearrange("p (k n) -> p k n", k=8)
        tile_cmp = blk_f[:, 6144:6144 + 2 * ETILES * NE].rearrange("p (q t k) -> p q t k", q=2, k=NE)
        wide = blk_f[:, 7168:7168 + NT * TOP]
        code_f = flat[:, 0:W5]
        place_f = stT[:, :, :, :].rearrange("p a b c -> p (a b c)")[:, 0:W5]

        ps = ctx.enter_context(nc.psum_tensor("ps", [P, 8, 512], F32))

        def bank_h(b):
            return ps[:, b, :].bitcast(F16)

        s_edges, s_x, s_w, s_word_st, s_cmax_st, s_cmax_ld, s_win, s_gather = [
            sig(n) for n in ("edges_loaded", "x_loaded", "weights_loaded", "words_stored", "cmax_stored",
                             "cmax_loaded", "windows_written", "windows_gathered")]
        dve, act, pool, pe = sig("dve_step"), sig("act_step"), sig("pool_step"), sig("pe_step")

        def V(fn, *after):
            return put("dve", fn, after, dve)

        def A(fn, *after):
            return put("act", fn, after, act)

        def G(fn, *after):
            return put("pool", fn, after, pool)

        k_iota = put("pool", lambda e: e.iota(iota_i[:, :], [[1, P]], base=0, channel_multiplier=0), (), pool)
        k_part = put("pool", lambda e: e.iota(part_i[:, :], [[1, 1]], base=0, channel_multiplier=1), (), pool)
        k_g5 = put("pool", lambda e: e.iota(g5_i[:, :], [[GROUP * 125, NG // 125]], base=0, channel_multiplier=GROUP), (), pool)

        pad_i = V(lambda e: e.memset(dst_i[96:128, :], 4095))
        pad_s = V(lambda e: e.memset(src_i[96:128, :], 0))
        pad_r = V(lambda e: e.memset(pad_row[:, :], NO_EDGE))
        for name, arr, tile in (("dst", dst, dst_i), ("src", src, src_i)):
            full = arr[0:EFULL * EROW].rearrange("(p m) -> p m", m=EROW)
            rest = arr[EFULL * EROW:E].rearrange("(p m) -> p m", p=1)
            dma("sp", lambda e, t=tile, f=full: e.dma_start(t[0:96, :], f[0:96, :]), (), s_edges)
            dma("sp", lambda e, t=tile, f=full: e.dma_start(t[96:EFULL, :], f[96:EFULL, :]), (pad_i, pad_s), s_edges)
            edges = dma("sp", lambda e, t=tile, r=rest: e.dma_start(t[EFULL:EFULL + 1, 0:EREST], r), (pad_i, pad_s), s_edges)

        zero_x = V(lambda e: e.memset(xt[:, NT - 1, :], 0.0))
        dma("act", lambda e: e.dma_start(xt[:, 0:NT - 1, :], x[0:(NT - 1) * P, :].rearrange("(a q) f -> q a f", q=P)), (), s_x)
        x_in = dma("act", lambda e: e.dma_start(xt[0:TAIL, NT - 1, :], x[(NT - 1) * P:N, :]), (zero_x,), s_x)
        for fn in (lambda e: e.dma_start(gw1[:, :, :], gW1.rearrange("(b p) f -> p b f", p=P)),
                   lambda e: e.dma_start(gw2[:, :, :], gW2.rearrange("(b p) f -> p b f", p=P)),
                   lambda e: e.dma_start(gb1c[:, :], gb1.rearrange("(b p) -> p b", p=P)),
                   lambda e: e.dma_start(gb2row[:, :], gb2.partition_broadcast(P)),
                   lambda e: e.dma_start(alpha[:, :], prelu_a.partition_broadcast(P)),
                   lambda e: e.dma_start(gatew[:, :, :], gate_w.rearrange("(b p) n -> p b n", p=P)),
                   lambda e: e.dma_start(gatebr[:, :], gate_b.partition_broadcast(P))):
            w_in = dma("act", fn, (), s_w)

        words = V(lambda e: e.scalar_tensor_tensor(out=word_f[0:EPARTS, :], in0=dst_i[0:EPARTS, :], scalar=float(1 << SRC_BITS),
                                                   in1=src_i[0:EPARTS, :], op0=ALU.mult, op1=ALU.add), edges)
        cm = V(lambda e: e.tensor_reduce(cmax[0:EPARTS, :], word_f[0:EPARTS, :].rearrange("p (c k) -> p c k", k=CHUNK), AX.X, ALU.max), words)
        dma("sp", lambda e: e.dma_start(word_dram[0:EPARTS * EROW].rearrange("(p m) -> p m", m=EROW), word_f[0:EPARTS, :]), (words,), s_word_st)
        words_st = dma("sp", lambda e: e.dma_start(word_dram[EPARTS * EROW:].rearrange("(p m) -> p m", p=1), pad_row[:, :]), (pad_r,), s_word_st)
        cm_st = dma("act", lambda e: e.dma_start(cmax_dram.rearrange("(p m) -> p m", m=CH_ROW), cmax[0:EPARTS, :]), (cm,), s_cmax_st)
        cm_ld = dma("act", lambda e: e.dma_start(cm_all, cmax_dram.partition_broadcast(P)), (cm_st,), s_cmax_ld)
        win_src = bass.AP(tensor=word_dram.tensor, offset=0, ap=[[CHUNK, NCHUNK], [1, WINDOW]])
        win_ok = dma("sp", lambda e: e.dma_start(win_dram, win_src), (words_st,), s_win)
        zero_z = V(lambda e: e.memset(zeros, 0.0))
        V(lambda e: e.memset(ones_sq[:, :], 1.0))
        V(lambda e: e.memset(ones_f[:, :], 1.0))
        V(lambda e: e.memset(runs[:, 0, :], 0.0))
        low0 = V(lambda e: e.memset(lower[:, :, :], 0.0))
        for k in range(1, NE):
            V(lambda e, k=k: e.memset(lower[:, k, 0:k], 1.0), low0)
        for k in range(NE):
            V(lambda e, k=k: e.memset(e_row[:, k:k + 1], float(k * CAP)))
        for r in range(2):
            c_ih = V(lambda e, r=r: e.tensor_copy(iota_h[:, :, r], iota_i[:, :]), k_iota)
        c_if = V(lambda e: e.tensor_copy(iota_f[:, :], iota_i[:, :]))
        c_pf = V(lambda e: e.tensor_copy(part_f[:, :], part_i[:, :]), k_part)
        c_idf = V(lambda e: e.tensor_scalar(ident_f[:, :], iota_f[:, :], part_f[:, 0:1], None, ALU.is_equal), c_pf)
        c_idh = V(lambda e: e.tensor_scalar(ident_h[:, :], iota_f[:, :], part_f[:, 0:1], None, ALU.is_equal))
        V(lambda e: e.memset(ones_h[:, :], 1.0))
        V(lambda e: e.tensor_scalar(tri_h[:, :], iota_f[:, :], part_f[:, 0:1], None, ALU.is_gt))
        V(lambda e: e.tensor_scalar(valid[:, :], part_f[:, :], float(TAIL), None, ALU.is_lt))
        V(lambda e: e.tensor_copy(tcol[:, :], iota_i[:, 0:ETILES]))
        zero_rows = dma("sp", lambda e: e.dma_start(
            shared_dram[COUNTS:].rearrange("(p k c) -> p k c", p=P, c=ZW),
            zeros.rearrange("p (o c) -> p o c", o=1).broadcast_to([P, (NE * CAP * 2 * D - COUNTS) // P // ZW, ZW])), (zero_z,), sig("rows_zeroed"))
        V(lambda e: e.memset(epsc[:, :], LN_EPS))
        V(lambda e: e.memset(strips[96:128, 2:4, :], 0.0))
        c_gate = V(lambda e: e.tensor_scalar(gatew[:, :, :], gatew[:, :, :], 1.0 / FEATURE_SCALE, None, ALU.mult), w_in)
        c_g5 = V(lambda e: e.tensor_copy(g5_f[:, :], g5_i[:, :]), k_g5)
        c_thr = V(lambda e: e.tensor_scalar(thr[:, :], g5_f[:, :], float(1 << SRC_BITS), None, ALU.mult), c_g5)
        for a in range(NT):
            V(lambda e, a=a: e.bn_stats(bn6[:, a, :], xt[:, a, :]), x_in)
        t0 = (dve.sem, dve.value)
        for a in range(NT):
            t1 = V(lambda e, a=a: e.bn_aggr(mv[:, a, :], bn6[:, a, :]), t0)
        t2 = A(lambda e: e.activation(rstd[:, :], mv[:, :, 1], ACT.Sqrt, bias=epsc[:, 0:1]), t1)
        t3 = V(lambda e: e.reciprocal(rstd[:, :], rstd[:, :]), t2)
        t4 = V(lambda e: e.scalar_tensor_tensor(out=nmr[:, :], in0=mv[:, :, 0], scalar=-1.0, in1=rstd[:, :], op0=ALU.mult, op1=ALU.mult), t3)
        V(lambda e: e.tensor_scalar(rstd_s[:, :], rstd[:, :], FEATURE_SCALE, None, ALU.mult))
        t4 = V(lambda e: e.tensor_scalar(nmr_s[:, :], nmr[:, :], FEATURE_SCALE, None, ALU.mult), t4)

        rm = V(lambda e: e.tensor_tensor_scan(run_max, cm_all, cm_all, 0.0, ALU.max, ALU.max), cm_ld)
        for t in range(NG // 125):
            st = V(lambda e, t=t: e.tensor_scalar(cm_all, run_max, thr[:, t:t + 1], 0.0, ALU.is_lt, ALU.add, accum_out=start_f[:, t:t + 1]), rm, c_thr)
            rm = st
        st_u = V(lambda e: e.tensor_copy(start_u[:, :], start_f[:, :]), st)
        for t in range(NG // 125):
            gat = dma("pool", lambda e, t=t: e.indirect_dma_start(
                out=win[0:125, t, :], out_offset=None, in_=win_dram,
                in_offset=bass.IndirectOffsetOnAxis(ap=start_u[0:125, t:t + 1], axis=0)), (st_u, win_ok), s_gather)
        u1 = V(lambda e: e.tensor_copy(word_i[0:125, :], win[0:125, :, :].rearrange("p t w -> p (t w)")), gat)
        u2 = V(lambda e: e.tensor_scalar(place_i[0:125, :], word_i[0:125, :], P - 1, None, ALU.bitwise_and), u1)
        u3 = V(lambda e: e.tensor_scalar(tile_i[0:125, :], word_i[0:125, :], 7, 31, ALU.logical_shift_right, ALU.bitwise_and))
        u4 = V(lambda e: e.tensor_scalar(dest_i[0:125, :], word_i[0:125, :], SRC_BITS, None, ALU.logical_shift_right))
        u5 = V(lambda e: e.tensor_copy(place_f[0:125, :], place_i[0:125, :]), u2)
        for t in range(NG // 125):
            u6 = V(lambda e, t=t: e.tensor_scalar(code_f[0:125, t * WINDOW:(t + 1) * WINDOW], dest_i[0:125, t * WINDOW:(t + 1) * WINDOW],
                                                  g5_f[0:125, t:t + 1], float(NT), ALU.subtract, ALU.mult), u4)
        u7 = V(lambda e: e.tensor_tensor(code_f[0:125, :], code_f[0:125, :], tile_i[0:125, :], ALU.add), u6, u3)
        u7 = V(lambda e: e.tensor_scalar(code_f[0:125, :], code_f[0:125, :], -1.0, float(P - 1), ALU.max, ALU.min), u7)
        turned = None
        n_turn = 0
        bank_free = [None] * 8
        for srcf, dstT, ready in ((place_f, placeT, u5), (code_f, codeT, u7)):
            for r in range(2):
                for t0 in range(0, NG // 125, 4):
                    tn = min(4, NG // 125 - t0)
                    b = n_turn % 4
                    for t in range(t0, t0 + tn):
                        last = t == t0 + tn - 1
                        tok = put("pe", lambda e, t=t, t0=t0, b=b, s=srcf, r=r: e.transpose(
                            ps[:, b, (t - t0) * 125:(t - t0 + 1) * 125], s[0:125, t * WINDOW + r * P:t * WINDOW + r * P + P], ident_f[0:125, 0:125]),
                            (ready, c_idf, bank_free[b]), pe if last else None)
                    bank_free[b] = turned = V(lambda e, d=dstT, r=r, t0=t0, tn=tn, b=b: e.tensor_copy(
                        d[:, t0 * 125:(t0 + tn) * 125, r], ps[:, b, 0:tn * 125]), tok)
                    n_turn += 1

        V(lambda e: e.memset(ef[96:128, :, :], 0.0), (pe.sem, pe.value))

        feat_ready = [None] * NT

        def normalise(a):
            t5 = A(lambda e: e.activation(hbuf[:, a % 4, :], xt[:, a, :], ACT.Identity, bias=nmr_s[:, a:a + 1], scale=rstd_s[:, a:a + 1]),
                   t4, feat_ready[a - 4] if a >= 4 else None)
            t6 = A(lambda e: e.activation(feat[:, a, 0:D], hbuf[:, a % 4, :], ACT.Copy), t5)
            feat_ready[a] = G(lambda e: e.tensor_tensor(feat[:, a, D:2 * D], hbuf[:, a % 4, :], feat[:, a, 0:D], ALU.subtract), t6)

        def prepare_graph_weights():
            for b in range(FB):
                q1 = A(lambda e, b=b: e.activation(work[:, b, :], gw1[:, b, :], ACT.Square, accum_out=nrm[:, b:b + 1]), w_in)
            q2 = A(lambda e: e.activation(nrm[:, :], nrm[:, :], ACT.Sqrt), q1)
            q3 = V(lambda e: e.scalar_tensor_tensor(out=amax[:, :], in0=alpha[:, :], scalar=-1.0, in1=alpha[:, :], op0=ALU.mult, op1=ALU.max), w_in)
            q3 = V(lambda e: e.tensor_scalar(amax[:, :], amax[:, :], 1.0, None, ALU.max), q3)
            q4 = V(lambda e: e.scalar_tensor_tensor(out=gb1s[:, :], in0=gb1c[:, :], scalar=-1.0, in1=gb1c[:, :], op0=ALU.mult, op1=ALU.max))
            q5 = V(lambda e: e.scalar_tensor_tensor(out=invs[:, :], in0=nrm[:, :], scalar=16.0, in1=gb1s[:, :], op0=ALU.mult, op1=ALU.add), q2, q4)
            q6 = V(lambda e: e.tensor_scalar(invs[:, :], invs[:, :], amax[:, 0:1], 1.0 / HALF_TOP, ALU.mult, ALU.mult), q5)
            q7 = V(lambda e: e.tensor_scalar(invs[:, :], invs[:, :], 1e-30, None, ALU.max), q6)
            q8 = V(lambda e: e.reciprocal(scl[:, :], invs[:, :]), q7)
            q9 = V(lambda e: e.tensor_tensor(gb1s[:, :], gb1c[:, :], scl[:, :], ALU.mult), q8)
            for b in range(FB):
                q10 = V(lambda e, b=b: e.tensor_scalar(gw1[:, b, :], gw1[:, b, :], scl[:, b:b + 1], 1.0 / FEATURE_SCALE, ALU.mult, ALU.mult), q8)
            for b in range(FB):
                q11 = V(lambda e, b=b: e.tensor_scalar(gb1b[:, :], iota_f[:, :], 0.0, gb1s[:, b:b + 1], ALU.mult, ALU.add), q9, (pe.sem, pe.value))
                q12 = put("pe", lambda e, b=b: e.matmul(ps[:, 7, 0:P], gb1b[:, :], ident_f[:, :], start=True, stop=True), (q11, bank_free[7], c_idf), pe)
                q13 = V(lambda e, b=b: e.tensor_copy(gb1row[:, b * P:(b + 1) * P], ps[:, 7, 0:P]), q12)
                bank_free[7] = q13
            for w, wT, ready in ((gw1, gw1T, q10), (gw2, gw2T, w_in)):
                for ob in range(FB):
                    for fb in range(FB):
                        tok = put("pe", lambda e, w=w, ob=ob, fb=fb: e.transpose(ps[:, 7, 0:P], w[:, ob, fb * P:(fb + 1) * P], ident_f[:, :]), (ready, bank_free[7], c_idf), pe)
                        if wT is gw1T:
                            bank_free[7] = V(lambda e, ob=ob, fb=fb: e.tensor_copy(gw1T[:, fb, ob * P:(ob + 1) * P], ps[:, 7, 0:P]), tok)
                        else:
                            bank_free[7] = V(lambda e, ob=ob, fb=fb: e.tensor_scalar(gw2T[:, fb, ob * P:(ob + 1) * P], ps[:, 7, 0:P], invs[:, fb:fb + 1], None, ALU.mult), tok)
            return bank_free[7]

        s_oh, s_used, s_quad, s_quad_out = sig("onehots_made"), sig("onehots_used"), sig("quad_counted"), sig("quad_copied")
        s_turn, s_turn_out, s_p1, s_hi, s_lo = sig("tiles_turned"), sig("turned_copied"), sig("p1_summed"), sig("ef_high"), sig("ef_rest")
        s_st = [[sig(f"stored_{side}_{b}") for b in range(2)] for side in ("src", "dst")]
        used = []
        quad_out = [None, None]
        turn_out = [None, None]
        p1_out = [(None, None), (None, None)]
        src_stored = [None, None]
        dst_stored = [None, None]
        src_read = [None, None]
        dst_read = [None, None]
        n_quad = n_tg = 0

        def p1(bank, counts, rows, ready, free, done):
            for a in range(NT):
                for part in range(2):
                    fin = a == NT - 1 and part == 1
                    tok = put("pe", lambda e, a=a, part=part: e.matmul(
                        ps[0:rows, bank, 0:D], counts[:, a, :], feat[:, a, part * D:(part + 1) * D],
                        start=a == 0 and part == 0, stop=a == NT - 1 and part == 1),
                        tuple(free) + (ready, feat_ready[a]), done if fin else None)
            return tok

        def split_ef(bank, s, summed, extra=()):
            hi = put("act", lambda e: e.activation(ef[0:SROWS, s, 0:D], ps[0:SROWS, bank, 0:D], ACT.Copy, scale=binv[0:SROWS, s:s + 1]), (summed,) + tuple(extra), s_hi)
            lo = put("dve", lambda e: e.scalar_tensor_tensor(out=ef[0:SROWS, s, D:2 * D], in0=ps[0:SROWS, bank, 0:D], scalar=binv[0:SROWS, s:s + 1],
                                                             in1=ef[0:SROWS, s, 0:D], op0=ALU.mult, op1=ALU.subtract), (summed, hi), s_lo)
            return hi, lo

        QUAD_BANKS = (0, 1, 7)
        quad_out = [None] * 3
        split_due = None
        weights_ready = None

        def work_on(s, strip_ready):
            slot = s % 2
            counts = strips[:, slot, 0:NT * SROWS].rearrange("p (a j) -> p a j", j=SROWS)
            state = {}

            def turn(k):
                a0, an = TGROUPS[k]
                b = k % 2
                for a in range(a0, a0 + an):
                    tok = put("pe", lambda e, a=a: e.transpose(bank_h(2 + b)[0:SROWS, (a - a0) * P:(a - a0 + 1) * P], counts[:, a, :], ident_h[:, :]),
                              (strip_ready, turn_out[b], c_idh), s_turn if a == a0 + an - 1 else None)
                turn_out[b] = put("act", lambda e: e.activation(strips[0:SROWS, 2 + slot, a0 * P:(a0 + an) * P], bank_h(2 + b)[0:SROWS, 0:an * P], ACT.Copy,
                                                                accum_out=degj[0:SROWS, slot, k:k + 1]),
                                  (tok, dst_stored[slot], dst_read[slot], deg_read[slot]), s_turn_out)
                if k == len(TGROUPS) - 1:
                    state["turned"] = turn_out[b]
                    dst_stored[slot] = dma("sp", lambda e: e.dma_start(dstside_dram[s], strips[:, 2 + slot, :]), (turn_out[b], zero_pad), s_st[1][slot])
                    stored_upto[s] = (dst_stored[0], dst_stored[1])

            def product(a0, a1):
                for a in range(a0, a1):
                    for part in range(2):
                        fin = a == NT - 1 and part == 1
                        tok = put("pe", lambda e, a=a, part=part: e.matmul(
                            ps[0:SROWS, 4 + s % 2, 0:D], counts[:, a, :], feat[:, a, part * D:(part + 1) * D],
                            start=a == 0 and part == 0, stop=a == NT - 1 and part == 1),
                            tuple(p1_out[s % 2]) + (strip_ready, feat_ready[a]), s_p1 if fin else None)
                if a1 == NT:
                    src_read[slot] = state["summed"] = tok

            def source_degrees(a0, a1):
                for a in range(a0, a1):
                    dst_read[slot] = put("pe", lambda e, a=a: e.matmul(
                        ps[:, 6, a:a + 1], strips[:, 2 + slot, a * P:(a + 1) * P], ones_h[:, :], start=s == 0 and a == 0,
                        stop=s == NS - 1 and a == NT - 1, skip_group_check=True), (state["turned"], zero_pad), s_deg if a == NT - 1 else None)

            def part(k, of=len(QUADS)):
                if k == 0:
                    src_stored[slot] = dma("sp", lambda e: e.dma_start(srcside_dram[s], strips[:, slot, 0:NT * SROWS]), (strip_ready,), s_st[0][slot])
                if k < len(TGROUPS):
                    turn(k)
                product(NT * k // of, NT * (k + 1) // of)
                if k > len(TGROUPS):
                    n = of - len(TGROUPS) - 1
                    i = k - len(TGROUPS) - 1
                    source_degrees(NT * i // n, NT * (i + 1) // n)

            def split():
                deg_read[slot] = r1 = V(lambda e: e.tensor_reduce(binv[0:SROWS, s:s + 1], degj[0:SROWS, slot, :], AX.X, ALU.add), state["turned"])
                r2 = V(lambda e: e.tensor_scalar(binv[0:SROWS, s:s + 1], binv[0:SROWS, s:s + 1], 1.0, None, ALU.max), r1)
                r3 = V(lambda e: e.reciprocal(binv[0:SROWS, s:s + 1], binv[0:SROWS, s:s + 1]), r2)
                p1_out[s % 2] = split_ef(4 + s % 2, s, state["summed"], (r3, zero_pad))

            return part, split

        s_deg = sig("source_degrees_summed")
        deg_read = [None, None]
        stored_upto = [None] * NS
        zero_pad = (dve.sem, dve.value)
        part = split = split_before = None
        for s in range(NS):
            slot = s % 2
            strip_view = strips[:, slot, 0:NT * SROWS].rearrange("p (a j) -> p j a", j=SROWS)
            if s == 2:
                bank_free[7] = (s_quad_out.sem, s_quad_out.value)
                weights_ready = prepare_graph_weights()
            for qi, (q0, qn) in enumerate(QUADS):
                g0 = s * STRIP_GROUPS + q0
                ring = n_quad % OH_RING
                b = n_quad % 3
                bank = QUAD_BANKS[b]
                put("dve", lambda e, g0=g0, qn=qn, ring=ring: e.tensor_tensor(
                    ohA[:, ring, 0:qn, 0:GC, :], codeT[:, g0:g0 + qn, :].rearrange("p g (o r) -> p g o r", o=1).broadcast_to([P, qn, GC, 2]),
                    iota_h[:, 0:GC, :].rearrange("p (o c) r -> p o c r", o=1).broadcast_to([P, qn, GC, 2]), ALU.is_equal),
                    (used[n_quad - OH_RING] if n_quad >= OH_RING else None, turned, c_ih), None)
                made = put("dve", lambda e, g0=g0, qn=qn, ring=ring: e.tensor_tensor(
                    ohQ[:, ring, 0:qn, :, :], placeT[:, g0:g0 + qn, :].rearrange("p g (o r) -> p g o r", o=1).broadcast_to([P, qn, P, 2]),
                    iota_h[:, :, :].rearrange("p (o c) r -> p o c r", o=1).broadcast_to([P, qn, P, 2]), ALU.is_equal), (), s_oh)
                n_quad += 1
                for k in range(qn):
                    for r in range(2):
                        tok = put("pe", lambda e, k=k, ring=ring, r=r, bank=bank: e.matmul(
                            ps[:, bank, k * GC:(k + 1) * GC], ohQ[:, ring, k, :, r], ohA[:, ring, k, 0:GC, r], start=r == 0, stop=r == 1),
                            (made, quad_out[b], turned, bank_free[7]), s_used if k == qn - 1 and r == 1 else None)
                used.append(tok)
                quad_out[b] = put("act", lambda e, v=strip_view, q0=q0, qn=qn, bank=bank: e.activation(
                    v[:, q0 * GROUP:(q0 + qn) * GROUP, :], ps[:, bank, 0:qn * GC].rearrange("p (j a) -> p j a", a=NT), ACT.Copy),
                    (tok, src_stored[slot], src_read[slot]), s_quad_out)
                if s == 0:
                    for a in range(NT * qi // len(QUADS), NT * (qi + 1) // len(QUADS)):
                        normalise(a)
                if part:
                    part(qi)
                if qi == OH_RING and split_before:
                    split_before()
            split_before = split
            part, split = work_on(s, quad_out[b])
        for k in range(len(QUADS)):
            part(k)
            if k == 0:
                split_before()
        split()
        dv1 = V(lambda e: e.tensor_scalar(dinv[:, :], ps[:, 6, 0:NT], 1.0, None, ALU.max), dst_read[(NS - 1) % 2])
        dinv_ready = V(lambda e: e.reciprocal(dinv[:, :], dinv[:, :]), dv1)

        s_blk = [sig(f"block_loaded_{b}") for b in range(3)]
        s_p2, s_p2_out, s_wp = sig("p2_summed"), sig("p2_copied"), sig("weight_product")
        s_sr = [sig(f"strip_loaded_{b}") for b in range(4)]
        onehots_used = (s_used.sem, s_used.value)
        blk_read = [onehots_used] * 3
        p2_out = [(s_quad_out.sem, s_quad_out.value), (s_turn_out.sem, s_turn_out.value)]
        stT_free = [turned, turned]
        wp_out = [p1_out[0][1], p1_out[1][1]]
        n_blk = n_half = n_tile = 0
        later = []

        def point():
            for item in later:
                item[0] -= 1
            if later and later[0][0] < 0:
                later.pop(0)[1]()

        def p2_layer(wT, ef_ready, post, finish_block, behind_post):
            nonlocal n_blk, n_half, n_tile

            def weight(bi, buf, copied):
                nonlocal n_tile
                b0, bn = BLOCKS[bi]
                for k in range(bn):
                    bank = 4 + n_tile % 2
                    for fb in range(FB):
                        tok = put("pe", lambda e, fb=fb, k=k, bank=bank, buf=buf: e.matmul(
                            ps[:, bank, 0:D], stT[:, buf, fb, k * P:(k + 1) * P], wT[:, fb, :], start=fb == 0, stop=fb == FB - 1),
                            (copied, wp_out[n_tile % 2], weights_ready), s_wp if fb == FB - 1 else None)
                    wp_out[n_tile % 2] = post(b0 + k, bank, tok)
                    n_tile += 1
                stT_free[buf] = tok
                if finish_block:
                    finish_block(bi)

            for bi, (b0, bn) in enumerate(BLOCKS):
                buf = n_blk % 2
                n_blk += 1
                w = bn * P
                for s0, s1 in HALVES:
                    half = n_half % 3
                    n_half += 1
                    loaded = dma("sp", lambda e, b0=b0, w=w, half=half, s0=s0, s1=s1: e.dma_start(
                        blocks[:, half, 0:s1 - s0, 0:w], dstside_dram.rearrange("s p n -> p s n")[:, s0:s1, b0 * P:b0 * P + w]),
                        tuple(stored_upto[s1 - 1]) + (blk_read[half],), s_blk[half])
                    for s in range(s0, s1):
                        for fb in range(FB):
                            for part in range(2):
                                fin = s == s1 - 1 and fb == FB - 1 and part == 1
                                tok = put("pe", lambda e, s=s, fb=fb, part=part, buf=buf, w=w, half=half, s0=s0: e.matmul(
                                    ps[:, 2 * buf + fb, 0:w], ef[:, s, part * D + fb * P:part * D + (fb + 1) * P], blocks[:, half, s - s0, 0:w],
                                    start=s == 0 and part == 0, stop=s == NS - 1 and part == 1),
                                    (loaded, ef_ready, p2_out[buf], zero_pad), s_p2 if fin else None)
                        if s == NS - 1:
                            for fb in range(FB):
                                p2_out[buf] = put("act", lambda e, fb=fb, buf=buf, w=w: e.activation(stT[:, buf, fb, 0:w], ps[:, 2 * buf + fb, 0:w], ACT.Copy),
                                                  (tok, stT_free[buf]), s_p2_out)
                            later.append([1, lambda bi=bi, buf=buf, c=p2_out[buf]: weight(bi, buf, c)])
                            later.extend([n, lambda bi=bi, fn=fn: fn(bi)] for n, fn in behind_post)
                            later.sort(key=lambda item: item[0])
                        if s % 5 == 4:
                            point()
                    blk_read[half] = tok
            while later:
                later.pop(0)[1]()
            return (s_p2.sem, s_p2.value)

        def prelu_into(dst_ap, u, tok):
            m = V(lambda e: e.tensor_scalar(work[:, 3, :], u, 0.0, alpha[:, 0:1], ALU.min, ALU.mult), tok)
            return V(lambda e: e.scalar_tensor_tensor(out=dst_ap, in0=u, scalar=0.0, in1=work[:, 3, :], op0=ALU.max, op1=ALU.add), m)

        feat2_ready = [None] * NT

        def post1(a, bank, summed):
            u = V(lambda e: e.scalar_tensor_tensor(out=work[:, 0, :], in0=ps[:, bank, 0:D], scalar=dinv[:, a:a + 1], in1=gb1row[:, :], op0=ALU.mult, op1=ALU.add), summed, dinv_ready)
            v = prelu_into(work[:, 1, :], work[:, 0, :], u)
            hi = V(lambda e: e.tensor_copy(feat[:, a, 0:D], work[:, 1, :]), v)
            feat2_ready[a] = V(lambda e: e.tensor_tensor(feat[:, a, D:2 * D], work[:, 1, :], feat[:, a, 0:D], ALU.subtract), hi)
            return u

        ef_ready = p1_out[(NS - 1) % 2][1]
        last_p2 = p2_layer(gw1T, ef_ready, post1, None, [])

        s_stage = [sig(f"stage_loaded_{b}") for b in range(2)]
        s_stage_used, s_wpart = sig("stage_used"), sig("expert_parts")
        stage_free = [None, None]
        n_stage = 0

        def stage_piece(i):
            nonlocal n_stage
            k = n_stage % 2
            n_stage += 1
            piece = (W2 if i % 2 else W1)[i // 2].rearrange("(b p) n -> p b n", p=P)
            tok = dma("sp", lambda e: e.dma_start(stage[:, k, :].rearrange("p (b n) -> p b n", b=piece.shape[1]), piece), (stage_free[k],), s_stage[k])
            return k, tok

        def norm_piece(i):
            k, tok = stage_piece(i)
            stage_free[k] = put("act", lambda e: e.activation(stage[:, k, :], stage[:, k, :], ACT.Square, accum_out=sumsq[:, i:i + 1]), (tok,), s_stage_used)

        def split_piece(i, room):
            k, tok = stage_piece(i)
            n = 2 * H
            at = i * 2 * n
            sc = sW2 if i % 2 else sW1
            scaled = put("act", lambda e: e.activation(stage[:, k, :], stage[:, k, :], ACT.Copy, scale=sc[:, 0:1]), (tok, scales_ready), s_stage_used)
            hi = put("act", lambda e: e.activation(region[:, at:at + n], stage[:, k, :], ACT.Copy), (scaled, room), s_stage_used)
            stage_free[k] = put("pool", lambda e: e.tensor_tensor(region[:, at + n:at + 2 * n], stage[:, k, :], region[:, at:at + n], ALU.subtract), (hi,), s_wpart)

        def make_scales(bank_ok):
            nb = NE * H // P
            b1_in = dma("act", lambda e: e.dma_start(hbuf[:, 0, 0:nb], b1.rearrange("n h -> (n h)").rearrange("(p m) -> p m", p=P)), (feat_ready1,), sig("b1_loaded"))
            n1 = A(lambda e: e.activation(hbuf[:, 1, 0:nb], hbuf[:, 0, 0:nb], ACT.Square, accum_out=sumsq[:, 2 * NE:2 * NE + 1]), b1_in)
            V(lambda e: e.tensor_reduce(ssum[:, 0:2], sumsq[:, 0:2 * NE].rearrange("p (n k) -> p k n", k=2), AX.X, ALU.add), (s_stage_used.sem, s_stage_used.value))
            v = V(lambda e: e.tensor_copy(ssum[:, 2:3], sumsq[:, 2 * NE:2 * NE + 1]), n1)
            t = put("pe", lambda e: e.matmul(ps[:, 6, 0:3], ones_f[:, :], ssum[:, :], start=True, stop=True), (v, bank_ok), pe)
            a = A(lambda e: e.activation(ssum[:, :], ps[:, 6, 0:3], ACT.Sqrt), t)
            a = V(lambda e: e.tensor_scalar(ssum[:, :], ssum[:, :], 1e-15, None, ALU.max), a)
            v = V(lambda e: e.scalar_tensor_tensor(out=ssum[:, 2:3], in0=ssum[:, 0:1], scalar=16.0, in1=ssum[:, 2:3], op0=ALU.mult, op1=ALU.add), a)
            v = V(lambda e: e.tensor_scalar(ssum[:, 0:2], ssum[:, 0:2], 2.0 / HALF_TOP, None, ALU.mult), v)
            v = V(lambda e: e.tensor_scalar(ssum[:, 2:3], ssum[:, 2:3], 1.0 / HALF_TOP, None, ALU.mult), v)
            V(lambda e: e.reciprocal(sW1[:, :], ssum[:, 0:1]), v)
            V(lambda e: e.reciprocal(sW2[:, :], ssum[:, 1:2]))
            V(lambda e: e.reciprocal(sH[:, :], ssum[:, 2:3]))
            V(lambda e: e.tensor_scalar(iW1[:, :], ssum[:, 0:1], 1.0 / FEATURE_SCALE, None, ALU.mult))
            return V(lambda e: e.tensor_tensor(iW2[:, :], ssum[:, 1:2], ssum[:, 2:3], ALU.mult))

        feat_ready1 = feat_ready[NT - 1]
        feat_ready = feat2_ready
        ring_read = [None] * 4
        all_stored = (src_stored[0], src_stored[1], dst_stored[0], dst_stored[1], dst_read[0], dst_read[1])
        for s in range(NS):
            slot_s = s % 4
            loaded = dma("sp", lambda e, s=s, slot_s=slot_s: e.dma_start(strips[:, slot_s, 0:NT * SROWS], srcside_dram[s]),
                         all_stored + (ring_read[slot_s],), s_sr[slot_s])
            counts = strips[:, slot_s, 0:NT * SROWS].rearrange("p (a j) -> p a j", j=SROWS)
            bank = 6 + s % 2
            free = p1_out[s % 2] if s >= 2 else (dv1, (s_quad_out.sem, s_quad_out.value))
            if s < 2 * NE:
                norm_piece(s)
            tok = p1(bank, counts, SROWS, loaded, free, s_p1)
            ring_read[slot_s] = tok
            p1_out[s % 2] = split_ef(bank, s, tok, (last_p2,))
        region_free = tok
        ef_ready = p1_out[(NS - 1) % 2][1]
        scales_ready = make_scales(ef_ready)
        strips_in = tuple((x.sem, x.value) for x in s_sr)

        s_yt, s_yt_out, s_y = sig("y_turned"), sig("y_copied"), sig("y_rows")
        s_send = [sig(f"rows_sent_{b}") for b in range(8)]
        sent = {}
        turn_free = [scales_ready, p1_out[1][1]]
        y_ready, logit_done, yrow_ready, b2_added = [None] * NT, [None] * NT, [None] * NT, [None] * NT
        ycol_free = [None, None]
        ybuf_free = [scales_ready] * 4
        n_piece = 0
        cwT_free = None
        b2_in = dma("act", lambda e: e.dma_start(b2sb, b2), (onehots_used,), sig("b2_loaded"))

        summed2 = {}

        def post2(a, bank, summed):
            summed2[a] = V(lambda e: e.scalar_tensor_tensor(out=work[:, a % 4, :], in0=ps[:, bank, 0:D], scalar=dinv[:, a:a + 1], in1=gb2row[:, :], op0=ALU.mult, op1=ALU.add),
                           summed, dinv_ready, x_added.get(a - 4))
            return summed2[a]

        x_added = {}

        def finish2(bi):
            b0, bn = BLOCKS[bi]
            tiles = range(b0, b0 + bn)
            t = {}
            for a in tiles:
                t[a] = A(lambda e, a=a: e.activation(ybuf[:, a % 4, :], xt[:, a, :], ACT.Identity, bias=nmr[:, a:a + 1], scale=rstd[:, a:a + 1]),
                         ybuf_free[a % 4], yrow_ready[a - 4] if a >= 4 else None)
            for a in tiles:
                t[a] = V(lambda e, a=a: e.tensor_tensor(work[:, a % 4, :], work[:, a % 4, :], ybuf[:, a % 4, :], ALU.add), t[a], summed2[a])
            for a in tiles:
                t[a] = V(lambda e, a=a: e.tensor_scalar(ybuf[:, a % 4, :], work[:, a % 4, :], 0.0, alpha[:, 0:1], ALU.min, ALU.mult), t[a])
            for a in tiles:
                t[a] = V(lambda e, a=a: e.scalar_tensor_tensor(out=work[:, a % 4, :], in0=work[:, a % 4, :], scalar=0.0, in1=ybuf[:, a % 4, :], op0=ALU.max, op1=ALU.add), t[a])
                x_added[a] = t[a] = G(lambda e, a=a: e.tensor_tensor(xt[:, a, :], xt[:, a, :], work[:, a % 4, :], ALU.add), t[a])
            for a in tiles:
                t[a] = V(lambda e, a=a: e.bn_stats(bn6[:, a, :], xt[:, a, :]), t[a])
            for a in tiles:
                ag = V(lambda e, a=a: e.bn_aggr(mv[:, a, :], bn6[:, a, :]), t[a])
            sq = A(lambda e: e.activation(rstd[:, b0:b0 + bn], mv[:, b0:b0 + bn, 1], ACT.Sqrt, bias=epsc[:, 0:1]), ag)
            rc = V(lambda e: e.reciprocal(rstd[:, b0:b0 + bn], rstd[:, b0:b0 + bn]), sq)
            rc = V(lambda e: e.tensor_scalar(rstd[:, b0:b0 + bn], rstd[:, b0:b0 + bn], FEATURE_SCALE, None, ALU.mult), rc)
            for a in tiles:
                k, r = a % 4, a % 8
                y = y_ready[a] = V(lambda e, a=a, k=k: e.tensor_scalar(ybuf[:, k, :], xt[:, a, :], mv[:, a, 0:1], rstd[:, a:a + 1], ALU.subtract, ALU.mult), rc)
                hi = put("act", lambda e, r=r, k=k: e.activation(yrow[:, r, 0:D], ybuf[:, k, :], ACT.Copy), (y, turned, sent.get(a - 8)), s_y)
                yrow_ready[a] = G(lambda e, r=r, k=k: e.tensor_tensor(yrow[:, r, D:2 * D], ybuf[:, k, :], yrow[:, r, 0:D], ALU.subtract), hi)

        def logits(bi):
            nonlocal n_piece
            b0, bn = BLOCKS[bi]
            copied = {}

            def product(a):
                k = a % 2
                for fb in range(FB):
                    tok = put("pe", lambda e, fb=fb: e.matmul(ps[:, 6 + k, D:D + NE], ycol[:, k, fb * P:(fb + 1) * P], gatew[:, fb, :], start=fb == 0, stop=fb == FB - 1),
                              (copied[a], c_gate), s_yt if fb == FB - 1 else None)
                ycol_free[k] = tok
                turn_free[k] = logit_done[a] = V(lambda e: e.tensor_copy(logit_acc[:, a - b0, :], ps[:, 6 + k, D:D + NE]), tok)

            for a in range(b0, b0 + bn):
                k = a % 2
                if a - 2 >= b0:
                    product(a - 2)
                for fb in range(FB):
                    tok = put("pe", lambda e, fb=fb, a=a, k=k: e.transpose(ps[:, 6 + k, fb * P:(fb + 1) * P], ybuf[:, a % 4, fb * P:(fb + 1) * P], ident_f[:, :]),
                              (y_ready[a], turn_free[k]), s_yt if fb == FB - 1 else None)
                ybuf_free[a % 4] = tok
                copied[a] = put("act", lambda e, k=k: e.activation(ycol[:, k, :], ps[:, 6 + k, 0:D], ACT.Copy), (tok, ycol_free[k]), s_yt_out)
            for a in range(max(b0, b0 + bn - 2), b0 + bn):
                product(a)
            for _ in range(3):
                if n_piece < 2 * NE:
                    split_piece(n_piece, region_free)
                    n_piece += 1

        def gate(bi):
            nonlocal cwT_free
            b0, bn = BLOCKS[bi]
            gb = bi % 2
            bank = 6 + gb
            shp3, shp4 = [P, bn, NE], [P, bn, NE, NE]
            p3, c3, r3, l3 = pr[:, 0:bn, :], cw[:, 0:bn, :], rank[:, 0:bn, :], place[:, 0:bn, :]
            ca, cb = cmp_a[:, 0:bn], cmp_b[:, 0:bn]
            per_node = rd[:, 0:bn].rearrange("p (a o) -> p a o", o=1).broadcast_to(shp3)
            low = lower[:, :, :].rearrange("p (o k) n -> p o k n", o=1).broadcast_to(shp4)
            v = V(lambda e: e.tensor_tensor(p3, logit_acc[:, 0:bn, :], gatebr[:, :].rearrange("p (o k) -> p o k", o=1).broadcast_to(shp3), ALU.add), logit_done[b0 + bn - 1])
            v = V(lambda e: e.tensor_reduce(rd[:, 0:bn], p3, AX.X, ALU.max), v)
            v = V(lambda e: e.tensor_tensor(p3, p3, per_node, ALU.subtract), v)
            v = A(lambda e: e.activation(p3, p3, ACT.Exp), v)
            v = V(lambda e: e.tensor_reduce(rd[:, 0:bn], p3, AX.X, ALU.add), v)
            v = V(lambda e: e.reciprocal(rd[:, 0:bn], rd[:, 0:bn]), v)
            v = V(lambda e: e.tensor_tensor(p3, p3, per_node, ALU.mult), v)
            mine = p3.rearrange("p a (k o) -> p a k o", o=1).broadcast_to(shp4)
            other = p3.rearrange("p a (o k) -> p a o k", o=1).broadcast_to(shp4)
            v = V(lambda e: e.tensor_tensor(ca, other, mine, ALU.is_equal), v)
            v = V(lambda e: e.tensor_tensor(ca, ca, low, ALU.mult), v)
            v = V(lambda e: e.tensor_tensor(cb, other, mine, ALU.is_gt))
            v = V(lambda e: e.tensor_tensor(ca, ca, cb, ALU.add), v)
            v = V(lambda e: e.tensor_reduce(r3, ca, AX.X, ALU.add), v)
            v = V(lambda e: e.tensor_scalar(r3, r3, float(TOP), None, ALU.is_lt), v)
            if b0 + bn == NT:
                v = V(lambda e: e.tensor_scalar(rank[:, bn - 1, :], rank[:, bn - 1, :], valid[:, 0:1], None, ALU.mult), v)
            picked = V(lambda e: e.tensor_copy(pick_h[:, 0:bn, :], r3), v)
            cw_ok = V(lambda e: e.tensor_tensor(c3, p3, r3, ALU.mult), cwT_free)
            n = bn * NE
            ph = pick_h[:, 0:bn, :].rearrange("p a k -> p (a k)")
            put("pe", lambda e: e.matmul(ps[:, bank, 256:256 + n], tri_h[:, :], ph, start=True, stop=True), (picked, turn_free[0], turn_free[1]), None)
            t = put("pe", lambda e: e.matmul(ps[:, bank, 320:320 + n], ones_sq[:, :], ph, start=True, stop=True), (), s_yt)
            v = V(lambda e: e.tensor_tensor(ca, r3.rearrange("p a (o k) -> p a o k", o=1).broadcast_to(shp4), low, ALU.mult))
            v = V(lambda e: e.tensor_reduce(l3, ca, AX.X, ALU.add), v)
            v = V(lambda e: e.tensor_tensor(pick[:, b0:b0 + bn, 1, :], l3, r3, ALU.mult), v)
            v = V(lambda e: e.tensor_tensor(pick[:, b0:b0 + bn, 0, :], r3, pick[:, b0:b0 + bn, 1, :], ALU.subtract), v)
            for k in range(bn):
                v = V(lambda e, k=k: e.tensor_tensor(runs[:, b0 + k + 1, :], ps[:, bank, 320 + k * NE:320 + (k + 1) * NE], runs[:, b0 + k, :], ALU.add), t, v)
            v = V(lambda e: e.tensor_tensor(l3, ps[:, bank, 256:256 + n].rearrange("p (a k) -> p a k", k=NE), runs[:, b0:b0 + bn, :], ALU.add), v)
            turn_free[gb] = v
            v = V(lambda e: e.tensor_tensor(l3, l3, e_row[:, :].rearrange("p (o k) -> p o k", o=1).broadcast_to(shp3), ALU.add), v)
            for c in range(TOP):
                for values, to in ((l3, node_row), (c3, wgt)):
                    v = V(lambda e, c=c, values=values: e.tensor_tensor(cb[:, :, 0, :], pick[:, b0:b0 + bn, c, :], values, ALU.mult), v)
                    v = V(lambda e, c=c, to=to: e.tensor_reduce(to[:, b0:b0 + bn, c], cb[:, :, 0, :], AX.X, ALU.add), v)
            v = V(lambda e: e.tensor_copy(node_row_u[:, b0:b0 + bn, :], node_row[:, b0:b0 + bn, :]), v)
            for a in range(b0, b0 + bn):
                rows = P if a < NT - 1 else TAIL
                for c in range(TOP):
                    sent[a] = dma("pool", lambda e, a=a, c=c, rows=rows: e.indirect_dma_start(
                        out=sent_dram, out_offset=bass.IndirectOffsetOnAxis(ap=node_row_u[0:rows, a, c:c + 1], axis=0),
                        in_=yrow[0:rows, a % 8, :], in_offset=None),
                        (v, yrow_ready[a], zero_rows) + strips_in, s_send[a % 8])
            for k in range(bn):
                a = b0 + k
                t = put("pe", lambda e, k=k: e.transpose(ps[0:NE, bank, 0:P], cw[:, k, :], ident_f[:, :]), (cw_ok, turn_free[gb]), s_yt)
                c = V(lambda e: e.tensor_copy(cwT, ps[0:NE, bank, 0:P]), t, turned)
                t = put("pe", lambda e: e.matmul(ps[:, bank, P:P + D], cwT, b2sb, start=True, stop=True), (c, b2_in), s_yt)
                turn_free[gb] = cwT_free = b2_added[a] = V(lambda e, a=a: e.tensor_tensor(xt[:, a, :], xt[:, a, :], ps[:, bank, P:P + D], ALU.add), t)

        p2_layer(gw2T, ef_ready, post2, finish2, [(4, logits), (5, gate)])
        while n_piece < 2 * NE:
            split_piece(n_piece, region_free)
            n_piece += 1
        weights_in = (s_wpart.sem, s_wpart.value)
        p2_done = (s_p2.sem, s_p2.value)
        gated = (dve.sem, dve.value)
        all_sent = tuple((x.sem, x.value) for x in s_send)

        b1_rows_in = dma("sp", lambda e: e.dma_start(b1rows, b1.rearrange("n h -> (n h)").partition_broadcast(P)), (p2_done,), sig("b1_rows_loaded"))

        def along(ap, n):
            return ap.rearrange("p (o k) -> p o k", o=1).broadcast_to([P, n, NE])

        v = V(lambda e: e.tensor_scalar(tiles_f[:, :], runs[:, NT, :], float(P - 1), None, ALU.add), gated)
        v = V(lambda e: e.tensor_copy(tiles_i[:, :], tiles_f[:, :]), v)
        v = V(lambda e: e.tensor_scalar(tiles_i[:, :], tiles_i[:, :], 7, None, ALU.logical_shift_right), v)
        v = V(lambda e: e.tensor_copy(tiles_f[:, :], tiles_i[:, :]), v)
        v = V(lambda e: e.tensor_tensor(cmp_a[:, 0], lower[:, :, :], along(tiles_f[:, :], NE), ALU.mult), v)
        v = V(lambda e: e.tensor_reduce(base_f[:, :], cmp_a[:, 0], AX.X, ALU.add), v)
        v = V(lambda e: e.tensor_tensor(ends_f[:, :], base_f[:, :], tiles_f[:, :], ALU.add), v)
        over = tile_cmp[:, 0]
        v = V(lambda e: e.tensor_tensor(over, tcol[:, :].rearrange("p (t o) -> p t o", o=1).broadcast_to([P, ETILES, NE]), along(ends_f[:, :], ETILES), ALU.is_ge), v, p2_done)
        v0 = V(lambda e: e.tensor_reduce(tile_e[:, :], over, AX.X, ALU.add), v)
        v = V(lambda e: e.tensor_tensor(tile_cmp[:, 1], over, along(tiles_f[:, :], ETILES), ALU.mult))
        v = V(lambda e: e.tensor_reduce(tile_b[:, :], tile_cmp[:, 1], AX.X, ALU.add), v)
        v1 = V(lambda e: e.tensor_scalar(tile_e[:, :], tile_e[:, :], float(NE - 1), None, ALU.min), v0)
        v2 = V(lambda e: e.tensor_scalar(off_w[:, :], tile_e[:, :], float(EW), None, ALU.mult), v1)
        offs = V(lambda e: e.tensor_scalar(off_b[:, :], tile_e[:, :], float(H), None, ALU.mult))
        v = V(lambda e: e.tensor_tensor(tile_b[:, :], tcol[:, :], tile_b[:, :], ALU.subtract), v)
        v = V(lambda e: e.tensor_scalar(tile_b[:, :], tile_b[:, :], float(P), None, ALU.mult), v)
        v = V(lambda e: e.scalar_tensor_tensor(out=tile_b[:, :], in0=tile_e[:, :], scalar=float(CAP), in1=tile_b[:, :], op0=ALU.mult, op1=ALU.add), v)
        v = V(lambda e: e.tensor_scalar(tile_b[:, :], tile_b[:, :], float(NE * CAP - P), part_f[:, 0:1], ALU.min, ALU.add), v)
        rows_ok = V(lambda e: e.tensor_copy(row_u[:, :], tile_b[:, :]), v)
        v = V(lambda e: e.scalar_tensor_tensor(out=ends_f[:, :], in0=base_f[:, :], scalar=float(P), in1=e_row[:, :], op0=ALU.mult, op1=ALU.subtract))
        pick_flat = pick[:, :, :, :].rearrange("p a c k -> p (a c) k")
        v = V(lambda e: e.tensor_tensor(pick_flat, pick_flat, along(ends_f[:, :], NT * TOP), ALU.mult), v)
        v = V(lambda e: e.tensor_reduce(wide, pick_flat, AX.X, ALU.add), v)
        v = V(lambda e: e.tensor_tensor(node_row[:, :, :], node_row[:, :, :], wide.rearrange("p (a c) -> p a c", c=TOP), ALU.add), v)
        back_ok = V(lambda e: e.tensor_copy(node_row_u[:, :, :], node_row[:, :, :]), v, *all_sent)

        s_xg = [sig(f"rows_in_{b}") for b in range(4)]
        s_xt, s_xt_out, s_g1, s_pre, s_gelu, s_ht, s_hhi, s_hlo, s_g2, s_yo = [sig(n) for n in (
            "rows_turned", "rows_turned_copied", "hidden_summed", "hidden_biased", "hidden_gelu", "hidden_turned",
            "hidden_high", "hidden_rest", "expert_summed", "expert_copied")]
        s_ys = [sig(f"expert_stored_{b}") for b in range(4)]
        rows_in, rows_turned, xcol_ok, g1_ok, pre_ok, gelu_ok, hid_turned, parts_ok, g2_ok, yo_ok, stored = [{} for _ in range(11)]
        offset = {}

        def load_offset(engine, table, top, t):
            def fn(e):
                offset[engine, t] = e.value_load(table[0:1, t:t + 1], min_val=0, max_val=top)
            put(engine, fn, (offs, v2), None)

        def fetch(t):
            rows_in[t] = dma("pool", lambda e: e.indirect_dma_start(
                out=xg[:, t % 4, :], out_offset=None, in_=sent_dram, in_offset=bass.IndirectOffsetOnAxis(ap=row_u[:, t:t + 1], axis=0)),
                (rows_ok, rows_turned.get(t - 4), p2_done) + all_sent, s_xg[t % 4])

        def turn_rows(t):
            bank = bank_h(6)[:, (t % 2) * 2 * D:(t % 2 + 1) * 2 * D]
            for k in range(2 * FB):
                rows_turned[t] = put("pe", lambda e, k=k: e.transpose(bank[:, k * P:(k + 1) * P], xg[:, t % 4, k * P:(k + 1) * P], ident_h[:, :]),
                                     (rows_in[t], xcol_ok.get(t - 2), gated), s_xt if k == 2 * FB - 1 else None)
            xcol_ok[t] = put("dve", lambda e: e.tensor_copy(xcol[:, t % 2, :], bank), (rows_turned[t], g1_ok.get(t - 2)), s_xt_out)

        def hidden(t):
            load_offset("pe", off_w, (NE - 1) * EW, t)
            b = t % 2
            terms = [(xp, wp, fb) for xp, wp in ((0, 0), (0, 1), (1, 0)) for fb in range(FB)]
            for i, (xp, wp, fb) in enumerate(terms):
                last = i == len(terms) - 1
                g1_ok[t] = put("pe", lambda e, xp=xp, wp=wp, fb=fb, i=i, last=last: e.matmul(
                    ps[:, b, :], xcol[:, b, (xp * FB + fb) * P:(xp * FB + fb + 1) * P],
                    region[:, bass.ds(offset["pe", t] + (wp * FB + fb) * H, H)], start=i == 0, stop=last),
                    (xcol_ok[t], pre_ok.get(t - 2), weights_in, p2_out[0]), s_g1 if last else None)
            load_offset("dve", off_b, (NE - 1) * H, t)
            pre_ok[t] = put("dve", lambda e: e.scalar_tensor_tensor(out=hid[:, b, :], in0=ps[:, b, :], scalar=iW1[:, 0:1],
                                                                    in1=b1rows[:, bass.ds(offset["dve", t], H)], op0=ALU.mult, op1=ALU.add),
                            (g1_ok[t], b1_rows_in, hid_turned.get(t - 2)), s_pre)
            gelu_ok[t] = put("act", lambda e: e.activation(hid[:, b, :], hid[:, b, :], ACT.Gelu), (pre_ok[t],), s_gelu)

        def turn_hidden(t):
            b = t % 2
            for hb in range(HB):
                hid_turned[t] = put("pe", lambda e, hb=hb: e.transpose(ps[:, 2 + b, hb * P:(hb + 1) * P], hid[:, b, hb * P:(hb + 1) * P], ident_f[:, :]),
                                    (gelu_ok[t], parts_ok.get(t - 2), p2_out[1]), s_ht if hb == HB - 1 else None)
            hi = put("act", lambda e: e.activation(hcol[:, b, 0, :], ps[:, 2 + b, :], ACT.Copy, scale=sH[:, 0:1]), (hid_turned[t], g2_ok.get(t - 2)), s_hhi)
            parts_ok[t] = put("dve", lambda e: e.scalar_tensor_tensor(out=hcol[:, b, 1, :], in0=ps[:, 2 + b, :], scalar=sH[:, 0:1], in1=hcol[:, b, 0, :],
                                                                      op0=ALU.mult, op1=ALU.subtract), (hi,), s_hlo)

        def result(t):
            b = t % 2
            terms = [(hp, wp, hb) for hp, wp in ((0, 0), (0, 1), (1, 0)) for hb in range(HB)]
            for i, (hp, wp, hb) in enumerate(terms):
                last = i == len(terms) - 1
                g2_ok[t] = put("pe", lambda e, hp=hp, wp=wp, hb=hb, i=i, last=last: e.matmul(
                    ps[:, 4 + b, 0:D], hcol[:, b, hp, hb * P:(hb + 1) * P],
                    region[:, bass.ds(offset["pe", t] + 2 * FB * H + (wp * HB + hb) * D, D)], start=i == 0, stop=last),
                    (parts_ok[t], yo_ok.get(t - 2)), s_g2 if last else None)
            yo_ok[t] = put("act", lambda e: e.activation(yo[:, t % 4, :], ps[:, 4 + b, 0:D], ACT.Copy, scale=iW2[:, 0:1]), (g2_ok[t], stored.get(t - 4)), s_yo)
            stored[t] = dma("sp", lambda e: e.dma_start(expert_out_dram[t * P:(t + 1) * P, :], yo[:, t % 4, :]), (yo_ok[t],), s_ys[t % 4])

        for t in range(3):
            fetch(t)
        turn_rows(0)
        for t in range(ETILES + 2):
            if t < ETILES:
                hidden(t)
            if t + 1 < ETILES:
                turn_rows(t + 1)
            if t + 3 < ETILES:
                fetch(t + 3)
            if 1 <= t <= ETILES:
                turn_hidden(t - 1)
            if t >= 2:
                result(t - 2)

        s_back = [sig(f"rows_back_{b}") for b in range(8)]
        all_out = tuple((x.sem, x.value) for x in s_ys)
        back_used = {}
        x_acc = [None] * NT
        n_back = 0
        for a in range(NT):
            rows = P if a < NT - 1 else TAIL
            for c in range(TOP):
                r = n_back % 8
                got = dma("pool", lambda e, a=a, c=c, r=r, rows=rows: e.indirect_dma_start(
                    out=back[0:rows, r, :], out_offset=None, in_=expert_out_dram, in_offset=bass.IndirectOffsetOnAxis(ap=node_row_u[0:rows, a, c:c + 1], axis=0)),
                    all_out + (back_ok, back_used.get(n_back - 8)), s_back[r])
                x_acc[a] = back_used[n_back] = V(lambda e, a=a, c=c, r=r, rows=rows: e.scalar_tensor_tensor(
                    out=xt[0:rows, a, :], in0=back[0:rows, r, :], scalar=wgt[0:rows, a, c:c + 1], in1=xt[0:rows, a, :], op0=ALU.mult, op1=ALU.add),
                    got, x_acc[a] if c else b2_added[a])
                n_back += 1

        s_out = sig("out_stored")
        dma("sp", lambda e: e.dma_start(out[0:(NT - 1) * P, :].rearrange("(a q) f -> q a f", q=P), xt[:, 0:NT - 1, :]), (x_acc[NT - 2], x_acc[NT - 1]), s_out)
        fin = dma("sp", lambda e: e.dma_start(out[(NT - 1) * P:N, :], xt[0:TAIL, NT - 1, :]), (x_acc[NT - 1],), s_out)
        put("sp", lambda e: e.nop(), (fin,), None)

        ctx.enter_context(nc.allow_non_contiguous_dma(reason="bias columns, a few kilobytes"))
        block = ctx.enter_context(nc.Block())

        @block.tensor
        def _(e):
            prog.emit("pe", e)

        @block.scalar
        def _(e):
            prog.emit("act", e)

        @block.vector
        def _(e):
            prog.emit("dve", e)

        @block.gpsimd
        def _(e):
            prog.emit("pool", e)

        @block.sync
        def _(e):
            prog.emit("sp", e)


_INS = ["x", "src", "dst", "L0_gnn_W1", "L0_gnn_b1", "L0_gnn_W2", "L0_gnn_b2", "L0_gnn_prelu_a", "L0_ffn_gate_w",
        "L0_ffn_gate_b", "L0_ffn_W1", "L0_ffn_b1", "L0_ffn_W2", "L0_ffn_b2"]


def kernel(**inputs):
    import numpy as np
    import concourse.bacc as bacc
    from concourse.bass_utils import run_bass_kernel_spmd

    nc = bacc.Bacc("TRN2", target_bir_lowering=False, num_devices=1)
    arrays, args = {}, []
    for name in _INS:
        a = np.ascontiguousarray(inputs[name])
        a = a.reshape(a.shape or (1,))
        arrays[name] = a
        args.append(nc.dram_tensor(name, a.shape, mybir.dt.from_np(a.dtype), kind="ExternalInput").ap())
    out = nc.dram_tensor("out", arrays["x"].shape, F32, kind="ExternalOutput").ap()
    gnn_moe_kernel(nc, *args, out)
    r = run_bass_kernel_spmd(nc, [arrays], core_ids=[0])
    return r.results[0]["out"]
```

```python
from contextlib import ExitStack

import concourse.bass as bass
from concourse import mybir

ALU = mybir.AluOpType
ACT = mybir.ActivationFunctionType
AX = mybir.AxisListType
F32 = mybir.dt.float32
F16 = mybir.dt.float16
I32 = mybir.dt.int32
U32 = mybir.dt.uint32

P = 128
GROUP = 5
STRIP_GROUPS = 25
CHUNK = 32
WINDOW = 256
SRC_BITS = 12
FEATURE_SCALE = 1024.0
HALF_TOP = 16384.0
LN_EPS = 1e-5
TOP = 2


class Signal:

    def __init__(self, sem):
        self.sem, self.value = sem, 0

    def up(self, by=1):
        self.value += by
        return (self.sem, self.value)

    def now(self):
        return (self.sem, self.value)


class Turn:

    def __init__(self, clock):
        self.clock = clock
        self.bodies = {"pe": [], "act": [], "dve": [], "pool": [], "sp": []}

    def step(self, engine, *fns, by=1):
        before = self.clock.value
        self.clock.value += by

        def body(e):
            if before:
                e.wait_ge(self.clock.sem, before)
            for fn in fns:
                ins = fn(e)
            ins.then_inc(self.clock.sem, by)
        self.bodies[engine].append(body)

    def loop(self, count, first, second):
        before = self.clock.value
        self.clock.value += 2 * count
        for place, (engine, fn) in enumerate((first, second)):
            def body(e, place=place, fn=fn):
                with e.Fori(0, count) as i:
                    e.wait_ge(self.clock.sem, i * 2 + (before + place))
                    fn(e, i).then_inc(self.clock.sem, 1)
            self.bodies[engine].append(body)


class Program:

    def __init__(self):
        self.queues = {"pe": [], "act": [], "dve": [], "pool": [], "sp": []}

    def put(self, engine, fn, after=(), done=None):
        token = done.up() if done is not None else None
        self.queues[engine].append((tuple(after), fn, done, 1))
        return token

    def dma(self, engine, fn, after=(), done=None):
        token = done.up(16)
        self.queues[engine].append((tuple(after), fn, done, 16))
        return token

    def emit(self, engine, eng):
        reached = {}
        for after, fn, done, by in self.queues[engine]:
            for wait in after:
                if wait is None:
                    continue
                sem, value = wait
                if reached.get(id(sem), 0) < value:
                    eng.wait_ge(sem, value)
                    reached[id(sem)] = value
            ins = fn(eng)
            if done is not None:
                ins.then_inc(done.sem, by)


def gnn_moe_kernel(nc, x, src, dst, gW1, gb1, gW2, gb2, prelu_a, gate_w, gate_b, W1, b1, W2, b2, out):
    N, D = x.shape
    E = src.shape[0]
    NE, _, H = W1.shape
    NT = -(-N // P)
    TAIL = N - (NT - 1) * P
    NG = N // GROUP
    NS = NG // STRIP_GROUPS
    SROWS = GROUP * STRIP_GROUPS
    GC = GROUP * NT
    NPAD = NT * P
    FB = D // P
    HB = H // P
    CH_ROW = 26
    EROW = CH_ROW * CHUNK
    EPARTS = 125
    NCHUNK = CH_ROW * EPARTS
    EFULL = E // EROW
    EREST = E - EFULL * EROW
    assert N == NG * GROUP and NG == NS * STRIP_GROUPS and SROWS == 125 and EPARTS * EROW > E
    NO_EDGE = float(4095 * 4096)
    QUADS = [(q, min(4, STRIP_GROUPS - q)) for q in range(0, STRIP_GROUPS, 4)]
    TGROUPS = [(0, 7), (7, 6), (13, 6), (19, 6)]
    BLOCKS = [(b, 4) for b in range(0, NT - 5, 4)] + [(NT - 5, 3), (NT - 2, 2)]
    HALVES = [(0, 13), (13, NS)]
    CAP = NPAD
    ETILES = (TOP * N + NE * (P - 1)) // P

    with ExitStack() as ctx:
        def sb(name, shape, dt):
            return ctx.enter_context(nc.sbuf_tensor(name, shape, dt))

        all_signals = []

        def sig(name):
            all_signals.append(Signal(ctx.enter_context(nc.semaphore(name))))
            return all_signals[-1]

        prog = Program()
        put, dma = prog.put, prog.dma

        word_dram = nc.dram_tensor("edge_words", [NCHUNK * CHUNK + WINDOW], F32, kind="Internal").ap()
        win_dram = nc.dram_tensor("windows", [NCHUNK, WINDOW], F32, kind="Internal").ap()
        shared_dram = nc.dram_tensor("counts_src_side_then_rows", [NE * CAP * 2 * D], F16, kind="Internal").ap()
        COUNTS = NS * P * NT * SROWS
        srcside_dram = shared_dram[0:COUNTS].rearrange("(s p n) -> s p n", s=NS, p=P)
        sent_dram = shared_dram.rearrange("(r c) -> r c", c=2 * D)
        expert_out_dram = nc.dram_tensor("expert_rows", [ETILES * P, D], F32, kind="Internal").ap()
        dstside_dram = nc.dram_tensor("counts_dst_side", [NS, SROWS, NPAD], F16, kind="Internal").ap()

        xt = sb("xt", [P, NT, D], F32)
        EW = 2 * FB * H + 2 * HB * D
        region = sb("region", [P, NE * EW], F16)
        feat = region[:, 0:NT * 2 * D].rearrange("p (a c) -> p a c", c=2 * D)
        strips = region[:, NT * 2 * D:NT * 2 * D + 4 * NPAD].rearrange("p (k n) -> p k n", k=4)
        SPARE = NT * 2 * D + 4 * NPAD
        ef = sb("ef", [P, NS, 2 * D], F16)
        blocks = sb("blocks", [P, 3, 13, 512], F16)
        stT = sb("stT", [P, 2, FB, 512], F32)
        edge_cols = sb("edge_cols", [P, 2, 2, NG], F32)
        edge_cols_h = edge_cols[:, :, :, :].rearrange("p a b c -> p (a b c)").bitcast(F16)
        codeT = edge_cols_h[:, 0:2 * NG].rearrange("p (g r) -> p g r", r=2)
        placeT = edge_cols_h[:, 2 * NG:4 * NG].rearrange("p (g r) -> p g r", r=2)
        iota_h = sb("iota_h", [P, P, 2], F16)
        iota_f = sb("iota_f", [P, P], F32)
        part_i = sb("part_i", [P, 1], I32)
        part_f = sb("part_f", [P, 1], F32)
        ident_h = sb("ident_h", [P, P], F16)
        ident_f = sb("ident_f", [P, P], F32)
        ones_h = sb("ones_h", [P, 1], F16)
        g5_i = sb("g5_i", [P, NG // 125], I32)
        g5_f = sb("g5_f", [P, NG // 125], F32)
        start_u = sb("start_u", [P, NG // 125], U32)
        cmax = sb("cmax", [P, CH_ROW], F32)
        work = sb("work", [P, 4, D], F32)
        gb1b = work[:, 2, 0:P]
        bn6 = sb("bn6", [P, NT, 6], F32)
        mv = sb("mv", [P, NT, 2], F32)
        rstd = sb("rstd", [P, NT], F32)
        nmr = sb("nmr", [P, NT], F32)
        rstd_s, nmr_s = sb("rstd_s", [P, NT], F32), sb("nmr_s", [P, NT], F32)
        epsc = sb("epsc", [P, 1], F32)
        degj = sb("degj", [P, 2, 4], F32)
        binv = sb("binv", [P, NS], F32)
        dinv = sb("dinv", [P, NT], F32)
        alpha = sb("alpha", [P, 1], F32)
        amax = sb("amax", [P, 1], F32)
        gw1T = sb("gw1T", [P, FB, D], F32)
        gw2T = sb("gw2T", [P, FB, D], F32)
        gb1c = sb("gb1c", [P, FB], F32)
        gb1s = sb("gb1s", [P, FB], F32)
        gb1row = sb("gb1row", [P, D], F32)
        gb2row = sb("gb2row", [P, D], F32)
        nrm = sb("nrm", [P, FB], F32)
        invs = sb("invs", [P, FB], F32)
        scl = sb("scl", [P, FB], F32)
        gatew = sb("gatew", [P, FB, NE], F32)
        gatebr = sb("gatebr", [P, NE], F32)
        stage = sb("stage", [P, 2, 2 * H], F32)
        ybuf = sb("ybuf", [P, 4, D], F32)
        hbuf = ybuf
        ycol = sb("ycol", [P, 2, D], F32)
        lower = sb("lower", [P, NE, NE], F32)
        e_row = sb("e_row", [P, NE], F32)
        tri_h = sb("tri_h", [P, P], F16)
        ones_sq = sb("ones_sq", [P, P], F16)
        ones_f = sb("ones_f", [P, P], F32)
        valid = sb("valid", [P, 1], F32)
        pr = sb("pr", [P, 4, NE], F32)
        rd = sb("rd", [P, 4], F32)
        rank = sb("rank", [P, 4, NE], F32)
        place = sb("place", [P, 4, NE], F32)
        cw = sb("cw", [P, 4, NE], F32)
        pick = sb("pick", [P, NT, TOP, NE], F32)
        pick_h = sb("pick_h", [P, 4, NE], F16)
        cmps = sb("cmps", [P, 2, 4, NE, NE], F32)
        cmp_a, cmp_b = cmps[:, 0], cmps[:, 1]
        iota_i = cmps[:, 0, 0:2, :, :].rearrange("p a b c -> p (a b c)").bitcast(I32)
        logit_acc = sb("logit_acc", [P, 4, NE], F32)
        runs = sb("runs", [P, NT + 1, NE], F32)
        wgt = sb("wgt", [P, NT, TOP], F32)
        node_row = sb("node_row", [P, NT, TOP], F32)
        node_row_u = sb("node_row_u", [P, NT, TOP], U32)
        sumsq = sb("sumsq", [P, 2 * NE + 1], F32)
        ssum = sb("ssum", [P, 3], F32)
        sW1, sW2, sH, iW1, iW2 = [sb(n, [P, 1], F32) for n in ("sW1", "sW2", "sH", "iW1", "iW2")]
        tiles_i = sb("tiles_i", [P, NE], I32)
        tiles_f = sb("tiles_f", [P, NE], F32)
        base_f = sb("base_f", [P, NE], F32)
        ends_f = sb("ends_f", [P, NE], F32)
        tcol = sb("tcol", [P, ETILES], F32)
        tile_e = sb("tile_e", [P, ETILES], F32)
        tile_b = sb("tile_b", [P, ETILES], F32)
        row_u = sb("row_u", [P, ETILES], U32)
        off_w = sb("off_w", [P, ETILES], I32)
        off_b = sb("off_b", [P, ETILES], I32)
        cols_flat = edge_cols[:, :, :, :].rearrange("p a b c -> p (a b c)")
        yrow = cols_flat[:, 0:8 * D].bitcast(F16).rearrange("p (k c) -> p k c", k=8)

        flat = ef[:, :, :].rearrange("p a b -> p (a b)").bitcast(F32)
        W5 = (NG // 125) * WINDOW
        win = flat[:, 0:W5].rearrange("p (t w) -> p t w", w=WINDOW)
        word_i = flat[:, W5:2 * W5].bitcast(I32)
        place_i = flat[:, 2 * W5:3 * W5].bitcast(I32)
        tile_i = flat[:, 3 * W5:4 * W5].bitcast(I32)
        dest_i = flat[:, 4 * W5:5 * W5].bitcast(I32)
        blk_f = blocks[:, :, :, :].rearrange("p a b c -> p (a b c)").bitcast(F32)
        OH_RING = 4
        OHW = 4 * P * 2 // 2
        ohA, ohQ = [blk_f[:, k * OH_RING * OHW:(k + 1) * OH_RING * OHW].bitcast(F16).rearrange(
            "p (o g c r) -> p o g c r", o=OH_RING, g=4, r=2) for k in range(2)]
        CMP_RING, CMP_ROW = 20, NG + NG % 2
        below = blk_f[:, 0:CMP_RING * CMP_ROW // 2].bitcast(F16).rearrange("p (k g) -> p k g", k=CMP_RING)
        first_word = blk_f[:, 2 * NCHUNK + 3 * EROW + WINDOW:2 * NCHUNK + 3 * EROW + WINDOW + NG]
        first_word_i = flat[:, 0:NG].bitcast(I32)
        src_i = blk_f[:, 2 * NCHUNK:2 * NCHUNK + EROW].bitcast(I32)
        dst_i = blk_f[:, 2 * NCHUNK + EROW:2 * NCHUNK + 2 * EROW].bitcast(I32)
        word_f = blk_f[:, 2 * NCHUNK + 2 * EROW:2 * NCHUNK + 3 * EROW]
        spare_f = region[:, SPARE:].bitcast(F32)
        gw1 = spare_f[:, 0:FB * D].rearrange("p (b d) -> p b d", b=FB)
        gw2 = spare_f[:, FB * D:2 * FB * D].rearrange("p (b d) -> p b d", b=FB)
        ZW = 971
        zeros = region[:, SPARE + 4 * FB * D:SPARE + 4 * FB * D + ZW]
        pad_row = blk_f[0:1, 2 * NCHUNK + 3 * EROW:2 * NCHUNK + 3 * EROW + WINDOW]
        b1rows = flat[:, 0:NE * H]
        hid = flat[:, NE * H:NE * H + 2 * H].rearrange("p (k n) -> p k n", k=2)
        yo = flat[:, NE * H + 2 * H:NE * H + 2 * H + 4 * D].rearrange("p (k n) -> p k n", k=4)
        blk_h = blk_f.bitcast(F16)
        xg = blk_h[:, 0:8 * D].rearrange("p (k n) -> p k n", k=4)
        xcol = blk_h[:, 8 * D:12 * D].rearrange("p (k n) -> p k n", k=2)
        hcol = blk_h[:, 12 * D:12 * D + 4 * H].rearrange("p (k q n) -> p k q n", k=2, q=2)
        back = blk_f[:, 4096:4096 + 8 * D].rearrange("p (k n) -> p k n", k=8)
        tile_cmp = blk_f[:, 6144:6144 + 2 * ETILES * NE].rearrange("p (q t k) -> p q t k", q=2, k=NE)
        wide = blk_f[:, 7168:7168 + NT * TOP]
        b2rows = blk_f[:, 7424:7424 + NE * D]
        code_f = flat[:, 0:W5]
        place_f = stT[:, :, :, :].rearrange("p a b c -> p (a b c)")[:, 0:W5]

        EDGE_COLS = -(-NCHUNK * CHUNK // P)
        TRIO = 3
        assert EDGE_COLS % TRIO == 0 and P * EDGE_COLS <= NCHUNK * CHUNK + WINDOW
        g_words, g_place, g_dst, g_all, g_code = [blk_f[:, k * EDGE_COLS:(k + 1) * EDGE_COLS] for k in range(5)]
        g_words_i, g_int = g_words.bitcast(I32), g_code.bitcast(I32)
        G_AT = 5 * EDGE_COLS
        G_OH = NT * SROWS + 1
        g_ohc = blk_f[:, G_AT:G_AT + TRIO * G_OH // 2 + 1].bitcast(F16)
        G_AT += TRIO * G_OH // 2 + 1
        g_ohp = blk_f[:, G_AT:G_AT + TRIO * P // 2].bitcast(F16).rearrange("p (k n) -> p k n", k=TRIO)
        g_src_side, g_dst_side = strips[:, 0, :], strips[0:SROWS, 1, :]
        g_codes1 = strips[:, 2:4, :].rearrange("p k n -> p (k n)").bitcast(F32)[:, 0:NT * SROWS]
        covered = ssum[:, 0:2]
        uncovered = sb("uncovered", [P, 1], I32)

        ps = ctx.enter_context(nc.psum_tensor("ps", [P, 8, 512], F32))

        def bank_h(b):
            return ps[:, b, :].bitcast(F16)

        s_edges, s_x, s_w, s_word_st, s_win, s_gather = [
            sig(n) for n in ("edges_loaded", "x_loaded", "weights_loaded", "words_stored",
                             "windows_written", "windows_gathered")]
        dve, act, pool, pe = sig("dve_step"), sig("act_step"), sig("pool_step"), sig("pe_step")

        def V(fn, *after):
            return put("dve", fn, after, dve)

        def A(fn, *after):
            return put("act", fn, after, act)

        def G(fn, *after):
            return put("pool", fn, after, pool)

        k_iota = put("pool", lambda e: e.iota(iota_i[:, :], [[1, P]], base=0, channel_multiplier=0), (), pool)
        k_part = put("pool", lambda e: e.iota(part_i[:, :], [[1, 1]], base=0, channel_multiplier=1), (), pool)
        k_g5 = put("pool", lambda e: e.iota(g5_i[:, :], [[GROUP * 125, NG // 125]], base=0, channel_multiplier=GROUP), (), pool)

        k_first = put("pool", lambda e: e.iota(first_word_i, [[GROUP << SRC_BITS, NG]], base=0, channel_multiplier=0), (), pool)

        pad_i = V(lambda e: e.memset(dst_i[96:128, :], 4095))
        pad_s = V(lambda e: e.memset(src_i[96:128, :], 0))
        pad_r = V(lambda e: e.memset(pad_row[:, :], NO_EDGE))
        for name, arr, tile in (("dst", dst, dst_i), ("src", src, src_i)):
            full = arr[0:EFULL * EROW].rearrange("(p m) -> p m", m=EROW)
            rest = arr[EFULL * EROW:E].rearrange("(p m) -> p m", p=1)
            dma("sp", lambda e, t=tile, f=full: e.dma_start(t[0:96, :], f[0:96, :]), (), s_edges)
            dma("sp", lambda e, t=tile, f=full: e.dma_start(t[96:EFULL, :], f[96:EFULL, :]), (pad_i, pad_s), s_edges)
            edges = dma("sp", lambda e, t=tile, r=rest: e.dma_start(t[EFULL:EFULL + 1, 0:EREST], r), (pad_i, pad_s), s_edges)

        firsts = V(lambda e: e.tensor_copy(first_word, first_word_i), k_first)
        ones_in = V(lambda e: e.memset(ones_h[:, :], 1.0))
        zero_x = V(lambda e: e.memset(xt[:, NT - 1, :], 0.0))
        dma("act", lambda e: e.dma_start(xt[:, 0:NT - 1, :], x[0:(NT - 1) * P, :].rearrange("(a q) f -> q a f", q=P)), (), s_x)
        x_in = dma("act", lambda e: e.dma_start(xt[0:TAIL, NT - 1, :], x[(NT - 1) * P:N, :]), (zero_x,), s_x)
        for fn in (lambda e: e.dma_start(gw1[:, :, :], gW1.rearrange("(b p) f -> p b f", p=P)),
                   lambda e: e.dma_start(gw2[:, :, :], gW2.rearrange("(b p) f -> p b f", p=P)),
                   lambda e: e.dma_start(gb1c[:, :], gb1.rearrange("(b p) -> p b", p=P)),
                   lambda e: e.dma_start(gb2row[:, :], gb2.partition_broadcast(P)),
                   lambda e: e.dma_start(alpha[:, :], prelu_a.partition_broadcast(P)),
                   lambda e: e.dma_start(gatew[:, :, :], gate_w.rearrange("(b p) n -> p b n", p=P)),
                   lambda e: e.dma_start(gatebr[:, :], gate_b.partition_broadcast(P))):
            w_in = dma("act", fn, (), s_w)

        words = V(lambda e: e.scalar_tensor_tensor(out=word_f[0:EPARTS, :], in0=dst_i[0:EPARTS, :], scalar=float(1 << SRC_BITS),
                                                   in1=src_i[0:EPARTS, :], op0=ALU.mult, op1=ALU.add), edges)
        cm = V(lambda e: e.tensor_reduce(cmax[0:EPARTS, :], word_f[0:EPARTS, :].rearrange("p (c k) -> p c k", k=CHUNK), AX.X, ALU.max), words)
        dma("sp", lambda e: e.dma_start(word_dram[0:EPARTS * EROW].rearrange("(p m) -> p m", m=EROW), word_f[0:EPARTS, :]), (words,), s_word_st)
        words_st = dma("sp", lambda e: e.dma_start(word_dram[EPARTS * EROW:].rearrange("(p m) -> p m", p=1), pad_row[:, :]), (pad_r,), s_word_st)
        starts = ps[0:125, 6, 0:NG // 125]
        cmp_read = []
        for c in range(CH_ROW):
            r = c % CMP_RING
            cmp = V(lambda e, c=c, r=r: e.tensor_scalar(below[0:EPARTS, r, 0:NG], first_word[0:EPARTS, :], cmax[0:EPARTS, c:c + 1], None, ALU.is_gt),
                    cm, firsts, cmp_read[c - CMP_RING] if c >= CMP_RING else None)
            for t in range(NG // 125):
                end = t == NG // 125 - 1
                tok = put("pe", lambda e, c=c, r=r, t=t, end=end: e.matmul(
                    ps[0:125, 6, t:t + 1], below[0:EPARTS, r, t * 125:(t + 1) * 125], ones_h[0:EPARTS, :], start=c == 0 and t == 0,
                    stop=c == CH_ROW - 1 and end, skip_group_check=True), (cmp, ones_in), pe if end else None)
            cmp_read.append(tok)
        st_u = V(lambda e: e.tensor_copy(start_u[0:125, :], starts), tok)
        win_src = bass.AP(tensor=word_dram.tensor, offset=0, ap=[[CHUNK, NCHUNK], [1, WINDOW]])
        win_ok = dma("sp", lambda e: e.dma_start(win_dram, win_src), (words_st,), s_win)
        zero_z = V(lambda e: e.memset(zeros, 0.0))
        V(lambda e: e.memset(ones_sq[:, :], 1.0))
        V(lambda e: e.memset(ones_f[:, :], 1.0))
        V(lambda e: e.memset(runs[:, 0, :], 0.0))
        low0 = V(lambda e: e.memset(lower[:, :, :], 0.0))
        for k in range(1, NE):
            V(lambda e, k=k: e.memset(lower[:, k, 0:k], 1.0), low0)
        for k in range(NE):
            V(lambda e, k=k: e.memset(e_row[:, k:k + 1], float(k * CAP)))
        for r in range(2):
            c_ih = V(lambda e, r=r: e.tensor_copy(iota_h[:, :, r], iota_i[:, :]), k_iota)
        V(lambda e: e.tensor_copy(iota_f[:, :], iota_i[:, :]))
        c_pf = V(lambda e: e.tensor_copy(part_f[:, :], part_i[:, :]), k_part)
        c_idf = V(lambda e: e.tensor_scalar(ident_f[:, :], iota_f[:, :], part_f[:, 0:1], None, ALU.is_equal), c_pf)
        c_idh = V(lambda e: e.tensor_scalar(ident_h[:, :], iota_f[:, :], part_f[:, 0:1], None, ALU.is_equal))
        V(lambda e: e.tensor_scalar(tri_h[:, :], iota_f[:, :], part_f[:, 0:1], None, ALU.is_gt))
        V(lambda e: e.tensor_scalar(valid[:, :], part_f[:, :], float(TAIL), None, ALU.is_lt))
        V(lambda e: e.tensor_copy(tcol[:, :], iota_i[:, 0:ETILES]))
        V(lambda e: e.memset(epsc[:, :], LN_EPS))
        c_gate = V(lambda e: e.tensor_scalar(gatew[:, :, :], gatew[:, :, :], 1.0 / FEATURE_SCALE, None, ALU.mult), w_in)
        V(lambda e: e.tensor_copy(g5_f[:, :], g5_i[:, :]), k_g5)
        for a in range(NT):
            V(lambda e, a=a: e.bn_stats(bn6[:, a, :], xt[:, a, :]), x_in)
        t0 = (dve.sem, dve.value)
        for a in range(NT):
            t1 = V(lambda e, a=a: e.bn_aggr(mv[:, a, :], bn6[:, a, :]), t0)
        t2 = A(lambda e: e.activation(rstd[:, :], mv[:, :, 1], ACT.Sqrt, bias=epsc[:, 0:1]), t1)
        t3 = V(lambda e: e.reciprocal(rstd[:, :], rstd[:, :]), t2)
        t4 = V(lambda e: e.scalar_tensor_tensor(out=nmr[:, :], in0=mv[:, :, 0], scalar=-1.0, in1=rstd[:, :], op0=ALU.mult, op1=ALU.mult), t3)
        V(lambda e: e.tensor_scalar(rstd_s[:, :], rstd[:, :], FEATURE_SCALE, None, ALU.mult))
        t4 = V(lambda e: e.tensor_scalar(nmr_s[:, :], nmr[:, :], FEATURE_SCALE, None, ALU.mult), t4)

        for t in range(NG // 125):
            gat = dma("pool", lambda e, t=t: e.indirect_dma_start(
                out=win[0:125, t, :], out_offset=None, in_=win_dram,
                in_offset=bass.IndirectOffsetOnAxis(ap=start_u[0:125, t:t + 1], axis=0)), (st_u, win_ok), s_gather)
        zero_rows = dma("sp", lambda e: e.dma_start(
            shared_dram[COUNTS:].rearrange("(p k c) -> p k c", p=P, c=ZW),
            zeros.rearrange("p (o c) -> p o c", o=1).broadcast_to([P, (NE * CAP * 2 * D - COUNTS) // P // ZW, ZW])), (zero_z, gat), sig("rows_zeroed"))
        u1 = V(lambda e: e.tensor_copy(word_i[0:125, :], win[0:125, :, :].rearrange("p t w -> p (t w)")), gat)
        u2 = V(lambda e: e.tensor_scalar(place_i[0:125, :], word_i[0:125, :], P - 1, None, ALU.bitwise_and), u1)
        u3 = V(lambda e: e.tensor_scalar(tile_i[0:125, :], word_i[0:125, :], 7, 31, ALU.logical_shift_right, ALU.bitwise_and))
        u4 = V(lambda e: e.tensor_scalar(dest_i[0:125, :], word_i[0:125, :], SRC_BITS, None, ALU.logical_shift_right))
        u5 = V(lambda e: e.tensor_copy(place_f[0:125, :], place_i[0:125, :]), u2)
        for t in range(NG // 125):
            u6 = V(lambda e, t=t: e.tensor_scalar(code_f[0:125, t * WINDOW:(t + 1) * WINDOW], dest_i[0:125, t * WINDOW:(t + 1) * WINDOW],
                                                  g5_f[0:125, t:t + 1], float(NT), ALU.subtract, ALU.mult), u4)
        u7 = V(lambda e: e.tensor_tensor(code_f[0:125, :], code_f[0:125, :], tile_i[0:125, :], ALU.add), u6, u3)
        u7 = V(lambda e: e.tensor_scalar(code_f[0:125, :], code_f[0:125, :], -1.0, float(P - 1), ALU.max, ALU.min), u7)
        turned = None
        n_turn = 0
        bank_free = [None] * 8
        for srcf, dstT, ready in ((place_f, placeT, u5), (code_f, codeT, u7)):
            for r in range(2):
                for t0 in range(0, NG // 125, 4):
                    tn = min(4, NG // 125 - t0)
                    b = n_turn % 4
                    for t in range(t0, t0 + tn):
                        last = t == t0 + tn - 1
                        tok = put("pe", lambda e, t=t, t0=t0, b=b, s=srcf, r=r: e.transpose(
                            ps[:, b, (t - t0) * 125:(t - t0 + 1) * 125], s[0:125, t * WINDOW + r * P:t * WINDOW + r * P + P], ident_f[0:125, 0:125]),
                            (ready, c_idf, bank_free[b]), pe if last else None)
                    bank_free[b] = turned = V(lambda e, d=dstT, r=r, t0=t0, tn=tn, b=b: e.tensor_copy(
                        d[:, t0 * 125:(t0 + tn) * 125, r], ps[:, b, 0:tn * 125]), tok)
                    n_turn += 1

        feat_ready = [None] * NT

        def normalise(a):
            t5 = V(lambda e: e.tensor_scalar(hbuf[:, a % 4, :], xt[:, a, :], rstd_s[:, a:a + 1], nmr_s[:, a:a + 1], ALU.mult, ALU.add),
                   t4, feat_ready[a - 4] if a >= 4 else None)
            t6 = A(lambda e: e.activation(feat[:, a, 0:D], xt[:, a, :], ACT.Identity, bias=nmr_s[:, a:a + 1], scale=rstd_s[:, a:a + 1]), t4)
            feat_ready[a] = G(lambda e: e.tensor_tensor(feat[:, a, D:2 * D], hbuf[:, a % 4, :], feat[:, a, 0:D], ALU.subtract), t5, t6)

        def prepare_graph_weights():
            for b in range(FB):
                q1 = A(lambda e, b=b: e.activation(work[:, b, :], gw1[:, b, :], ACT.Square, accum_out=nrm[:, b:b + 1]), w_in)
            q2 = A(lambda e: e.activation(nrm[:, :], nrm[:, :], ACT.Sqrt), q1)
            q3 = V(lambda e: e.scalar_tensor_tensor(out=amax[:, :], in0=alpha[:, :], scalar=-1.0, in1=alpha[:, :], op0=ALU.mult, op1=ALU.max), w_in)
            q3 = V(lambda e: e.tensor_scalar(amax[:, :], amax[:, :], 1.0, None, ALU.max), q3)
            q4 = V(lambda e: e.scalar_tensor_tensor(out=gb1s[:, :], in0=gb1c[:, :], scalar=-1.0, in1=gb1c[:, :], op0=ALU.mult, op1=ALU.max))
            q5 = V(lambda e: e.scalar_tensor_tensor(out=invs[:, :], in0=nrm[:, :], scalar=16.0, in1=gb1s[:, :], op0=ALU.mult, op1=ALU.add), q2, q4)
            q6 = V(lambda e: e.tensor_scalar(invs[:, :], invs[:, :], amax[:, 0:1], 1.0 / HALF_TOP, ALU.mult, ALU.mult), q5)
            q7 = V(lambda e: e.tensor_scalar(invs[:, :], invs[:, :], 1e-30, None, ALU.max), q6)
            q8 = V(lambda e: e.reciprocal(scl[:, :], invs[:, :]), q7)
            q9 = V(lambda e: e.tensor_tensor(gb1s[:, :], gb1c[:, :], scl[:, :], ALU.mult), q8)
            for b in range(FB):
                q10 = V(lambda e, b=b: e.tensor_scalar(gw1[:, b, :], gw1[:, b, :], scl[:, b:b + 1], 1.0 / FEATURE_SCALE, ALU.mult, ALU.mult), q8)
            for b in range(FB):
                q11 = V(lambda e, b=b: e.tensor_scalar(gb1b[:, :], iota_f[:, :], 0.0, gb1s[:, b:b + 1], ALU.mult, ALU.add), q9, (pe.sem, pe.value))
                q12 = put("pe", lambda e, b=b: e.matmul(ps[:, 7, 0:P], gb1b[:, :], ident_f[:, :], start=True, stop=True), (q11, bank_free[7], c_idf), pe)
                q13 = V(lambda e, b=b: e.tensor_copy(gb1row[:, b * P:(b + 1) * P], ps[:, 7, 0:P]), q12)
                bank_free[7] = q13
            for w, wT, ready in ((gw1, gw1T, q10), (gw2, gw2T, w_in)):
                for ob in range(FB):
                    for fb in range(FB):
                        tok = put("pe", lambda e, w=w, ob=ob, fb=fb: e.transpose(ps[:, 7, 0:P], w[:, ob, fb * P:(fb + 1) * P], ident_f[:, :]), (ready, bank_free[7], c_idf), pe)
                        if wT is gw1T:
                            bank_free[7] = V(lambda e, ob=ob, fb=fb: e.tensor_copy(gw1T[:, fb, ob * P:(ob + 1) * P], ps[:, 7, 0:P]), tok)
                        else:
                            bank_free[7] = V(lambda e, ob=ob, fb=fb: e.tensor_scalar(gw2T[:, fb, ob * P:(ob + 1) * P], ps[:, 7, 0:P], invs[:, fb:fb + 1], None, ALU.mult), tok)
            return bank_free[7]

        def count_covered():
            counted = u7
            for k, bound in enumerate((0.0, float(GC))):
                counted = V(lambda e, k=k, bound=bound: e.tensor_scalar(tile_i[0:125, :].bitcast(F32), code_f[0:125, :], bound, 0.0, ALU.is_ge, ALU.add,
                                                                        accum_out=covered[0:125, k:k + 1]), counted)
            return V(lambda e: e.tensor_tensor(covered[0:125, 0:1], covered[0:125, 0:1], covered[0:125, 1:2], ALU.subtract), counted)

        def look_for_uncovered():
            t = put("pe", lambda e: e.matmul(ps[:, 7, 0:1], ones_f[0:125, :], covered[0:125, 0:1], start=True, stop=True), (counted, bank_free[7]), pe)
            bank_free[7] = V(lambda e: e.tensor_scalar(uncovered[:, :], ps[:, 7, 0:1], float(E), None, ALU.not_equal), t)
            return bank_free[7]

        s_oh, s_used, s_quad_out = sig("onehots_made"), sig("onehots_used"), sig("quad_copied")
        s_turn, s_turn_out, s_p1, s_hi, s_lo = sig("tiles_turned"), sig("turned_copied"), sig("p1_summed"), sig("ef_high"), sig("ef_rest")
        s_st = [[sig(f"stored_{side}_{b}") for b in range(2)] for side in ("src", "dst")]
        used = []
        quad_out = [None, None]
        turn_out = [None, None]
        p1_out = [(None, None), (None, None)]
        src_stored = [None, None]
        dst_stored = [None, None]
        src_read = [None, None]
        dst_read = [None, None]
        n_quad = 0

        def p1(bank, counts, rows, ready, free, done):
            for a in range(NT):
                for part in range(2):
                    fin = a == NT - 1 and part == 1
                    tok = put("pe", lambda e, a=a, part=part: e.matmul(
                        ps[0:rows, bank, 0:D], counts[:, a, :], feat[:, a, part * D:(part + 1) * D],
                        start=a == 0 and part == 0, stop=a == NT - 1 and part == 1),
                        tuple(free) + (ready, feat_ready[a]), done if fin else None)
            return tok

        def ef_high(bank, s, summed, *more):
            return put("act", lambda e: e.activation(ef[0:SROWS, s, 0:D], ps[0:SROWS, bank, 0:D], ACT.Copy, scale=binv[0:SROWS, s:s + 1]), (summed,) + more, s_hi)

        def ef_rest(bank, s, summed, high):
            return put("dve", lambda e: e.scalar_tensor_tensor(out=ef[0:SROWS, s, D:2 * D], in0=ps[0:SROWS, bank, 0:D], scalar=binv[0:SROWS, s:s + 1],
                                                               in1=ef[0:SROWS, s, 0:D], op0=ALU.mult, op1=ALU.subtract), (summed, high), s_lo)

        QUAD_BANKS = (0, 1, 7)
        quad_out = [None] * 3
        weights_ready = None

        def work_on(s, strip_ready):
            slot = s % 2
            counts = strips[:, slot, 0:NT * SROWS].rearrange("p (a j) -> p a j", j=SROWS)
            state = {}

            def turn(k):
                a0, an = TGROUPS[k]
                b = k % 2
                for a in range(a0, a0 + an):
                    tok = put("pe", lambda e, a=a: e.transpose(bank_h(2 + b)[0:SROWS, (a - a0) * P:(a - a0 + 1) * P], counts[:, a, :], ident_h[:, :]),
                              (strip_ready, turn_out[b], c_idh), s_turn if a == a0 + an - 1 else None)
                turn_out[b] = put("act", lambda e: e.activation(strips[0:SROWS, 2 + slot, a0 * P:(a0 + an) * P], bank_h(2 + b)[0:SROWS, 0:an * P], ACT.Copy,
                                                                accum_out=degj[0:SROWS, slot, k:k + 1]),
                                  (tok, dst_stored[slot], dst_read[slot], deg_read[slot]), s_turn_out)
                if k == len(TGROUPS) - 1:
                    state["turned"] = turn_out[b]
                    dst_stored[slot] = dma("sp", lambda e: e.dma_start(dstside_dram[s], strips[0:SROWS, 2 + slot, :]), (turn_out[b],), s_st[1][slot])
                    stored_upto[s] = (dst_stored[0], dst_stored[1])

            def product(a0, a1):
                for a in range(a0, a1):
                    for part in range(2):
                        fin = a == NT - 1 and part == 1
                        tok = put("pe", lambda e, a=a, part=part: e.matmul(
                            ps[0:SROWS, 4 + s % 2, 0:D], counts[:, a, :], feat[:, a, part * D:(part + 1) * D],
                            start=a == 0 and part == 0, stop=a == NT - 1 and part == 1),
                            tuple(p1_out[s % 2]) + (strip_ready, feat_ready[a]), s_p1 if fin else None)
                if a1 == NT:
                    src_read[slot] = state["summed"] = tok

            def source_degrees(a0, a1):
                for a in range(a0, a1):
                    dst_read[slot] = put("pe", lambda e, a=a: e.matmul(
                        ps[:, 6, a:a + 1], strips[0:SROWS, 2 + slot, a * P:(a + 1) * P], ones_h[0:SROWS, :], start=s == 0 and a == 0,
                        stop=s == NS - 1 and a == NT - 1, skip_group_check=True), (state["turned"],), s_deg if a == NT - 1 else None)

            def part(k, of=len(QUADS)):
                if k == 0:
                    src_stored[slot] = dma("sp", lambda e: e.dma_start(srcside_dram[s], strips[:, slot, 0:NT * SROWS]), (strip_ready,), s_st[0][slot])
                if k < len(TGROUPS):
                    turn(k)
                product(NT * k // of, NT * (k + 1) // of)
                if k > len(TGROUPS):
                    n = of - len(TGROUPS) - 1
                    i = k - len(TGROUPS) - 1
                    source_degrees(NT * i // n, NT * (i + 1) // n)

            def split(k):
                if k == 0:
                    deg_read[slot] = r1 = V(lambda e: e.tensor_reduce(binv[0:SROWS, s:s + 1], degj[0:SROWS, slot, :], AX.X, ALU.add), state["turned"])
                    r2 = V(lambda e: e.tensor_scalar(binv[0:SROWS, s:s + 1], binv[0:SROWS, s:s + 1], 1.0, None, ALU.max), r1)
                    state["inverse"] = V(lambda e: e.reciprocal(binv[0:SROWS, s:s + 1], binv[0:SROWS, s:s + 1]), r2)
                elif k == 1:
                    state["high"] = ef_high(4 + s % 2, s, state["summed"], state["inverse"])
                else:
                    p1_out[s % 2] = (state["high"], ef_rest(4 + s % 2, s, state["summed"], state["high"]))

            return part, split

        s_deg = sig("source_degrees_summed")
        deg_read = [None, None]
        stored_upto = [None] * NS
        part = split = split_before = None
        SPLIT_AT = [0, 1, 1 + OH_RING]
        for s in range(NS):
            slot = s % 2
            strip_view = strips[:, slot, 0:NT * SROWS].rearrange("p (a j) -> p j a", j=SROWS)
            if s == 2:
                bank_free[7] = (s_quad_out.sem, s_quad_out.value)
                weights_ready = prepare_graph_weights()
                flag_ready = look_for_uncovered()
            for qi, (q0, qn) in enumerate(QUADS):
                g0 = s * STRIP_GROUPS + q0
                ring = n_quad % OH_RING
                b = n_quad % 3
                bank = QUAD_BANKS[b]
                put("dve", lambda e, g0=g0, qn=qn, ring=ring: e.tensor_tensor(
                    ohA[:, ring, 0:qn, 0:GC, :], codeT[:, g0:g0 + qn, :].rearrange("p g (o r) -> p g o r", o=1).broadcast_to([P, qn, GC, 2]),
                    iota_h[:, 0:GC, :].rearrange("p (o c) r -> p o c r", o=1).broadcast_to([P, qn, GC, 2]), ALU.is_equal),
                    (used[n_quad - OH_RING] if n_quad >= OH_RING else None, turned, c_ih), None)
                made = put("dve", lambda e, g0=g0, qn=qn, ring=ring: e.tensor_tensor(
                    ohQ[:, ring, 0:qn, :, :], placeT[:, g0:g0 + qn, :].rearrange("p g (o r) -> p g o r", o=1).broadcast_to([P, qn, P, 2]),
                    iota_h[:, :, :].rearrange("p (o c) r -> p o c r", o=1).broadcast_to([P, qn, P, 2]), ALU.is_equal), (), s_oh)
                n_quad += 1
                for k in range(qn):
                    for r in range(2):
                        tok = put("pe", lambda e, k=k, ring=ring, r=r, bank=bank: e.matmul(
                            ps[:, bank, k * GC:(k + 1) * GC], ohQ[:, ring, k, :, r], ohA[:, ring, k, 0:GC, r], start=r == 0, stop=r == 1),
                            (made, quad_out[b], turned, bank_free[7]), s_used if k == qn - 1 and r == 1 else None)
                used.append(tok)
                quad_out[b] = put("act", lambda e, v=strip_view, q0=q0, qn=qn, bank=bank: e.activation(
                    v[:, q0 * GROUP:(q0 + qn) * GROUP, :], ps[:, bank, 0:qn * GC].rearrange("p (j a) -> p j a", a=NT), ACT.Copy),
                    (tok, src_stored[slot], src_read[slot]), s_quad_out)
                if s == 1 and qi == 3:
                    counted = count_covered()
                if s == 0:
                    for a in range(NT * qi // len(QUADS), NT * (qi + 1) // len(QUADS)):
                        normalise(a)
                if part:
                    part(qi)
                if split_before and qi in SPLIT_AT:
                    split_before(SPLIT_AT.index(qi))
            split_before = split
            part, split = work_on(s, quad_out[b])
        for k in range(len(QUADS)):
            part(k)
            if k == 0:
                for i in range(3):
                    split_before(i)
        for i in range(3):
            split(i)
        dv1 = V(lambda e: e.tensor_scalar(dinv[:, :], ps[:, 6, 0:NT], 1.0, None, ALU.max), dst_read[(NS - 1) % 2])
        dinv_ready = V(lambda e: e.reciprocal(dinv[:, :], dinv[:, :]), dv1)

        build_done = tuple(x.now() for x in all_signals if x.value)
        turn = Turn(sig("general_turn"))
        step = turn.step
        COUNT_SCALE = 0.25
        step("pool", lambda e: e.iota(g_ohc.bitcast(I32)[:, 0:NT * SROWS], [[1, NT * SROWS]], base=1, channel_multiplier=0))
        step("dve", lambda e: e.tensor_copy(g_codes1, g_ohc.bitcast(I32)[:, 0:NT * SROWS]))
        step("dve", lambda e: e.memset(g_ohc, 0.0))
        step("sp", lambda e: e.dma_start(g_words, word_dram[0:P * EDGE_COLS].rearrange("(p m) -> p m", m=EDGE_COLS)), by=16)
        step("dve", lambda e: e.tensor_copy(g_int, g_words))
        step("dve", lambda e: e.tensor_copy(g_words_i, g_int))
        step("dve", lambda e: e.tensor_scalar(g_int, g_words_i, P - 1, None, ALU.bitwise_and))
        step("dve", lambda e: e.tensor_copy(g_place, g_int))
        step("dve", lambda e: e.tensor_scalar(g_int, g_words_i, SRC_BITS, None, ALU.logical_shift_right))
        step("dve", lambda e: e.tensor_copy(g_dst, g_int))
        step("dve", lambda e: e.tensor_scalar(g_int, g_words_i, 7, 31, ALU.logical_shift_right, ALU.bitwise_and))
        step("dve", lambda e: e.tensor_copy(g_all, g_int))
        step("dve", lambda e: e.scalar_tensor_tensor(out=g_all, in0=g_all, scalar=float(SROWS), in1=g_dst, op0=ALU.mult, op1=ALU.add))

        def g_banks(lhsT, rhs, start, stop):
            return [lambda e, a=a: e.matmul(ps[:, a // 4, 0:(min(a + 4, NT) - a) * SROWS], lhsT, rhs[:, a * SROWS:min(a + 4, NT) * SROWS],
                                            start=start, stop=stop, skip_group_check=True) for a in range(0, NT, 4)]

        def g_onehots(e, i):
            for k in range(TRIO):
                e.tensor_scalar(g_ohc[:, k * G_OH:k * G_OH + NT * SROWS], g_codes1, g_code[:, bass.ds(i * TRIO + k, 1)], None, ALU.is_equal)
            for k in range(TRIO):
                ins = e.tensor_scalar(g_ohp[:, k, :], iota_f[:, :], g_place[:, bass.ds(i * TRIO + k, 1)], None, ALU.is_equal)
            return ins

        def g_count(e, i):
            for k in range(TRIO):
                for fn in g_banks(g_ohp[:, k, :], g_ohc[:, k * G_OH:(k + 1) * G_OH], False, False):
                    ins = fn(e)
            return ins

        for s in range(NS):
            step("dve", lambda e, s=s: e.tensor_scalar(g_code, g_dst, float(s * SROWS), None, ALU.is_ge))
            step("dve", lambda e, s=s: e.scalar_tensor_tensor(out=g_code, in0=g_dst, scalar=float((s + 1) * SROWS), in1=g_code, op0=ALU.is_lt, op1=ALU.mult))
            step("dve", lambda e, s=s: e.scalar_tensor_tensor(out=g_code, in0=g_all, scalar=float(1 - s * SROWS), in1=g_code, op0=ALU.add, op1=ALU.mult),
                 lambda e: e.memset(g_ohp[:, 0, :], 0.0))
            step("pe", *g_banks(g_ohp[:, 0, :], g_ohc, True, False))
            turn.loop(EDGE_COLS // TRIO, ("dve", g_onehots), ("pe", g_count))
            step("dve", lambda e: e.memset(g_ohp[:, 0, :], 0.0))
            step("pe", *g_banks(g_ohp[:, 0, :], g_ohc, False, True))
            step("act", *[lambda e, a=a: e.activation(g_src_side[:, a * SROWS:min(a + 4, NT) * SROWS], ps[:, a // 4, 0:(min(a + 4, NT) - a) * SROWS],
                                                      ACT.Copy, scale=COUNT_SCALE) for a in range(0, NT, 4)])
            step("sp", lambda e, s=s: e.dma_start(srcside_dram[s], g_src_side[:, 0:NT * SROWS]), by=16)
            for k, (a0, an) in enumerate(TGROUPS):
                step("pe", *[lambda e, a=a, a0=a0: e.transpose(bank_h(7)[0:SROWS, (a - a0) * P:(a - a0 + 1) * P], g_src_side[:, a * SROWS:(a + 1) * SROWS],
                                                              ident_h[:, :]) for a in range(a0, a0 + an)])
                step("act", lambda e, k=k, a0=a0, an=an: e.activation(g_dst_side[:, a0 * P:(a0 + an) * P], bank_h(7)[0:SROWS, 0:an * P], ACT.Copy,
                                                                      accum_out=degj[0:SROWS, 0, k:k + 1]))
            step("sp", lambda e, s=s: e.dma_start(dstside_dram[s], g_dst_side), by=16)
            step("pe", *[lambda e, a=a, part=part: e.matmul(ps[0:SROWS, 7, 0:D], g_src_side[:, a * SROWS:(a + 1) * SROWS], feat[:, a, part * D:(part + 1) * D],
                                                            start=a == 0 and part == 0, stop=a == NT - 1 and part == 1)
                         for a in range(NT) for part in range(2)])
            inv = binv[0:SROWS, s:s + 1]
            step("dve", lambda e, inv=inv: e.tensor_reduce(inv, degj[0:SROWS, 0, :], AX.X, ALU.add))
            step("dve", lambda e, inv=inv: e.tensor_scalar(inv, inv, 1.0, COUNT_SCALE, ALU.mult, ALU.max))
            step("dve", lambda e, inv=inv: e.reciprocal(inv, inv))
            step("act", lambda e, s=s, inv=inv: e.activation(ef[0:SROWS, s, 0:D], ps[0:SROWS, 7, 0:D], ACT.Copy, scale=inv))
            step("dve", lambda e, s=s, inv=inv: e.scalar_tensor_tensor(out=ef[0:SROWS, s, D:2 * D], in0=ps[0:SROWS, 7, 0:D], scalar=inv,
                                                                       in1=ef[0:SROWS, s, 0:D], op0=ALU.mult, op1=ALU.subtract))
            step("pe", *[lambda e, a=a: e.matmul(ps[:, 7, a:a + 1], g_dst_side[:, a * P:(a + 1) * P], ones_h[0:SROWS, :], start=True, stop=True) for a in range(NT)])
            if s == 0:
                step("dve", lambda e: e.tensor_copy(dinv[:, :], ps[:, 7, 0:NT]))
            else:
                step("dve", lambda e: e.tensor_tensor(dinv[:, :], dinv[:, :], ps[:, 7, 0:NT], ALU.add))
        step("dve", lambda e: e.tensor_scalar(dinv[:, :], dinv[:, :], COUNT_SCALE, None, ALU.max))
        step("dve", lambda e: e.reciprocal(dinv[:, :], dinv[:, :]))

        def general_path(engine):
            def fn(e):
                flag = e.value_load(uncovered[0:1, 0:1], min_val=0, max_val=1)
                with e.If(flag):
                    for sem, value in build_done:
                        e.wait_ge(sem, value)
                    for body in turn.bodies[engine]:
                        body(e)
                    e.wait_ge(turn.clock.sem, turn.clock.value)
            put(engine, fn, (flag_ready,), None)

        for engine in prog.queues:
            general_path(engine)

        s_blk = [sig(f"block_loaded_{b}") for b in range(3)]
        s_p2, s_p2_out, s_wp = sig("p2_summed"), sig("p2_copied"), sig("weight_product")
        s_sr = [sig(f"strip_loaded_{b}") for b in range(4)]
        onehots_used = (s_used.sem, s_used.value)
        blk_read = [onehots_used] * 3
        p2_out = [(s_quad_out.sem, s_quad_out.value), (s_turn_out.sem, s_turn_out.value)]
        stT_free = [turned, turned]
        wp_out = [p1_out[0][1], p1_out[1][1]]
        n_blk = n_half = n_tile = 0
        later = []

        def point():
            for item in later:
                item[0] -= 1
            if later and later[0][0] < 0:
                later.pop(0)[1]()

        def p2_layer(wT, ef_ready, post, finish_block, behind_post):
            nonlocal n_blk, n_half, n_tile

            def weight(bi, buf, copied):
                nonlocal n_tile
                b0, bn = BLOCKS[bi]
                for k in range(bn):
                    bank = 4 + n_tile % 2
                    for fb in range(FB):
                        tok = put("pe", lambda e, fb=fb, k=k, bank=bank, buf=buf: e.matmul(
                            ps[:, bank, 0:D], stT[:, buf, fb, k * P:(k + 1) * P], wT[:, fb, :], start=fb == 0, stop=fb == FB - 1),
                            (copied, wp_out[n_tile % 2], weights_ready), s_wp if fb == FB - 1 else None)
                    wp_out[n_tile % 2] = post(b0 + k, bank, tok)
                    n_tile += 1
                stT_free[buf] = tok
                if finish_block:
                    finish_block(bi)

            for bi, (b0, bn) in enumerate(BLOCKS):
                buf = n_blk % 2
                n_blk += 1
                w = bn * P
                for s0, s1 in HALVES:
                    half = n_half % 3
                    n_half += 1
                    loaded = dma("sp", lambda e, b0=b0, w=w, half=half, s0=s0, s1=s1: e.dma_start(
                        blocks[0:SROWS, half, 0:s1 - s0, 0:w], dstside_dram.rearrange("s p n -> p s n")[:, s0:s1, b0 * P:b0 * P + w]),
                        tuple(stored_upto[s1 - 1]) + (blk_read[half],), s_blk[half])
                    for s in range(s0, s1):
                        for fb in range(FB):
                            for part in range(2):
                                fin = s == s1 - 1 and fb == FB - 1 and part == 1
                                tok = put("pe", lambda e, s=s, fb=fb, part=part, buf=buf, w=w, half=half, s0=s0: e.matmul(
                                    ps[:, 2 * buf + fb, 0:w], ef[0:SROWS, s, part * D + fb * P:part * D + (fb + 1) * P], blocks[0:SROWS, half, s - s0, 0:w],
                                    start=s == 0 and part == 0, stop=s == NS - 1 and part == 1),
                                    (loaded, ef_ready, p2_out[buf]), s_p2 if fin else None)
                        if s == NS - 1:
                            for fb in range(FB):
                                p2_out[buf] = put("act", lambda e, fb=fb, buf=buf, w=w: e.activation(stT[:, buf, fb, 0:w], ps[:, 2 * buf + fb, 0:w], ACT.Copy),
                                                  (tok, stT_free[buf]), s_p2_out)
                            later.append([1, lambda bi=bi, buf=buf, c=p2_out[buf]: weight(bi, buf, c)])
                            later.extend([n, lambda bi=bi, fn=fn: fn(bi)] for n, fn in behind_post)
                            later.sort(key=lambda item: item[0])
                        if s % 5 == 4:
                            point()
                    blk_read[half] = tok
            while later:
                later.pop(0)[1]()
            return (s_p2.sem, s_p2.value)

        def prelu_into(dst_ap, u, tok):
            m = V(lambda e: e.tensor_scalar(work[:, 3, :], u, 0.0, alpha[:, 0:1], ALU.min, ALU.mult), tok)
            return V(lambda e: e.scalar_tensor_tensor(out=dst_ap, in0=u, scalar=0.0, in1=work[:, 3, :], op0=ALU.max, op1=ALU.add), m)

        feat2_ready = [None] * NT

        def post1(a, bank, summed):
            u = V(lambda e: e.scalar_tensor_tensor(out=work[:, 0, :], in0=ps[:, bank, 0:D], scalar=dinv[:, a:a + 1], in1=gb1row[:, :], op0=ALU.mult, op1=ALU.add), summed, dinv_ready)
            v = prelu_into(work[:, 1, :], work[:, 0, :], u)
            hi = V(lambda e: e.tensor_copy(feat[:, a, 0:D], work[:, 1, :]), v)
            feat2_ready[a] = V(lambda e: e.tensor_tensor(feat[:, a, D:2 * D], work[:, 1, :], feat[:, a, 0:D], ALU.subtract), hi)
            return u

        ef_ready = p1_out[(NS - 1) % 2][1]
        last_p2 = p2_layer(gw1T, ef_ready, post1, None, [])

        s_stage = [sig(f"stage_loaded_{b}") for b in range(2)]
        s_restage = [sig(f"stage_loaded_again_{b}") for b in range(2)]
        s_stage_used, s_wpart = sig("stage_used"), sig("expert_parts")
        stage_free = [None, None]
        n_stage = 0

        def stage_piece(i, engine="sp"):
            nonlocal n_stage
            k = n_stage % 2
            n_stage += 1
            piece = (W2 if i % 2 else W1)[i // 2].rearrange("(b p) n -> p b n", p=P)
            tok = dma(engine, lambda e: e.dma_start(stage[:, k, :].rearrange("p (b n) -> p b n", b=piece.shape[1]), piece), (stage_free[k],), (s_stage if engine == "sp" else s_restage)[k])
            return k, tok

        def norm_piece(i):
            k, tok = stage_piece(i)
            stage_free[k] = put("act", lambda e: e.activation(stage[:, k, :], stage[:, k, :], ACT.Square, accum_out=sumsq[:, i:i + 1]), (tok,), s_stage_used)

        def split_piece(i, room):
            k, tok = staged[i]
            n = 2 * H
            at = i * 2 * n
            sc = sW2 if i % 2 else sW1
            scaled = put("act", lambda e: e.activation(stage[:, k, :], stage[:, k, :], ACT.Copy, scale=sc[:, 0:1]), (tok, scales_ready), s_stage_used)
            hi = put("act", lambda e: e.activation(region[:, at:at + n], stage[:, k, :], ACT.Copy), (scaled, room), s_stage_used)
            stage_free[k] = put("pool", lambda e: e.tensor_tensor(region[:, at + n:at + 2 * n], stage[:, k, :], region[:, at:at + n], ALU.subtract), (hi,), s_wpart)
            if i + 2 < 2 * NE:
                staged[i + 2] = stage_piece(i + 2, "pool")

        def make_scales(bank_ok):
            nb = NE * H // P
            b1_in = dma("act", lambda e: e.dma_start(hbuf[:, 0, 0:nb], b1.rearrange("n h -> (n h)").rearrange("(p m) -> p m", p=P)), (feat_ready1,), sig("b1_loaded"))
            n1 = A(lambda e: e.activation(hbuf[:, 1, 0:nb], hbuf[:, 0, 0:nb], ACT.Square, accum_out=sumsq[:, 2 * NE:2 * NE + 1]), b1_in)
            V(lambda e: e.tensor_reduce(ssum[:, 0:2], sumsq[:, 0:2 * NE].rearrange("p (n k) -> p k n", k=2), AX.X, ALU.add), (s_stage_used.sem, s_stage_used.value))
            v = V(lambda e: e.tensor_copy(ssum[:, 2:3], sumsq[:, 2 * NE:2 * NE + 1]), n1)
            t = put("pe", lambda e: e.matmul(ps[:, 6, 0:3], ones_f[:, :], ssum[:, :], start=True, stop=True), (v, bank_ok), pe)
            a = A(lambda e: e.activation(ssum[:, :], ps[:, 6, 0:3], ACT.Sqrt), t)
            a = V(lambda e: e.tensor_scalar(ssum[:, :], ssum[:, :], 1e-15, None, ALU.max), a)
            v = V(lambda e: e.scalar_tensor_tensor(out=ssum[:, 2:3], in0=ssum[:, 0:1], scalar=16.0, in1=ssum[:, 2:3], op0=ALU.mult, op1=ALU.add), a)
            v = V(lambda e: e.tensor_scalar(ssum[:, 0:2], ssum[:, 0:2], 2.0 / HALF_TOP, None, ALU.mult), v)
            v = V(lambda e: e.tensor_scalar(ssum[:, 2:3], ssum[:, 2:3], 1.0 / HALF_TOP, None, ALU.mult), v)
            V(lambda e: e.reciprocal(sW1[:, :], ssum[:, 0:1]), v)
            V(lambda e: e.reciprocal(sW2[:, :], ssum[:, 1:2]))
            V(lambda e: e.reciprocal(sH[:, :], ssum[:, 2:3]))
            V(lambda e: e.tensor_scalar(iW1[:, :], ssum[:, 0:1], 1.0 / FEATURE_SCALE, None, ALU.mult))
            return V(lambda e: e.tensor_tensor(iW2[:, :], ssum[:, 1:2], ssum[:, 2:3], ALU.mult))

        feat_ready1 = feat_ready[NT - 1]
        feat_ready = feat2_ready
        ring_read = [None] * 4
        all_stored = (src_stored[0], src_stored[1], dst_stored[0], dst_stored[1], dst_read[0], dst_read[1])
        for s in range(NS):
            slot_s = s % 4
            loaded = dma("sp", lambda e, s=s, slot_s=slot_s: e.dma_start(strips[:, slot_s, 0:NT * SROWS], srcside_dram[s]),
                         all_stored + (ring_read[slot_s],), s_sr[slot_s])
            counts = strips[:, slot_s, 0:NT * SROWS].rearrange("p (a j) -> p a j", j=SROWS)
            bank = 6 + s % 2
            free = p1_out[s % 2] if s >= 2 else (dv1, (s_quad_out.sem, s_quad_out.value))
            if s < 2 * NE:
                norm_piece(s)
            tok = p1(bank, counts, SROWS, loaded, free, s_p1)
            ring_read[slot_s] = tok
            high = ef_high(bank, s, tok, last_p2)
            p1_out[s % 2] = (high, ef_rest(bank, s, tok, high))
        region_free = tok
        ef_ready = p1_out[(NS - 1) % 2][1]
        scales_ready = make_scales(ef_ready)
        staged = {i: stage_piece(i, "pool") for i in range(2)}
        strips_in = tuple((x.sem, x.value) for x in s_sr)

        s_yt, s_yt_out, s_y = sig("y_turned"), sig("y_copied"), sig("y_rows")
        s_send = [sig(f"rows_sent_{b}") for b in range(8)]
        sent = {}
        turn_free = [scales_ready, p1_out[1][1]]
        y_ready, logit_done, yrow_ready = [None] * NT, [None] * NT, [None] * NT
        ycol_free = [None, None]
        ybuf_free = [scales_ready] * 4
        n_piece = 0

        summed2 = {}

        def post2(a, bank, summed):
            summed2[a] = V(lambda e: e.scalar_tensor_tensor(out=work[:, a % 4, :], in0=ps[:, bank, 0:D], scalar=dinv[:, a:a + 1], in1=gb2row[:, :], op0=ALU.mult, op1=ALU.add),
                           summed, dinv_ready, x_added.get(a - 4))
            return summed2[a]

        x_added = {}

        def finish2(bi):
            b0, bn = BLOCKS[bi]
            tiles = range(b0, b0 + bn)
            t = {}
            for a in tiles:
                t[a] = A(lambda e, a=a: e.activation(ybuf[:, a % 4, :], xt[:, a, :], ACT.Identity, bias=nmr[:, a:a + 1], scale=rstd[:, a:a + 1]),
                         ybuf_free[a % 4], yrow_ready[a - 4] if a >= 4 else None)
            for a in tiles:
                t[a] = V(lambda e, a=a: e.tensor_tensor(work[:, a % 4, :], work[:, a % 4, :], ybuf[:, a % 4, :], ALU.add), t[a], summed2[a])
            for a in tiles:
                t[a] = V(lambda e, a=a: e.tensor_scalar(ybuf[:, a % 4, :], work[:, a % 4, :], 0.0, alpha[:, 0:1], ALU.min, ALU.mult), t[a])
            for a in tiles:
                t[a] = V(lambda e, a=a: e.scalar_tensor_tensor(out=work[:, a % 4, :], in0=work[:, a % 4, :], scalar=0.0, in1=ybuf[:, a % 4, :], op0=ALU.max, op1=ALU.add), t[a])
                x_added[a] = t[a] = G(lambda e, a=a: e.tensor_tensor(xt[:, a, :], xt[:, a, :], work[:, a % 4, :], ALU.add), t[a])
            for a in tiles:
                t[a] = V(lambda e, a=a: e.bn_stats(bn6[:, a, :], xt[:, a, :]), t[a])
            for a in tiles:
                ag = V(lambda e, a=a: e.bn_aggr(mv[:, a, :], bn6[:, a, :]), t[a])
            sq = A(lambda e: e.activation(rstd[:, b0:b0 + bn], mv[:, b0:b0 + bn, 1], ACT.Sqrt, bias=epsc[:, 0:1]), ag)
            rc = V(lambda e: e.reciprocal(rstd[:, b0:b0 + bn], rstd[:, b0:b0 + bn]), sq)
            rc = V(lambda e: e.tensor_scalar(rstd[:, b0:b0 + bn], rstd[:, b0:b0 + bn], FEATURE_SCALE, None, ALU.mult), rc)
            for a in tiles:
                k, r = a % 4, a % 8
                y = y_ready[a] = V(lambda e, a=a, k=k: e.tensor_scalar(ybuf[:, k, :], xt[:, a, :], mv[:, a, 0:1], rstd[:, a:a + 1], ALU.subtract, ALU.mult), rc)
                hi = put("act", lambda e, r=r, k=k: e.activation(yrow[:, r, 0:D], ybuf[:, k, :], ACT.Copy), (y, turned, sent.get(a - 8)), s_y)
                yrow_ready[a] = G(lambda e, r=r, k=k: e.tensor_tensor(yrow[:, r, D:2 * D], ybuf[:, k, :], yrow[:, r, 0:D], ALU.subtract), hi)

        def logits(bi):
            b0, bn = BLOCKS[bi]
            copied = {}

            def product(a):
                k = a % 2
                for fb in range(FB):
                    tok = put("pe", lambda e, fb=fb: e.matmul(ps[:, 6 + k, D:D + NE], ycol[:, k, fb * P:(fb + 1) * P], gatew[:, fb, :], start=fb == 0, stop=fb == FB - 1),
                              (copied[a], c_gate), s_yt if fb == FB - 1 else None)
                ycol_free[k] = tok
                turn_free[k] = logit_done[a] = V(lambda e: e.tensor_copy(logit_acc[:, a - b0, :], ps[:, 6 + k, D:D + NE]), tok)

            for a in range(b0, b0 + bn):
                k = a % 2
                if a - 2 >= b0:
                    product(a - 2)
                for fb in range(FB):
                    tok = put("pe", lambda e, fb=fb, a=a, k=k: e.transpose(ps[:, 6 + k, fb * P:(fb + 1) * P], ybuf[:, a % 4, fb * P:(fb + 1) * P], ident_f[:, :]),
                              (y_ready[a], turn_free[k]), s_yt if fb == FB - 1 else None)
                ybuf_free[a % 4] = tok
                copied[a] = put("act", lambda e, k=k: e.activation(ycol[:, k, :], ps[:, 6 + k, 0:D], ACT.Copy), (tok, ycol_free[k]), s_yt_out)
            for a in range(max(b0, b0 + bn - 2), b0 + bn):
                product(a)

        picked_ready = {}

        def gate(bi):
            nonlocal n_piece
            b0, bn = BLOCKS[bi]
            shp3, shp4 = [P, bn, NE], [P, bn, NE, NE]
            p3, c3, r3, l3 = pr[:, 0:bn, :], cw[:, 0:bn, :], rank[:, 0:bn, :], place[:, 0:bn, :]
            ca, cb = cmp_a[:, 0:bn], cmp_b[:, 0:bn]
            per_node = rd[:, 0:bn].rearrange("p (a o) -> p a o", o=1).broadcast_to(shp3)
            low = lower[:, :, :].rearrange("p (o k) n -> p o k n", o=1).broadcast_to(shp4)
            v = V(lambda e: e.tensor_tensor(p3, logit_acc[:, 0:bn, :], gatebr[:, :].rearrange("p (o k) -> p o k", o=1).broadcast_to(shp3), ALU.add), logit_done[b0 + bn - 1])
            v = V(lambda e: e.tensor_reduce(rd[:, 0:bn], p3, AX.X, ALU.max), v)
            v = V(lambda e: e.tensor_tensor(p3, p3, per_node, ALU.subtract), v)
            v = A(lambda e: e.activation(p3, p3, ACT.Exp), v)
            for _ in range(3):
                if n_piece < 2 * NE:
                    split_piece(n_piece, region_free)
                    n_piece += 1
            v = V(lambda e: e.tensor_reduce(rd[:, 0:bn], p3, AX.X, ALU.add), v)
            v = V(lambda e: e.reciprocal(rd[:, 0:bn], rd[:, 0:bn]), v)
            v = V(lambda e: e.tensor_tensor(p3, p3, per_node, ALU.mult), v)
            mine = p3.rearrange("p a (k o) -> p a k o", o=1).broadcast_to(shp4)
            other = p3.rearrange("p a (o k) -> p a o k", o=1).broadcast_to(shp4)
            v = V(lambda e: e.tensor_tensor(ca, other, mine, ALU.is_equal), v)
            v = V(lambda e: e.tensor_tensor(ca, ca, low, ALU.mult), v)
            v = V(lambda e: e.tensor_tensor(cb, other, mine, ALU.is_gt))
            v = V(lambda e: e.tensor_tensor(ca, ca, cb, ALU.add), v)
            v = V(lambda e: e.tensor_reduce(r3, ca, AX.X, ALU.add), v)
            v = V(lambda e: e.tensor_scalar(r3, r3, float(TOP), None, ALU.is_lt), v)
            if b0 + bn == NT:
                v = V(lambda e: e.tensor_scalar(rank[:, bn - 1, :], rank[:, bn - 1, :], valid[:, 0:1], None, ALU.mult), v)
            picked_ready[bi] = V(lambda e: e.tensor_copy(pick_h[:, 0:bn, :], r3), v)
            V(lambda e: e.tensor_tensor(c3, p3, r3, ALU.mult))
            v = V(lambda e: e.tensor_tensor(ca, r3.rearrange("p a (o k) -> p a o k", o=1).broadcast_to(shp4), low, ALU.mult))
            v = V(lambda e: e.tensor_reduce(l3, ca, AX.X, ALU.add), v)
            v = V(lambda e: e.tensor_tensor(pick[:, b0:b0 + bn, 1, :], l3, r3, ALU.mult), v)
            rank_free[bi] = V(lambda e: e.tensor_tensor(pick[:, b0:b0 + bn, 0, :], r3, pick[:, b0:b0 + bn, 1, :], ALU.subtract), v)

        rank_free = {}

        def send(bi):
            b0, bn = BLOCKS[bi]
            gb = bi % 2
            bank = 6 + gb
            picked = picked_ready[bi]
            c3, l3, cb = cw[:, 0:bn, :], place[:, 0:bn, :], cmp_b[:, 0:bn]
            shp3 = [P, bn, NE]
            n = bn * NE
            ph = pick_h[:, 0:bn, :].rearrange("p a k -> p (a k)")
            put("pe", lambda e: e.matmul(ps[:, bank, 256:256 + n], tri_h[:, :], ph, start=True, stop=True), (picked, turn_free[0], turn_free[1]), None)
            t = put("pe", lambda e: e.matmul(ps[:, bank, 320:320 + n], ones_sq[:, :], ph, start=True, stop=True), (), s_yt)
            v = rank_free[bi]
            for k in range(bn):
                v = V(lambda e, k=k: e.tensor_tensor(runs[:, b0 + k + 1, :], ps[:, bank, 320 + k * NE:320 + (k + 1) * NE], runs[:, b0 + k, :], ALU.add), t, v)
            v = V(lambda e: e.tensor_tensor(l3, ps[:, bank, 256:256 + n].rearrange("p (a k) -> p a k", k=NE), runs[:, b0:b0 + bn, :], ALU.add), v)
            turn_free[gb] = v
            v = V(lambda e: e.tensor_tensor(l3, l3, e_row[:, :].rearrange("p (o k) -> p o k", o=1).broadcast_to(shp3), ALU.add), v)
            for c in range(TOP):
                for values, to in ((l3, node_row), (c3, wgt)):
                    v = V(lambda e, c=c, values=values: e.tensor_tensor(cb[:, :, 0, :], pick[:, b0:b0 + bn, c, :], values, ALU.mult), v)
                    v = V(lambda e, c=c, to=to: e.tensor_reduce(to[:, b0:b0 + bn, c], cb[:, :, 0, :], AX.X, ALU.add), v)
            v = V(lambda e: e.tensor_copy(node_row_u[:, b0:b0 + bn, :], node_row[:, b0:b0 + bn, :]), v)
            for a in range(b0, b0 + bn):
                rows = P if a < NT - 1 else TAIL
                for c in range(TOP):
                    sent[a] = dma("pool", lambda e, a=a, c=c, rows=rows: e.indirect_dma_start(
                        out=sent_dram, out_offset=bass.IndirectOffsetOnAxis(ap=node_row_u[0:rows, a, c:c + 1], axis=0),
                        in_=yrow[0:rows, a % 8, :], in_offset=None),
                        (v, yrow_ready[a], zero_rows) + strips_in, s_send[a % 8])
        p2_layer(gw2T, ef_ready, post2, finish2, [(4, logits), (5, gate), (7, send)])
        while n_piece < 2 * NE:
            split_piece(n_piece, region_free)
            n_piece += 1
        weights_in = (s_wpart.sem, s_wpart.value)
        p2_done = (s_p2.sem, s_p2.value)
        gated = (dve.sem, dve.value)
        all_sent = tuple((x.sem, x.value) for x in s_send)

        b1_rows_in = dma("sp", lambda e: e.dma_start(b1rows, b1.rearrange("n h -> (n h)").partition_broadcast(P)), (p2_done,), sig("b1_rows_loaded"))

        b2_rows_in = dma("act", lambda e: e.dma_start(b2rows, b2.rearrange("n d -> (n d)").partition_broadcast(P)), (p2_done,), sig("b2_rows_loaded"))

        def along(ap, n):
            return ap.rearrange("p (o k) -> p o k", o=1).broadcast_to([P, n, NE])

        v = V(lambda e: e.tensor_scalar(tiles_f[:, :], runs[:, NT, :], float(P - 1), None, ALU.add), gated)
        v = V(lambda e: e.tensor_copy(tiles_i[:, :], tiles_f[:, :]), v)
        v = V(lambda e: e.tensor_scalar(tiles_i[:, :], tiles_i[:, :], 7, None, ALU.logical_shift_right), v)
        v = V(lambda e: e.tensor_copy(tiles_f[:, :], tiles_i[:, :]), v)
        v = V(lambda e: e.tensor_tensor(cmp_a[:, 0], lower[:, :, :], along(tiles_f[:, :], NE), ALU.mult), v)
        v = V(lambda e: e.tensor_reduce(base_f[:, :], cmp_a[:, 0], AX.X, ALU.add), v)
        v = V(lambda e: e.tensor_tensor(ends_f[:, :], base_f[:, :], tiles_f[:, :], ALU.add), v)
        over = tile_cmp[:, 0]
        v = V(lambda e: e.tensor_tensor(over, tcol[:, :].rearrange("p (t o) -> p t o", o=1).broadcast_to([P, ETILES, NE]), along(ends_f[:, :], ETILES), ALU.is_ge), v, p2_done)
        v0 = V(lambda e: e.tensor_reduce(tile_e[:, :], over, AX.X, ALU.add), v)
        v = V(lambda e: e.tensor_tensor(tile_cmp[:, 1], over, along(tiles_f[:, :], ETILES), ALU.mult))
        v = V(lambda e: e.tensor_reduce(tile_b[:, :], tile_cmp[:, 1], AX.X, ALU.add), v)
        v1 = V(lambda e: e.tensor_scalar(tile_e[:, :], tile_e[:, :], float(NE - 1), None, ALU.min), v0)
        v2 = V(lambda e: e.tensor_scalar(off_w[:, :], tile_e[:, :], float(EW), None, ALU.mult), v1)
        offs = V(lambda e: e.tensor_scalar(off_b[:, :], tile_e[:, :], float(D), None, ALU.mult))
        v = V(lambda e: e.tensor_tensor(tile_b[:, :], tcol[:, :], tile_b[:, :], ALU.subtract), v)
        v = V(lambda e: e.tensor_scalar(tile_b[:, :], tile_b[:, :], float(P), None, ALU.mult), v)
        v = V(lambda e: e.scalar_tensor_tensor(out=tile_b[:, :], in0=tile_e[:, :], scalar=float(CAP), in1=tile_b[:, :], op0=ALU.mult, op1=ALU.add), v)
        v = V(lambda e: e.tensor_scalar(tile_b[:, :], tile_b[:, :], float(NE * CAP - P), part_f[:, 0:1], ALU.min, ALU.add), v)
        rows_ok = V(lambda e: e.tensor_copy(row_u[:, :], tile_b[:, :]), v)
        v = V(lambda e: e.scalar_tensor_tensor(out=ends_f[:, :], in0=base_f[:, :], scalar=float(P), in1=e_row[:, :], op0=ALU.mult, op1=ALU.subtract))
        pick_flat = pick[:, :, :, :].rearrange("p a c k -> p (a c) k")
        v = V(lambda e: e.tensor_tensor(pick_flat, pick_flat, along(ends_f[:, :], NT * TOP), ALU.mult), v)
        v = V(lambda e: e.tensor_reduce(wide, pick_flat, AX.X, ALU.add), v)
        v = V(lambda e: e.tensor_tensor(node_row[:, :, :], node_row[:, :, :], wide.rearrange("p (a c) -> p a c", c=TOP), ALU.add), v)
        back_ok = V(lambda e: e.tensor_copy(node_row_u[:, :, :], node_row[:, :, :]), v, *all_sent)

        s_xg = [sig(f"rows_in_{b}") for b in range(4)]
        s_xt, s_xt_out, s_g1, s_pre, s_gelu, s_ht, s_hhi, s_hlo, s_g2, s_yo = [sig(n) for n in (
            "rows_turned", "rows_turned_copied", "hidden_summed", "hidden_biased", "hidden_gelu", "hidden_turned",
            "hidden_high", "hidden_rest", "expert_summed", "expert_copied")]
        s_ys = [sig(f"expert_stored_{b}") for b in range(4)]
        rows_in, rows_turned, xcol_ok, g1_ok, pre_ok, gelu_ok, hid_turned, parts_ok, g2_ok, yo_ok, stored = [{} for _ in range(11)]
        offset = {}

        def load_offset(engine, table, top, t):
            def fn(e):
                offset[engine, t] = e.value_load(table[0:1, t:t + 1], min_val=0, max_val=top)
            put(engine, fn, (offs, v2), None)

        def fetch(t):
            rows_in[t] = dma("pool", lambda e: e.indirect_dma_start(
                out=xg[:, t % 4, :], out_offset=None, in_=sent_dram, in_offset=bass.IndirectOffsetOnAxis(ap=row_u[:, t:t + 1], axis=0)),
                (rows_ok, rows_turned.get(t - 4), p2_done) + all_sent, s_xg[t % 4])

        def turn_rows(t):
            bank = bank_h(6)[:, (t % 2) * 2 * D:(t % 2 + 1) * 2 * D]
            for k in range(2 * FB):
                rows_turned[t] = put("pe", lambda e, k=k: e.transpose(bank[:, k * P:(k + 1) * P], xg[:, t % 4, k * P:(k + 1) * P], ident_h[:, :]),
                                     (rows_in[t], xcol_ok.get(t - 2), gated), s_xt if k == 2 * FB - 1 else None)
            xcol_ok[t] = put("dve", lambda e: e.tensor_copy(xcol[:, t % 2, :], bank), (rows_turned[t], g1_ok.get(t - 2)), s_xt_out)

        def hidden(t):
            load_offset("pe", off_w, (NE - 1) * EW, t)
            b = t % 2
            terms = [(xp, wp, fb) for xp, wp in ((0, 0), (0, 1), (1, 0)) for fb in range(FB)]
            for i, (xp, wp, fb) in enumerate(terms):
                last = i == len(terms) - 1
                g1_ok[t] = put("pe", lambda e, xp=xp, wp=wp, fb=fb, i=i, last=last: e.matmul(
                    ps[:, b, :], xcol[:, b, (xp * FB + fb) * P:(xp * FB + fb + 1) * P],
                    region[:, bass.ds(offset["pe", t] + (wp * FB + fb) * H, H)], start=i == 0, stop=last),
                    (xcol_ok[t], pre_ok.get(t - 2), weights_in, p2_out[0]), s_g1 if last else None)
            load_offset("dve", off_b, (NE - 1) * D, t)
            pre_ok[t] = put("dve", lambda e: e.scalar_tensor_tensor(out=hid[:, b, :], in0=ps[:, b, :], scalar=iW1[:, 0:1],
                                                                    in1=b1rows[:, bass.ds(offset["dve", t] * (H // D), H)], op0=ALU.mult, op1=ALU.add),
                            (g1_ok[t], b1_rows_in, hid_turned.get(t - 2)), s_pre)
            gelu_ok[t] = put("act", lambda e: e.activation(hid[:, b, :], hid[:, b, :], ACT.Gelu), (pre_ok[t],), s_gelu)

        def turn_hidden(t):
            b = t % 2
            for hb in range(HB):
                hid_turned[t] = put("pe", lambda e, hb=hb: e.transpose(ps[:, 2 + b, hb * P:(hb + 1) * P], hid[:, b, hb * P:(hb + 1) * P], ident_f[:, :]),
                                    (gelu_ok[t], parts_ok.get(t - 2), p2_out[1]), s_ht if hb == HB - 1 else None)
            hi = put("act", lambda e: e.activation(hcol[:, b, 0, :], ps[:, 2 + b, :], ACT.Copy, scale=sH[:, 0:1]), (hid_turned[t], g2_ok.get(t - 2)), s_hhi)
            parts_ok[t] = put("dve", lambda e: e.scalar_tensor_tensor(out=hcol[:, b, 1, :], in0=ps[:, 2 + b, :], scalar=sH[:, 0:1], in1=hcol[:, b, 0, :],
                                                                      op0=ALU.mult, op1=ALU.subtract), (hi,), s_hlo)

        def result(t):
            b = t % 2
            terms = [(hp, wp, hb) for hp, wp in ((0, 0), (0, 1), (1, 0)) for hb in range(HB)]
            for i, (hp, wp, hb) in enumerate(terms):
                last = i == len(terms) - 1
                g2_ok[t] = put("pe", lambda e, hp=hp, wp=wp, hb=hb, i=i, last=last: e.matmul(
                    ps[:, 4 + b, 0:D], hcol[:, b, hp, hb * P:(hb + 1) * P],
                    region[:, bass.ds(offset["pe", t] + 2 * FB * H + (wp * HB + hb) * D, D)], start=i == 0, stop=last),
                    (parts_ok[t], yo_ok.get(t - 2)), s_g2 if last else None)
            yo_ok[t] = put("dve", lambda e: e.scalar_tensor_tensor(out=yo[:, t % 4, :], in0=ps[:, 4 + b, 0:D], scalar=iW2[:, 0:1],
                                                                   in1=b2rows[:, bass.ds(offset["dve", t], D)], op0=ALU.mult, op1=ALU.add),
                           (g2_ok[t], b2_rows_in, stored.get(t - 4)), s_yo)
            stored[t] = dma("sp", lambda e: e.dma_start(expert_out_dram[t * P:(t + 1) * P, :], yo[:, t % 4, :]), (yo_ok[t],), s_ys[t % 4])

        for t in range(3):
            fetch(t)
        turn_rows(0)
        for t in range(ETILES + 2):
            if t < ETILES:
                hidden(t)
            if t + 1 < ETILES:
                turn_rows(t + 1)
            if t + 3 < ETILES:
                fetch(t + 3)
            if 1 <= t <= ETILES:
                turn_hidden(t - 1)
            if t >= 2:
                result(t - 2)

        s_back = [sig(f"rows_back_{b}") for b in range(8)]
        all_out = tuple((x.sem, x.value) for x in s_ys)
        back_used = {}
        x_acc = [None] * NT
        n_back = 0
        for a in range(NT):
            rows = P if a < NT - 1 else TAIL
            for c in range(TOP):
                r = n_back % 8
                got = dma("pool", lambda e, a=a, c=c, r=r, rows=rows: e.indirect_dma_start(
                    out=back[0:rows, r, :], out_offset=None, in_=expert_out_dram, in_offset=bass.IndirectOffsetOnAxis(ap=node_row_u[0:rows, a, c:c + 1], axis=0)),
                    all_out + (back_ok, back_used.get(n_back - 8)), s_back[r])
                x_acc[a] = back_used[n_back] = V(lambda e, a=a, c=c, r=r, rows=rows: e.scalar_tensor_tensor(
                    out=xt[0:rows, a, :], in0=back[0:rows, r, :], scalar=wgt[0:rows, a, c:c + 1], in1=xt[0:rows, a, :], op0=ALU.mult, op1=ALU.add),
                    got, x_acc[a] if c else x_added[a])
                n_back += 1

        s_out = sig("out_stored")
        for a0 in range(0, NT - 1, 6):
            a1 = min(a0 + 6, NT - 1)
            dma("sp", lambda e, a0=a0, a1=a1: e.dma_start(out[a0 * P:a1 * P, :].rearrange("(a q) f -> q a f", q=P), xt[:, a0:a1, :]), (x_acc[a1 - 1],), s_out)
        fin = dma("sp", lambda e: e.dma_start(out[(NT - 1) * P:N, :], xt[0:TAIL, NT - 1, :]), (x_acc[NT - 1],), s_out)
        put("sp", lambda e: e.nop(), (fin,), None)

        ctx.enter_context(nc.allow_non_contiguous_dma(reason="bias columns, a few kilobytes"))
        block = ctx.enter_context(nc.Block())

        @block.tensor
        def _(e):
            prog.emit("pe", e)

        @block.scalar
        def _(e):
            prog.emit("act", e)

        @block.vector
        def _(e):
            prog.emit("dve", e)

        @block.gpsimd
        def _(e):
            prog.emit("pool", e)

        @block.sync
        def _(e):
            prog.emit("sp", e)


_INS = ["x", "src", "dst", "L0_gnn_W1", "L0_gnn_b1", "L0_gnn_W2", "L0_gnn_b2", "L0_gnn_prelu_a", "L0_ffn_gate_w",
        "L0_ffn_gate_b", "L0_ffn_W1", "L0_ffn_b1", "L0_ffn_W2", "L0_ffn_b2"]


def kernel(**inputs):
    import numpy as np
    import concourse.bacc as bacc
    from concourse.bass_utils import run_bass_kernel_spmd

    nc = bacc.Bacc("TRN2", target_bir_lowering=False, num_devices=1)
    arrays, args = {}, []
    for name in _INS:
        a = np.ascontiguousarray(inputs[name])
        a = a.reshape(a.shape or (1,))
        arrays[name] = a
        args.append(nc.dram_tensor(name, a.shape, mybir.dt.from_np(a.dtype), kind="ExternalInput").ap())
    out = nc.dram_tensor("out", arrays["x"].shape, F32, kind="ExternalOutput").ap()
    gnn_moe_kernel(nc, *args, out)
    r = run_bass_kernel_spmd(nc, [arrays], core_ids=[0])
    return r.results[0]["out"]
```
